# Optimizing a Trainium2 kernel written in Bass

```python
import numpy as np
import jax
import jax.numpy as jnp

def _softmax(x, axis=-1):
    return jax.nn.softmax(x, axis=axis)

def _gelu(x):
    return jax.nn.gelu(x, approximate=True)

def _silu(x):
    return jax.nn.silu(x)

def _sigmoid(x):
    return jax.nn.sigmoid(x)

def _layernorm(x, axis=-1, eps=1e-05):
    m = jnp.mean(x, axis=axis, keepdims=True)
    v = jnp.var(x, axis=axis, keepdims=True)
    return (x - m) / jnp.sqrt(v + eps)

def _scatter_add(tgt, idx, src, axis=0):
    return tgt.at[idx].add(src)

def _segment_sum(src, seg, n):
    return jax.ops.segment_sum(src, seg, n)
kernel_name = 'mk_flamingo_gated_d2_seqx_r8_0dd4af'

def setup_inputs(seed: int=0):
    np.random.seed(seed)
    _w = jnp.asarray

    def _rec_inputs():
        import jax
        import jax.numpy as jnp
        _rk = jax.random.key(seed)
        x = 0.0003765 + 1 * jax.random.normal(jax.random.fold_in(_rk, 1), (16, 128, 128), jnp.float32)
        _lenS = 128 - jax.random.randint(jax.random.fold_in(_rk, 7), (16,), 0, max(1, 128 // 4) + 1, jnp.int32)
        _lenS2 = 128 - jax.random.randint(jax.random.fold_in(_rk, 8), (16,), 0, max(1, 128 // 4) + 1, jnp.int32)
        _ctx_1024P = jax.random.normal(jax.random.fold_in(_rk, 11), (16, 16, 128), jnp.float32)
        _ctx_1024c = jax.random.dirichlet(jax.random.fold_in(_rk, 511), 0.3 * jnp.ones((16,), jnp.float32), (16, 128))
        _ctx_1024t = jnp.einsum('bsk,bkd->bsd', _ctx_1024c, _ctx_1024P)
        _ctx_1024t = _ctx_1024t * jax.lax.rsqrt(jnp.mean(jnp.square(_ctx_1024t)) + 1e-12) * 0.953939
        ctx_1024 = -0.000292821 + 1.00034 * (_ctx_1024t + 0.3 * jax.random.normal(jax.random.fold_in(_rk, 611), (16, 128, 128), jnp.float32))
        _g = jax.random.normal(jax.random.fold_in(_rk, 9001), (2, 2), jnp.float32)
        _g = jnp.sign(_g) * jnp.maximum(jnp.abs(_g), 1.0) + (_g == 0) * 1.0
        g_xattn = _g[0]
        g_ffn = _g[1]
        return (x, ctx_1024, g_xattn, g_ffn)
    x, ctx_1024, g_xattn, g_ffn = _rec_inputs()

    def _L0_xattn_setup():
        import jax, jax.numpy as jnp
        import numpy as np
        NUM_HEADS = 16

        def _split_heads(x, num_heads):
            B, S, H = x.shape
            dh = H // num_heads
            return x.reshape(B, S, dh, num_heads).transpose(0, 3, 1, 2)
        key = jax.random.key(seed)
        ks = jax.random.split(key, 11)
        B, S, D, H = (2, 256, 128, 128)
        s = lambda k, shape, scale=1.0: jax.random.normal(k, shape, dtype=jnp.float32) * scale
        return {'KEY': s(ks[0], (B, S, D)), 'VALUE': s(ks[1], (B, S, D)), 'QUERY': s(ks[2], (B, S, D)), 'Wk_w': s(ks[3], (H, D), 0.02), 'Wk_b': s(ks[4], (H,), 0.02), 'Wq_w': s(ks[5], (H, D), 0.02), 'Wq_b': s(ks[6], (H,), 0.02), 'Wv_w': s(ks[7], (H, D), 0.02), 'Wv_b': s(ks[8], (H,), 0.02), 'Wo_w': s(ks[9], (H, H), 0.02), 'Wo_b': s(ks[10], (H,), 0.02)}
    _L0_xattn_all = _L0_xattn_setup()
    _L0_xattn_in = {k: v for k, v in _L0_xattn_all.items() if k in ('Wk_w', 'Wk_b', 'Wq_w', 'Wq_b', 'Wv_w', 'Wv_b', 'Wo_w', 'Wo_b')}
    del _L0_xattn_all

    def _L0_ffn_setup():
        import jax, jax.numpy as jnp
        import numpy as np
        NUM_EXPERTS = 8
        TOP_K = 2
        key = jax.random.key(seed)
        ks = jax.random.split(key, 5)
        B, L, E, H, N = (2, 256, 128, 256, NUM_EXPERTS)
        return {'x': jax.random.normal(ks[0], (B, L, E), dtype=jnp.float32), 'gate_kernel': jax.random.normal(ks[1], (E, N), dtype=jnp.float32) / np.sqrt(E), 'w0_kernel': jax.random.normal(ks[2], (N, E, H), dtype=jnp.float32) / np.sqrt(E), 'w1_kernel': jax.random.normal(ks[3], (N, E, H), dtype=jnp.float32) / np.sqrt(E), 'wo_kernel': jax.random.normal(ks[4], (N, H, E), dtype=jnp.float32) / np.sqrt(H)}
    _L0_ffn_all = _L0_ffn_setup()
    _L0_ffn_in = {k: v for k, v in _L0_ffn_all.items() if k in ('gate_kernel', 'w0_kernel', 'w1_kernel', 'wo_kernel')}
    del _L0_ffn_all

    def _L1_xattn_setup():
        import jax, jax.numpy as jnp
        import numpy as np
        B, C_LEN, Q_LEN, D = (8, 256, 64, 128)
        key = jax.random.key(seed)
        ks = jax.random.split(key, 10)
        scale = 1.0 / np.sqrt(D)
        return {'c': jax.random.normal(ks[0], (B, C_LEN, D), dtype=jnp.float32), 'q': jax.random.normal(ks[1], (B, Q_LEN, D), dtype=jnp.float32), 'w_cq': jax.random.normal(ks[2], (D,), dtype=jnp.float32) * scale, 'b_cq': jax.random.normal(ks[3], (), dtype=jnp.float32) * scale, 'w_c': jax.random.normal(ks[4], (D,), dtype=jnp.float32) * scale, 'b_c': jax.random.normal(ks[5], (), dtype=jnp.float32) * scale, 'w_q': jax.random.normal(ks[6], (D,), dtype=jnp.float32) * scale, 'b_q': jax.random.normal(ks[7], (), dtype=jnp.float32) * scale, 'W_l': jax.random.normal(ks[8], (D, 4 * D), dtype=jnp.float32) * (1.0 / np.sqrt(4 * D)), 'b_l': jax.random.normal(ks[9], (D,), dtype=jnp.float32) * (1.0 / np.sqrt(4 * D))}
    _L1_xattn_all = _L1_xattn_setup()
    _L1_xattn_in = {k: v for k, v in _L1_xattn_all.items() if k in ('w_cq', 'b_cq', 'w_c', 'b_c', 'w_q', 'b_q', 'W_l', 'b_l')}
    del _L1_xattn_all

    def _L1_ffn_setup():
        import jax, jax.numpy as jnp
        import numpy as np
        HIDDEN = 128
        INNER = 512

        def _weight_quant(w):
            scale = 1.0 / jnp.clip(jnp.mean(jnp.abs(w)), 1e-05)
            wq = jnp.clip(jnp.round(w * scale), -1.0, 1.0) / scale
            return w + jax.lax.stop_gradient(wq - w)

        def _act_quant(x):
            scale = 127.0 / jnp.clip(jnp.max(jnp.abs(x), axis=-1, keepdims=True), 1e-05)
            xq = jnp.clip(jnp.round(x * scale), -128.0, 127.0) / scale
            return x + jax.lax.stop_gradient(xq - x)

        def _bitlinear(x, w):
            return jnp.einsum('bsi,oi->bso', _act_quant(x), _weight_quant(w))
        key = jax.random.key(seed)
        k0, k1, k2, k3 = jax.random.split(key, 4)
        x = jax.random.normal(k0, (4, 256, HIDDEN), dtype=jnp.float32)
        w_gate = jax.random.normal(k1, (INNER, HIDDEN), dtype=jnp.float32) / np.sqrt(HIDDEN)
        w_up = jax.random.normal(k2, (INNER, HIDDEN), dtype=jnp.float32) / np.sqrt(HIDDEN)
        w_down = jax.random.normal(k3, (HIDDEN, INNER), dtype=jnp.float32) / np.sqrt(INNER)
        return {'x': x, 'w_gate': w_gate, 'w_up': w_up, 'w_down': w_down}
    _L1_ffn_all = _L1_ffn_setup()
    _L1_ffn_in = {k: v for k, v in _L1_ffn_all.items() if k in ('w_gate', 'w_up', 'w_down')}
    del _L1_ffn_all
    return {'x': x, 'ctx_1024': ctx_1024, 'g_xattn': g_xattn, 'g_ffn': g_ffn, 'L0_xattn_Wk_w': _L0_xattn_in['Wk_w'], 'L0_xattn_Wk_b': _L0_xattn_in['Wk_b'], 'L0_xattn_Wq_w': _L0_xattn_in['Wq_w'], 'L0_xattn_Wq_b': _L0_xattn_in['Wq_b'], 'L0_xattn_Wv_w': _L0_xattn_in['Wv_w'], 'L0_xattn_Wv_b': _L0_xattn_in['Wv_b'], 'L0_xattn_Wo_w': _L0_xattn_in['Wo_w'], 'L0_xattn_Wo_b': _L0_xattn_in['Wo_b'], 'L0_ffn_gate_kernel': _L0_ffn_in['gate_kernel'], 'L0_ffn_w0_kernel': _L0_ffn_in['w0_kernel'], 'L0_ffn_w1_kernel': _L0_ffn_in['w1_kernel'], 'L0_ffn_wo_kernel': _L0_ffn_in['wo_kernel'], 'L1_xattn_w_cq': _L1_xattn_in['w_cq'], 'L1_xattn_b_cq': _L1_xattn_in['b_cq'], 'L1_xattn_w_c': _L1_xattn_in['w_c'], 'L1_xattn_b_c': _L1_xattn_in['b_c'], 'L1_xattn_w_q': _L1_xattn_in['w_q'], 'L1_xattn_b_q': _L1_xattn_in['b_q'], 'L1_xattn_W_l': _L1_xattn_in['W_l'], 'L1_xattn_b_l': _L1_xattn_in['b_l'], 'L1_ffn_w_gate': _L1_ffn_in['w_gate'], 'L1_ffn_w_up': _L1_ffn_in['w_up'], 'L1_ffn_w_down': _L1_ffn_in['w_down']}

def reference(x, ctx_1024, g_xattn, g_ffn, L0_xattn_Wk_w, L0_xattn_Wk_b, L0_xattn_Wq_w, L0_xattn_Wq_b, L0_xattn_Wv_w, L0_xattn_Wv_b, L0_xattn_Wo_w, L0_xattn_Wo_b, L0_ffn_gate_kernel, L0_ffn_w0_kernel, L0_ffn_w1_kernel, L0_ffn_wo_kernel, L1_xattn_w_cq, L1_xattn_b_cq, L1_xattn_w_c, L1_xattn_b_c, L1_xattn_w_q, L1_xattn_b_q, L1_xattn_W_l, L1_xattn_b_l, L1_ffn_w_gate, L1_ffn_w_up, L1_ffn_w_down):
    import jax
    import jax.numpy as jnp

    def _L0_xattn_ref(KEY, VALUE, QUERY, Wk_w, Wk_b, Wq_w, Wq_b, Wv_w, Wv_b, Wo_w, Wo_b):
        import jax, jax.numpy as jnp
        import numpy as np
        NUM_HEADS = 16

        def _split_heads(x, num_heads):
            B, S, H = x.shape
            dh = H // num_heads
            return x.reshape(B, S, dh, num_heads).transpose(0, 3, 1, 2)
        nh = NUM_HEADS
        k = _split_heads(KEY @ Wk_w.T + Wk_b, nh)
        q = _split_heads(QUERY @ Wq_w.T + Wq_b, nh)
        v = _split_heads(VALUE @ Wv_w.T + Wv_b, nh)
        dh = q.shape[-1]
        score = jnp.einsum('bhij,bhkj->bhik', k, q) / jnp.sqrt(jnp.asarray(dh, k.dtype))
        attn = jax.nn.softmax(score, axis=1)
        out = jnp.einsum('bhik,bhij->bhjk', attn, v)
        B = out.shape[0]
        out = out.transpose(0, 2, 1, 3).reshape(B, -1, out.shape[-1]).transpose(0, 2, 1)
        res = out @ Wo_w.T + Wo_b
        return res

    def _L0_ffn_ref(x, gate_kernel, w0_kernel, w1_kernel, wo_kernel):
        import jax, jax.numpy as jnp
        import numpy as np
        NUM_EXPERTS = 8
        TOP_K = 2
        B, L, E = x.shape
        gate_logits = jnp.einsum('ble,en->bln', x, gate_kernel)
        top_k_weights, top_k_indices = jax.lax.top_k(gate_logits, TOP_K)
        softmax_probs = jax.nn.softmax(top_k_weights.astype(jnp.float32), axis=-1)
        weights = jnp.zeros_like(gate_logits)
        b_idx = jnp.arange(B)[:, None, None]
        l_idx = jnp.arange(L)[:, None]
        weights = weights.at[b_idx, l_idx, top_k_indices].set(softmax_probs)
        layer_w0 = jnp.einsum('ble,neh->blnh', x, w0_kernel)
        layer_w1 = jnp.einsum('ble,neh->blnh', x, w1_kernel)
        layer_mult = jax.nn.silu(layer_w0) * layer_w1
        intermediate = jnp.einsum('blnh,nhe->blne', layer_mult, wo_kernel)
        output = jnp.einsum('blne,bln->ble', intermediate, weights)
        return output

    def _L1_xattn_ref(c, q, w_cq, b_cq, w_c, b_c, w_q, b_q, W_l, b_l):
        import jax, jax.numpy as jnp
        import numpy as np
        B, C_LEN, Q_LEN, D = (8, 256, 64, 128)
        cq = jnp.einsum('bcd,bqd,d->bcq', c, q, w_cq) + b_cq
        s = (c @ w_c + b_c)[:, :, None] + (q @ w_q + b_q)[:, None, :] + cq
        a = jax.nn.softmax(s, axis=2)
        c2q_att = jnp.einsum('bcq,bqd->bcd', a, q)
        b_att = jax.nn.softmax(jnp.max(s, axis=2), axis=1)
        q2c_att = jnp.einsum('bc,bcd->bd', b_att, c)[:, None, :]
        x = jnp.concatenate([c, c2q_att, c * c2q_att, c * q2c_att], axis=-1)
        z = x @ W_l.T + b_l
        return z

    def _L1_ffn_ref(x, w_gate, w_up, w_down):
        import jax, jax.numpy as jnp
        import numpy as np
        HIDDEN = 128
        INNER = 512

        def _weight_quant(w):
            scale = 1.0 / jnp.clip(jnp.mean(jnp.abs(w)), 1e-05)
            wq = jnp.clip(jnp.round(w * scale), -1.0, 1.0) / scale
            return w + jax.lax.stop_gradient(wq - w)

        def _act_quant(x):
            scale = 127.0 / jnp.clip(jnp.max(jnp.abs(x), axis=-1, keepdims=True), 1e-05)
            xq = jnp.clip(jnp.round(x * scale), -128.0, 127.0) / scale
            return x + jax.lax.stop_gradient(xq - x)

        def _bitlinear(x, w):
            return jnp.einsum('bsi,oi->bso', _act_quant(x), _weight_quant(w))
        gate = jax.nn.silu(_bitlinear(x, w_gate))
        up = _bitlinear(x, w_up)
        return _bitlinear(gate * up, w_down)
    x = x + jnp.tanh(g_xattn[0]) * _L0_xattn_ref(ctx_1024, ctx_1024, _layernorm(x, axis=-1), L0_xattn_Wk_w, L0_xattn_Wk_b, L0_xattn_Wq_w, L0_xattn_Wq_b, L0_xattn_Wv_w, L0_xattn_Wv_b, L0_xattn_Wo_w, L0_xattn_Wo_b)
    x = x + jnp.tanh(g_ffn[0]) * _L0_ffn_ref(_layernorm(x, axis=-1), L0_ffn_gate_kernel, L0_ffn_w0_kernel, L0_ffn_w1_kernel, L0_ffn_wo_kernel)
    x = x + jnp.tanh(g_xattn[1]) * _L1_xattn_ref(_layernorm(x, axis=-1), ctx_1024, L1_xattn_w_cq, L1_xattn_b_cq, L1_xattn_w_c, L1_xattn_b_c, L1_xattn_w_q, L1_xattn_b_q, L1_xattn_W_l, L1_xattn_b_l)
    x = x + jnp.tanh(g_ffn[1]) * _L1_ffn_ref(_layernorm(x, axis=-1), L1_ffn_w_gate, L1_ffn_w_up, L1_ffn_w_down)
    return x

_drawn_inputs = setup_inputs


def setup_inputs(seed=0):
    import zlib

    import numpy as np

    out = dict(_drawn_inputs(seed))
    spreads = {'g_ffn': (-1.0, 0.6)}
    factors = {'L0_xattn_Wk_w': 2.942, 'L0_xattn_Wk_b': 8.0, 'L0_xattn_Wq_w': 2.914, 'L0_xattn_Wq_b': 8.0}
    for name, (base, spread) in spreads.items():
        noise = np.random.default_rng([zlib.crc32(name.encode()), seed]).standard_normal(out[name].shape)
        drawn = base * np.exp(spread * noise) if base else spread * noise
        out[name] = jnp.asarray(drawn.astype(out[name].dtype))
    for name, factor in factors.items():
        out[name] = (out[name] * factor).astype(out[name].dtype)
    return out
```

```python
from contextlib import ExitStack

import concourse.bass as bass
from concourse import mybir

ALU = mybir.AluOpType
ACT = mybir.ActivationFunctionType
AX = mybir.AxisListType
F32 = mybir.dt.float32
F32R = mybir.dt.float32r
BF16 = mybir.dt.bfloat16
U32 = mybir.dt.uint32

P = 128
BATCH = 16
PAIRS = BATCH // 2
TOK = 2 * P
HEADS = 16
DH = P // HEADS
HALF = P // 2
EXPERTS = 8
HID = 256
TILES = EXPERTS * HID // P
TPE = HID // P
INNER = 512
NI = INNER // P
EPS = 1e-5
ROUND = 1.5 * 2.0 ** 23
VSTEP = P + DH

SLOTS = 16
A_NORM, A_XT, A_K, A_Q, A_V = 0, 2, 3, 5, 15
A_UNIT = (12, 16, 20, 24)
A_OUT = (25, 28)
M_NORM, M_XT, M_GATE, M_UP = 30, 32, 33, 33
F_NORM = 52
G_NORM = 63
G_UNIT = (67, 69, 71, 73)
LAST = G_NORM + 16
TURNS = PAIRS + LAST // SLOTS
LOOP_FROM, LOOP_TO = LAST // SLOTS + 1, PAIRS


class Pair:

    def __init__(self, i, c):
        self.i, self.c = i, c
        self.first = isinstance(i, int) and c == 0

    def count(self, per_pair, k):
        return self.i * per_pair + (self.c * per_pair + k)

    def before(self, n=1):
        return Pair(self.i, self.c - n)

    def rows(self):
        return slice(self.c, self.c + 1) if isinstance(self.i, int) else bass.ds(self.i + self.c, 1)

    def after(self):
        return Pair(self.i, self.c + 1) if not isinstance(self.i, int) or self.c + 1 < PAIRS else None


def due(turn, j, offset):
    if (j - offset) % SLOTS:
        return None
    p = Pair(turn.i, turn.c - (offset - j) // SLOTS)
    return p if not isinstance(turn.i, int) or 0 <= p.c < PAIRS else None


def wait(eng, sem, value):
    if not isinstance(value, int) or value > 0:
        eng.wait_ge(sem, value)


def turns(eng, body):
    for t in range(LOOP_FROM):
        body(Pair(0, t))
    with eng.Fori(0, LOOP_TO - LOOP_FROM) as i:
        body(Pair(i, LOOP_FROM))
    for t in range(LOOP_TO, TURNS):
        body(Pair(0, t))


def build(nc, A, out):
    ctx = ExitStack()
    with ctx:
        def sb(name, shape, dt=F32):
            return ctx.enter_context(nc.sbuf_tensor(name, shape, dt))

        def bank(name, shape=(P, 512)):
            return ctx.enter_context(nc.psum_tensor(name, list(shape), F32))

        def sem(name):
            return ctx.enter_context(nc.semaphore(name))

        wqkv_raw = sb("wqkv_raw", [P, 3, P])
        wqkv_hi = sb("wqkv_hi", [P, 3, P], F32R)
        wqkv_lo = sb("wqkv_lo", [P, 3, P], F32R)
        bqk = sb("bqk", [P, 2])
        bv_all = sb("bv_all", [P, P])
        wo_t = sb("wo_t", [P, P])
        bo_all = sb("bo_all", [P, P])
        gains = sb("gains", [P, 4])
        th = sb("th", [P, 4])
        th_half = sb("th_half", [P, 1])
        w01_raw = sb("w01_raw", [P, 2, TILES * P])
        w01_hi = sb("w01_hi", [P, 2, TILES * P], F32R)
        w01_lo = sb("w01_lo", [P, 2, TILES * P], F32R)
        wdn = sb("wdn", [P, TILES, P])
        gate_raw = sb("gate_raw", [P, EXPERTS])
        gate_hi = sb("gate_hi", [P, EXPERTS], F32R)
        gate_lo = sb("gate_lo", [P, EXPERTS], F32R)
        wcq = sb("wcq", [P, 3])
        bsum3 = sb("bsum3", [P, 3])
        bsum = sb("bsum", [P, 1])
        wl = sb("wl", [P, 4, P])
        bl_all = sb("bl_all", [P, P])
        wf_raw = sb("wf_raw", [P, 3, INNER])
        wf_r = sb("wf_r", [P, 3, INNER])
        wf_t = sb("wf_t", [P, 3, INNER])
        wf_q = sb("wf_q", [P, 3, INNER], BF16)
        wabs = sb("wabs", [P, 3])
        wmean = sb("wmean", [P, 3])
        wscale = sb("wscale", [P, 3])
        cg = sb("cg", [P, 3])
        ident = sb("ident", [P, P])
        ident_bf = sb("ident_bf", [P, P], BF16)
        ones = sb("ones", [P, P])
        minus_half = sb("minus_half", [P, 2])
        eps_col = sb("eps_col", [P, 2])
        expert_no = sb("expert_no", [P, EXPERTS])

        x_in = sb("x_in", [P, 2, P])
        x_res = sb("x_res", [P, 2, P])
        ct_in = sb("ct_in", [P, TOK])
        ct_hi = sb("ct_hi", [P, TOK], F32R)
        ct_lo = sb("ct_lo", [P, TOK], F32R)
        a_st = sb("a_st", [P, 2, 6])
        a_mv = sb("a_mv", [P, 2, 2])
        a_rs = sb("a_rs", [P, 2, 2])
        a_xn = sb("a_xn", [P, 2, P])
        a_xhi = sb("a_xhi", [P, TOK], F32R)
        a_xlo = sb("a_xlo", [P, TOK], F32R)
        qk_parts = sb("qk_parts", [P, 2, 3, TOK], BF16)
        qk_rest = sb("qk_rest", [P, 2, TOK])
        k_rows = sb("k_rows", [P, HEADS // 2, TOK], BF16)
        q_rows = sb("q_rows", [P, HEADS // 2, TOK], BF16)
        v_diag = sb("v_diag", [P, 2, HEADS * VSTEP])
        head_max = sb("head_max", [P, 2, HALF])
        shifted = sb("shifted", [P, 2, HEADS, HALF])
        attn = sb("attn", [P, 2, HEADS, P])
        tree = sb("tree", [P, 15, HALF])
        head_sum = sb("head_sum", [P, HALF])
        head_inv = sb("head_inv", [P, HALF])
        o_t = sb("o_t", [P, 2, P])
        x1 = sb("x1", [P, 2, P])

        m_st = sb("m_st", [P, 2, 6])
        m_mv = sb("m_mv", [P, 2, 2])
        m_rs = sb("m_rs", [P, 2, 2])
        m_xn = sb("m_xn", [P, 2, P])
        m_xhi = sb("m_xhi", [P, TOK], F32R)
        m_xlo = sb("m_xlo", [P, TOK], F32R)
        logits = sb("logits", [P, 2, EXPERTS])
        top = sb("top", [P, 2, 8])
        top_no = sb("top_no", [P, 2, 8], U32)
        top_nof = sb("top_nof", [P, 2, 8])
        tdiff = sb("tdiff", [P, 2, 1])
        texp = sb("texp", [P, 2, 1])
        tsum = sb("tsum", [P, 2, 1])
        tprob = sb("tprob", [P, 2, 2])
        w_first = sb("w_first", [P, 2, EXPERTS])
        w_second = sb("w_second", [P, 2, EXPERTS])
        weights = sb("weights", [P, 2, EXPERTS])
        m_tanh = sb("m_tanh", [P, 2, TOK])
        m_u = sb("m_u", [P, 2, TOK])
        m_h = sb("m_h", [P, 4, TOK])
        y = sb("y", [P, 2, P])

        ctx_in = sb("ctx_in", [P, 2, P])
        ctf_in = sb("ctf_in", [P, TOK])
        f_st = sb("f_st", [P, 2, 6])
        f_mv = sb("f_mv", [P, 2, 2])
        f_rs = sb("f_rs", [P, 2, 2])
        f_c = sb("f_c", [P, 2, P])
        f_ct = sb("f_ct", [P, TOK])
        f_ctq = sb("f_ctq", [P, TOK])
        f_nmax = sb("f_nmax", [P, 2])
        f_m = sb("f_m", [P, 2])
        f_a = sb("f_a", [P, 2, P])
        f_asum = sb("f_asum", [P, 2])
        f_ainv = sb("f_ainv", [P, 2])
        f_an = sb("f_an", [P, 2, P])
        f_at = sb("f_at", [P, TOK])
        f_nmm = sb("f_nmm", [P, 2])
        f_erow = sb("f_erow", [P, 2, P])
        f_esum = sb("f_esum", [P, 2])
        f_einv = sb("f_einv", [P, 2])
        f_e = sb("f_e", [P, 2])
        f_c2q = sb("f_c2q", [P, TOK])
        f_prod = sb("f_prod", [P, TOK])
        f_q2c = sb("f_q2c", [P, 2])
        f_w14 = sb("f_w14", [P, 2, P])
        y_res = sb("y_res", [P, 2, P])
        x3 = sb("x3", [P, 2, P])

        g_st = sb("g_st", [P, 2, 6])
        g_mv = sb("g_mv", [P, 2, 2])
        g_rs = sb("g_rs", [P, 2, 2])
        g_h = sb("g_h", [P, 2, P])
        g_amax = sb("g_amax", [P, 2])
        g_amc = sb("g_amc", [P, 2])
        g_ainv = sb("g_ainv", [P, 2])
        g_sc = sb("g_sc", [P, 2, 3])
        g_r = sb("g_r", [P, 2, P])
        g_q = sb("g_q", [P, 2, P], BF16)
        g_qt = sb("g_qt", [P, TOK], BF16)
        g_tanh = sb("g_tanh", [P, 256])
        g_u = sb("g_u", [P, 256])
        g_p = sb("g_p", [P, 2, INNER])
        g_pmax = sb("g_pmax", [P, 2])
        g_pmc = sb("g_pmc", [P, 2])
        g_pinv = sb("g_pinv", [P, 2])
        g_ps = sb("g_ps", [P, 2, 2])
        g_pr = sb("g_pr", [P, 2, INNER])
        g_pq = sb("g_pq", [P, 2, INNER], BF16)
        g_pt = sb("g_pt", [P, 2, INNER], BF16)
        o_sb = sb("o_sb", [P, 2, P])

        ps_sc = bank("ps_sc", (P, 2, 512))
        ps_z = [bank("ps_z0"), bank("ps_z1")]
        ps_d = bank("ps_d")
        ps_a = bank("ps_a")
        ps_f = bank("ps_f")
        ps_g = bank("ps_g")

        parts_dram = nc.dram_tensor("parts_dram", (2, PAIRS, P, 3, TOK), BF16, kind="Internal").ap()

        w_attn = sem("w_attn"); w_moe = sem("w_moe"); w_fin = sem("w_fin"); w_ffn = sem("w_ffn")
        ld_a = sem("ld_a"); ld_res = sem("ld_res"); ld_f = sem("ld_f")
        parts_out = [sem("k_parts_out"), sem("q_parts_out")]
        rows_in = [sem("k_rows_in"), sem("q_rows_in")]
        stored = sem("stored")
        c_id = sem("c_id"); c_misc = sem("c_misc"); c_th = sem("c_th"); c_thh = sem("c_thh")
        c_zero = sem("c_zero")
        c_wq = sem("c_wq"); c_hi = sem("c_hi"); c_lo = sem("c_lo"); c_thbo = sem("c_thbo")
        c_mhi = sem("c_mhi"); c_mlo = sem("c_mlo"); c_bs = sem("c_bs")
        c_abs = sem("c_abs"); c_tot = sem("c_tot"); c_wm = sem("c_wm"); c_wr = sem("c_wr")
        s_passed = sem("s_passed"); s_sp_passed = sem("s_sp_passed")
        s_ast = sem("s_ast"); s_amv = sem("s_amv"); s_ars = sem("s_ars"); s_axn = sem("s_axn")
        s_axt = sem("s_axt"); s_axhi = sem("s_axhi"); s_axlo = sem("s_axlo")
        s_cthi = sem("s_cthi"); s_ctlo = sem("s_ctlo")
        s_proj = [sem("s_k"), sem("s_q")]
        s_p1 = [sem("s_k1"), sem("s_q1")]
        s_rest = [sem("s_krest"), sem("s_qrest")]
        s_p2 = [sem("s_k2"), sem("s_q2")]
        s_p3 = [sem("s_k3"), sem("s_q3")]
        s_v = sem("s_v"); s_vd = sem("s_vd")
        s_score = sem("s_score"); s_hmax = sem("s_hmax"); s_shift = sem("s_shift"); s_exp = sem("s_exp")
        s_tree = sem("s_tree"); s_hinv = sem("s_hinv"); s_attn = sem("s_attn")
        s_pv = sem("s_pv"); s_ot = sem("s_ot"); s_res = sem("s_res"); s_xb = sem("s_xb"); s_x1 = sem("s_x1")
        s_mst = sem("s_mst"); s_mmv = sem("s_mmv"); s_mrs = sem("s_mrs"); s_mxn = sem("s_mxn")
        s_mxt = sem("s_mxt"); s_mxhi = sem("s_mxhi"); s_mxlo = sem("s_mxlo")
        s_gate = sem("s_gate"); s_log = sem("s_log"); s_top = sem("s_top"); s_topi = sem("s_topi")
        s_tdf = sem("s_tdf"); s_texp = sem("s_texp"); s_tp = sem("s_tp"); s_w12 = sem("s_w12"); s_w = sem("s_w")
        s_z = sem("s_z"); s_mt = sem("s_mt"); s_mu = sem("s_mu"); s_mh = sem("s_mh")
        s_dn = sem("s_dn"); s_y = sem("s_y")
        s_fst = sem("s_fst"); s_fmv = sem("s_fmv"); s_frs = sem("s_frs"); s_fc = sem("s_fc")
        s_fyb = sem("s_fyb"); s_fct = sem("s_fct"); s_fcs = sem("s_fcs"); s_fcq = sem("s_fcq")
        s_fs = sem("s_fs"); s_fnm = sem("s_fnm"); s_fm = sem("s_fm"); s_fa = sem("s_fa"); s_fai = sem("s_fai")
        s_fan = sem("s_fan"); s_fat = sem("s_fat"); s_fats = sem("s_fats"); s_fnmm = sem("s_fnmm")
        s_fe = sem("s_fe"); s_fei = sem("s_fei"); s_fq = sem("s_fq"); s_fc2 = sem("s_fc2"); s_fpr = sem("s_fpr")
        s_fq2 = sem("s_fq2"); s_fw = sem("s_fw"); s_fz = sem("s_fz"); s_x3 = sem("s_x3")
        s_gst = sem("s_gst"); s_gmv = sem("s_gmv"); s_grs = sem("s_grs"); s_gh = sem("s_gh")
        s_gam = sem("s_gam"); s_gsc = sem("s_gsc"); s_gr = sem("s_gr"); s_gq = sem("s_gq")
        s_gqt = sem("s_gqt"); s_gqs = sem("s_gqs"); s_gu = sem("s_gu"); s_gt = sem("s_gt")
        s_guu = sem("s_guu"); s_gp = sem("s_gp"); s_gpm = sem("s_gpm"); s_gps = sem("s_gps")
        s_gpr = sem("s_gpr"); s_gpq = sem("s_gpq"); s_gpt = sem("s_gpt"); s_gpts = sem("s_gpts")
        s_gd = sem("s_gd"); s_o = sem("s_o")

        x_d = A["x"].rearrange("(p b) s d -> p s b d", b=2)
        c_d = A["ctx"].rearrange("(p b) s d -> p s b d", b=2)
        ct_d = A["ctx_t"].rearrange("(p b) d s -> p d b s", b=2)
        o_d = out.rearrange("(p b) s d -> p s b d", b=2)

        block = ctx.enter_context(nc.Block())

        @block.sync
        def _(sp):
            def body(t):
                for j in range(SLOTS):
                    if p := due(t, j, A_NORM):
                        q = p.before()
                        wait(sp, s_axn, q.count(2, 2))
                        sp.sem_inc(s_sp_passed, 1)
                        wait(sp, s_ctlo, q.count(1, 1))
                        sp.sem_inc(s_sp_passed, 1)
                        sp.dma_start(x_in[:], x_d[p.rows()].rearrange("o s b d -> s (o b) d")).then_inc(ld_a, 16)
                        sp.dma_start(ct_in[:].rearrange("d (b s) -> d b s", b=2),
                                     ct_d[p.rows()].rearrange("o d b s -> d (o b) s")).then_inc(ld_a, 16)
                    for n, (at, rows) in enumerate(((A_K, k_rows), (A_Q, q_rows))):
                        if p := due(t, j, at + 4):
                            sp.wait_ge(s_p3[n], p.count(1, 1))
                            sp.sem_inc(s_sp_passed, 1)
                            sp.dma_start(parts_dram[n][p.rows()].rearrange("o c r t -> c (o r) t"),
                                         qk_parts[:, n]).then_inc(parts_out[n], 16)
                    for n, rows in enumerate((k_rows, q_rows)):
                        if p := due(t, j, A_UNIT[0] - 2):
                            sp.wait_ge(parts_out[n], p.count(16, 16))
                            sp.sem_inc(s_sp_passed, 1)
                            wait(sp, s_score, p.before().count(4, 4))
                            sp.sem_inc(s_sp_passed, 1)
                            at = 0
                            for a, reps in enumerate((3, 2, 1)):
                                for hq in range(2):
                                    lo = hq * HALF + at * DH
                                    for b in range(reps):
                                        part = a if n == 0 else b
                                        src = parts_dram[n][p.rows(), hq * HALF:(hq + 1) * HALF, part, :]
                                        sp.dma_start(rows[lo + b * DH:lo + (b + 1) * DH, :, :],
                                                     src.rearrange("o (j h) t -> (o j) h t", h=HEADS // 2)
                                                     ).then_inc(rows_in[n], 16)
                                at += reps
                    if p := due(t, j, A_UNIT[1]):
                        wait(sp, s_x1, p.before().count(2, 2))
                        sp.sem_inc(s_sp_passed, 1)
                        sp.dma_start(x_res[:], x_d[p.rows()].rearrange("o s b d -> s (o b) d")).then_inc(ld_res, 16)
                    if p := due(t, j, F_NORM - 4):
                        wait(sp, s_fq, p.before().count(1, 1))
                        sp.sem_inc(s_sp_passed, 1)
                        sp.dma_start(ctx_in[:], c_d[p.rows()].rearrange("o s b d -> s (o b) d")).then_inc(ld_f, 16)
                        sp.dma_start(ctf_in[:].rearrange("d (b s) -> d b s", b=2),
                                     ct_d[p.rows()].rearrange("o d b s -> d (o b) s")).then_inc(ld_f, 16)
                    if p := due(t, j, LAST):
                        sp.wait_ge(s_o, p.count(2, 2))
                        sp.sem_inc(s_sp_passed, 1)
                        sp.dma_start(o_d[p.rows()].rearrange("o s b d -> s (o b) d"), o_sb[:]).then_inc(stored, 16)

            turns(sp, body)
            sp.wait_ge(stored, 16 * PAIRS)

        @block.gpsimd
        def _(pool):
            pool.memset(ident[:], 0.0).then_inc(c_id, 1)
            pool.wait_ge(c_id, 1)
            pool.affine_select(out=ident[:], in_=ident[:], compare_op=ALU.not_equal, fill=1.0, base=0,
                               pattern=[[-1, P]], channel_multiplier=1).then_inc(c_id, 1)
            pool.memset(minus_half[:], -0.5).then_inc(c_misc, 1)
            pool.memset(eps_col[:], EPS).then_inc(c_misc, 1)
            pool.iota(expert_no[:], pattern=[[1, EXPERTS]], base=0, channel_multiplier=0,
                      allow_small_or_imprecise_dtypes=True).then_inc(c_misc, 1)
            pool.memset(ones[:], 1.0).then_inc(c_misc, 1)
            pool.wait_ge(c_id, 2)
            pool.tensor_copy(ident_bf[:], ident[:]).then_inc(c_misc, 1)
            pool.memset(v_diag[:], 0.0).then_inc(c_zero, 1)
            pool.wait_ge(c_misc, 5)

            def rstd(p, s_mv, s_rs, mv, rs, readers):
                pool.wait_ge(s_mv, p.count(2, 2))
                wait(pool, readers, p.before().count(2, 2))
                pool.tensor_tensor(rs[:, 0, :], mv[:, :, 1], eps_col[:], ALU.add).then_inc(s_rs, 1)
                pool.wait_ge(s_rs, p.count(2, 1))
                pool.tensor_tensor(rs[:, 1, :], rs[:, 0, :], minus_half[:], ALU.pow).then_inc(s_rs, 1)

            def body(t):
                for j in range(SLOTS):
                    if p := due(t, j, A_NORM):
                        pool.wait_ge(s_cthi, p.count(1, 1))
                        wait(pool, s_v, p.before().count(1, 1))
                        pool.tensor_tensor(ct_lo[:], ct_in[:], ct_hi[:].bitcast(F32), ALU.subtract).then_inc(s_ctlo, 1)
                        rstd(p, s_amv, s_ars, a_mv, a_rs, s_axn)
                    if p := due(t, j, M_NORM):
                        rstd(p, s_mmv, s_mrs, m_mv, m_rs, s_mxn)
                    if p := due(t, j, F_NORM):
                        rstd(p, s_fmv, s_frs, f_mv, f_rs, s_fc)
                        wait(pool, s_x3, p.before().count(1, 1))
                        pool.wait_ge(s_y, p.count(2 * EXPERTS, 2 * EXPERTS))
                        pool.wait_ge(c_thbo, 2)
                        pool.tensor_tensor(y_res[:], y[:], bl_all[:].unsqueeze(1).to_broadcast([P, 2, P]),
                                           ALU.add).then_inc(s_fyb, 1)
                    if p := due(t, j, G_NORM + 1):
                        rstd(p, s_gmv, s_grs, g_mv, g_rs, s_gh)
                    if p := due(t, j, F_NORM + 9):
                        pool.wait_ge(s_fc2, p.count(1, 1))
                        wait(pool, s_fz, p.before().count(1, 1))
                        pool.tensor_tensor(f_prod[:], f_ct[:], f_c2q[:], ALU.mult).then_inc(s_fpr, 1)
                    if p := due(t, j, A_UNIT[1] + 1):
                        pool.wait_ge(ld_res, p.count(16, 16))
                        pool.wait_ge(c_thbo, 1)
                        pool.tensor_tensor(x_res[:], x_res[:], bo_all[:].unsqueeze(1).to_broadcast([P, 2, P]),
                                           ALU.add).then_inc(s_xb, 1)
                    for u in range(4):
                        b, k0 = u // 2, HALF * (u % 2)
                        e = attn[:, b, :, k0:k0 + HALF]
                        if p := due(t, j, A_UNIT[u] + 1):
                            pool.wait_ge(s_exp, p.count(4, u + 1))
                            wait(pool, s_hinv, p.count(4, u))
                            src, at, n = e, 0, HEADS // 2
                            lvl = 0
                            while n:
                                lvl += 1
                                dst = tree[:, at:at + n, :]
                                pool.tensor_tensor(dst, src[:, 0:n, :], src[:, n:2 * n, :], ALU.add).then_inc(s_tree, 1)
                                if n > 1:
                                    pool.wait_ge(s_tree, p.count(16, 4 * u + lvl))
                                src, at, n = dst, at + n, n // 2
                        if p := due(t, j, A_UNIT[u] + 2):
                            pool.wait_ge(s_hinv, p.count(4, u + 1))
                            pool.tensor_tensor(e, e, head_inv[:].unsqueeze(1).to_broadcast([P, HEADS, HALF]),
                                               ALU.mult).then_inc(s_attn, 1)

            turns(pool, body)

        @block.scalar
        def _(act):
            act.preload_act_table(ACT.Exp)
            for src, dst in (("wq", wqkv_raw[:, 0]), ("wk", wqkv_raw[:, 1]), ("wv", wqkv_raw[:, 2]),
                             ("bq", bqk[:, 0:1]), ("bk", bqk[:, 1:2])):
                act.dma_start(dst, A[src]).then_inc(w_attn, 16)
            act.dma_start(bv_all[:], A["bv"].partition_broadcast(P)).then_inc(w_attn, 16)
            act.dma_start(wo_t[:], A["wo"]).then_inc(w_attn, 16)
            act.dma_start(bo_all[:], A["bo"].partition_broadcast(P)).then_inc(w_attn, 16)
            act.dma_start(gains[:, 0:2], A["g_xattn"].partition_broadcast(P)).then_inc(w_attn, 16)
            act.dma_start(gains[:, 2:4], A["g_ffn"].partition_broadcast(P)).then_inc(w_attn, 16)
            act.dma_start(w01_raw[:, 0].rearrange("e (n h) -> e n h", n=EXPERTS),
                          A["w0"].rearrange("n e h -> e n h")).then_inc(w_moe, 16)
            act.dma_start(w01_raw[:, 1].rearrange("e (n h) -> e n h", n=EXPERTS),
                          A["w1"].rearrange("n e h -> e n h")).then_inc(w_moe, 16)
            act.dma_start(gate_raw[:], A["gate"]).then_inc(w_moe, 16)
            act.dma_start(wdn[:], A["wdn"].rearrange("n (t p) e -> p (n t) e", p=P)).then_inc(w_moe, 16)
            for i, src in enumerate(("w_cq", "w_q", "w_c")):
                act.dma_start(wcq[:, i:i + 1], A[src]).then_inc(w_fin, 16)
            for i, src in enumerate(("b_cq", "b_q", "b_c")):
                act.dma_start(bsum3[:, i:i + 1], A[src].partition_broadcast(P)).then_inc(w_fin, 16)
            act.dma_start(wl[:], A["wl"].rearrange("(k d) o -> d k o", d=P)).then_inc(w_fin, 16)
            act.dma_start(bl_all[:], A["bl"].partition_broadcast(P)).then_inc(w_fin, 16)
            act.dma_start(wf_raw[:, 0], A["wg"]).then_inc(w_ffn, 16)
            act.dma_start(wf_raw[:, 1], A["wu"]).then_inc(w_ffn, 16)
            act.dma_start(wf_raw[:, 2].rearrange("p (k o) -> p k o", k=NI),
                          A["wd"].rearrange("(k p) o -> p k o", p=P)).then_inc(w_ffn, 16)
            act.wait_ge(w_attn, 160)
            act.activation(th[:], gains[:], ACT.Tanh).then_inc(c_th, 1)
            act.wait_ge(c_wq, 1)
            act.activation(wqkv_hi[:], wqkv_raw[:], ACT.Copy).then_inc(c_hi, 1)

            def body(t):
                for j in range(SLOTS):
                    if p := due(t, j, A_NORM):
                        act.wait_ge(ld_a, p.count(32, 32))
                        wait(act, s_v, p.before().count(1, 1))
                        act.activation(ct_hi[:], ct_in[:], ACT.Copy).then_inc(s_cthi, 1)
                    if p := due(t, j, A_XT):
                        act.wait_ge(s_axt, p.count(1, 1))
                        act.activation(a_xhi[:], ps_a[:, 0:TOK], ACT.Copy).then_inc(s_axhi, 1)
                    for n, at in enumerate((A_K, A_Q)):
                        if p := due(t, j, at):
                            act.wait_ge(s_proj[n], p.count(1, 1))
                            wait(act, parts_out[n], p.before().count(16, 16))
                            act.activation(qk_parts[:, n, 0], ps_a[:, 0:TOK], ACT.Identity,
                                           bias=bqk[:, 1 - n:2 - n]).then_inc(s_p1[n], 1)
                    for k in range(TILES):
                        if p := due(t, j, M_UP + k):
                            act.wait_ge(s_z, p.count(TILES, k + 1))
                            wait(act, s_mu, p.count(TILES, k - 1))
                            act.activation(m_tanh[:, k % 2], ps_z[k % 2][:, 0:TOK], ACT.Tanh,
                                           scale=0.5).then_inc(s_mt, 1)
                    if p := due(t, j, M_XT):
                        act.wait_ge(s_mxt, p.count(1, 1))
                        wait(act, s_z, p.before().count(TILES, TILES))
                        act.activation(m_xhi[:], ps_a[:, 0:TOK], ACT.Copy).then_inc(s_mxhi, 1)
                    for u in range(4):
                        if p := due(t, j, A_UNIT[u] + 1):
                            b, k0 = u // 2, HALF * (u % 2)
                            act.wait_ge(s_shift, p.count(4, u + 1))
                            wait(act, s_pv, p.before().count(2, b + 1))
                            act.activation(attn[:, b, :, k0:k0 + HALF], shifted[:, u % 2], ACT.Exp).then_inc(s_exp, 1)
                    for b in range(2):
                        if p := due(t, j, A_OUT[b]):
                            act.wait_ge(s_pv, p.count(2, b + 1))
                            wait(act, s_res, p.before().count(2, b + 1))
                            act.activation(o_t[:, b], ps_a[:, 0:P], ACT.Copy).then_inc(s_ot, 1)
                    if p := due(t, j, M_GATE + 1):
                        act.wait_ge(s_tdf, p.count(1, 1))
                        wait(act, s_tp, p.before().count(4, 4))
                        act.activation(texp[:], tdiff[:], ACT.Exp).then_inc(s_texp, 1)
                    if p := due(t, j, F_NORM + 2):
                        act.wait_ge(s_fct, p.count(1, 1))
                        wait(act, s_fz, p.before().count(1, 1))
                        act.activation(f_ct[:], ps_f[:, 0:TOK], ACT.Copy).then_inc(s_fcs, 1)
                        wait(act, s_fs, p.before().count(1, 1))
                        act.activation(f_ctq[:], ps_f[:, 0:TOK], ACT.Identity, scale=wcq[:, 0:1],
                                       bias=wcq[:, 1:2]).then_inc(s_fcq, 1)
                    if p := due(t, j, F_NORM + 4):
                        act.wait_ge(s_fm, p.count(1, 1))
                        wait(act, s_fan, p.before().count(2, 2))
                        for b in range(2):
                            act.activation(f_a[:, b], ps_f[:, b * P:(b + 1) * P], ACT.Exp, bias=f_nmax[:, b:b + 1],
                                           accum_out=f_asum[:, b:b + 1]).then_inc(s_fa, 1)
                    if p := due(t, j, F_NORM + 6):
                        act.wait_ge(s_fat, p.count(1, 1))
                        wait(act, s_fq, p.before().count(1, 1))
                        act.activation(f_at[:], ps_f[:, 0:TOK], ACT.Copy).then_inc(s_fats, 1)
                    if p := due(t, j, F_NORM + 7):
                        act.wait_ge(s_fnmm, p.count(1, 1))
                        wait(act, s_fei, p.before().count(1, 1))
                        wait(act, s_fe, p.before().count(4, 4))
                        wait(act, s_fq, p.before().count(1, 1))
                        for b in range(2):
                            act.activation(f_erow[:, b], ps_f[:, TOK + b * P:TOK + (b + 1) * P], ACT.Exp,
                                           bias=f_nmm[:, b:b + 1], accum_out=f_esum[:, b:b + 1]).then_inc(s_fe, 1)
                        for b in range(2):
                            act.activation(f_e[:, b:b + 1], f_m[:, b:b + 1], ACT.Exp,
                                           bias=f_nmm[:, b:b + 1]).then_inc(s_fe, 1)
                    if p := due(t, j, F_NORM + 8):
                        act.wait_ge(s_fq, p.count(1, 1))
                        wait(act, s_fz, p.before().count(1, 1))
                        wait(act, s_fpr, p.before().count(1, 1))
                        act.activation(f_c2q[:], ps_f[:, 0:TOK], ACT.Copy).then_inc(s_fc2, 1)
                    if p := due(t, j, G_NORM + 3):
                        act.wait_ge(s_gqt, p.count(1, 1))
                        wait(act, s_gu, p.before().count(4, 4))
                        act.activation(g_qt[:], ps_g[:, 0:P].bitcast(BF16), ACT.Copy).then_inc(s_gqs, 1)
                    for u in range(4):
                        if p := due(t, j, G_UNIT[u]):
                            act.wait_ge(s_gu, p.count(4, u + 1))
                            wait(act, s_guu, p.count(4, u))
                            act.activation(g_tanh[:], ps_g[:, 0:256], ACT.Tanh,
                                           scale=g_sc[:, u // 2, 1:2]).then_inc(s_gt, 1)
                    for b in range(2):
                        if p := due(t, j, G_NORM + 11 + 2 * b):
                            act.wait_ge(s_gpr, p.count(2, b + 1))
                            wait(act, s_gpt, p.before().count(2, 2))
                            act.activation(g_pq[:, b], g_pr[:, b], ACT.Copy, bias=-ROUND).then_inc(s_gpq, 1)
                        if p := due(t, j, G_NORM + 12 + 2 * b):
                            act.wait_ge(s_gpt, p.count(2, b + 1))
                            wait(act, s_gd, p.before().count(2, 2))
                            act.activation(g_pt[:, b], ps_g[:, 0:TOK].bitcast(BF16), ACT.Copy).then_inc(s_gpts, 1)
                if t.first:
                    act.wait_ge(w_moe, 64)
                    act.activation(w01_hi[:], w01_raw[:], ACT.Copy).then_inc(c_mhi, 1)
                    act.activation(gate_hi[:], gate_raw[:], ACT.Copy).then_inc(c_mhi, 1)

            turns(act, body)

        @block.tensor
        def _(pe):
            def split_product(dst, hi_w, lo_w, hi_x, lo_x):
                pe.matmul(dst, hi_w, hi_x, start=True, stop=False)
                pe.matmul(dst, lo_w, hi_x, start=False, stop=False)
                return pe.matmul(dst, hi_w, lo_x, start=False, stop=True)

            def body(t):
                for j in range(SLOTS):
                    for u in range(4):
                        if p := due(t, j, A_UNIT[u]):
                            b, k0 = u // 2, HALF * (u % 2)
                            if u == 0:
                                for n in range(2):
                                    pe.wait_ge(rows_in[n], p.count(192, 192))
                            wait(pe, s_shift, p.count(4, u))
                            for hp in range(HEADS // 2):
                                for hq in range(2):
                                    r = slice(hq * HALF, hq * HALF + 6 * DH)
                                    last = pe.matmul(ps_sc[:, hq, hp * HALF:(hp + 1) * HALF],
                                                     k_rows[r, hp, b * P:(b + 1) * P],
                                                     q_rows[r, hp, b * P + k0:b * P + k0 + HALF],
                                                     start=True, stop=True, tile_position=(hq * HALF, 0))
                            last.then_inc(s_score, 1)
                    if p := due(t, j, M_XT):
                        if n := p.after():
                            pe.wait_ge(s_vd, n.count(2, 2))
                        pe.wait_ge(s_mxn, p.count(2, 2))
                        for b in range(2):
                            last = pe.transpose(ps_a[:, b * P:(b + 1) * P], m_xn[:, b], ident[:])
                        last.then_inc(s_mxt, 1)
                    if p := due(t, j, M_GATE):
                        pe.wait_ge(s_mxlo, p.count(1, 1))
                        if p.first:
                            pe.wait_ge(c_mlo, 2)
                        for b in range(2):
                            s = slice(b * P, (b + 1) * P)
                            last = split_product(ps_a[:, b * EXPERTS:(b + 1) * EXPERTS], m_xhi[:, s],
                                                 m_xlo[:, s], gate_hi[:], gate_lo[:])
                        last.then_inc(s_gate, 1)
                    if p := due(t, j, A_XT):
                        if t.first:
                            pe.wait_ge(c_id, 2)
                            pe.wait_ge(c_misc, 5)
                        pe.wait_ge(s_axn, p.count(2, 2))
                        wait(pe, s_log, p.before(2).count(1, 1))
                        wait(pe, s_vd, p.before().count(2, 2))
                        for b in range(2):
                            last = pe.transpose(ps_a[:, b * P:(b + 1) * P], a_xn[:, b], ident[:])
                        last.then_inc(s_axt, 1)
                    if p := due(t, j, A_K):
                        if t.first:
                            pe.wait_ge(c_lo, 1)
                        pe.wait_ge(s_ctlo, p.count(1, 1))
                        pe.wait_ge(s_axlo, p.count(1, 1))
                        split_product(ps_a[:, 0:TOK], wqkv_hi[:, 1], wqkv_lo[:, 1], ct_hi[:], ct_lo[:]
                                      ).then_inc(s_proj[0], 1)
                    if p := due(t, j, A_Q):
                        pe.wait_ge(s_rest[0], p.count(1, 1))
                        split_product(ps_a[:, 0:TOK], wqkv_hi[:, 0], wqkv_lo[:, 0], a_xhi[:], a_xlo[:]
                                      ).then_inc(s_proj[1], 1)
                    if p := due(t, j, A_V):
                        pe.wait_ge(s_rest[1], p.count(1, 1))
                        wait(pe, s_x1, p.before().count(2, 2))
                        for b in range(2):
                            s = slice(b * P, (b + 1) * P)
                            last = split_product(ps_a[:, s], ct_hi[:, s], ct_lo[:, s], wqkv_hi[:, 2], wqkv_lo[:, 2])
                        last.then_inc(s_v, 1)
                    if p := due(t, j, F_NORM + 2):
                        pe.wait_ge(s_fc, p.count(2, 2))
                        wait(pe, s_x3, p.before().count(1, 1))
                        for b in range(2):
                            last = pe.transpose(ps_f[:, b * P:(b + 1) * P], f_c[:, b], ident[:])
                        last.then_inc(s_fct, 1)
                    if p := due(t, j, F_NORM + 3):
                        pe.wait_ge(s_fcq, p.count(1, 1))
                        pe.wait_ge(ld_f, p.count(32, 32))
                        for b in range(2):
                            s = slice(b * P, (b + 1) * P)
                            pe.matmul(ps_f[:, s], f_ctq[:, s], ctf_in[:, s], start=True, stop=True)
                        for b in range(2):
                            s = slice(b * P, (b + 1) * P)
                            last = pe.matmul(ps_f[:, TOK + b:TOK + b + 1], f_ct[:, s], wcq[:, 2:3],
                                             start=True, stop=True)
                        last.then_inc(s_fs, 1)
                    if p := due(t, j, F_NORM + 6):
                        pe.wait_ge(s_fan, p.count(2, 2))
                        for b in range(2):
                            pe.transpose(ps_f[:, b * P:(b + 1) * P], f_an[:, b], ident[:])
                        for b in range(2):
                            last = pe.matmul(ps_f[:, TOK + b * P:TOK + (b + 1) * P],
                                             f_m[:, b:b + 1].to_broadcast([P, P]), ident[:], start=True, stop=True)
                        last.then_inc(s_fat, 1)
                    if p := due(t, j, F_NORM + 8):
                        pe.wait_ge(s_fats, p.count(1, 1))
                        pe.wait_ge(s_fe, p.count(4, 4))
                        for b in range(2):
                            pe.matmul(ps_f[:, b * P:(b + 1) * P], ctx_in[:, b], f_at[:, b * P:(b + 1) * P],
                                      start=True, stop=True)
                        for b in range(2):
                            last = pe.matmul(ps_f[:, TOK + b:TOK + b + 1], f_c[:, b], f_e[:, b:b + 1],
                                             start=True, stop=True)
                        last.then_inc(s_fq, 1)
                    if p := due(t, j, F_NORM + 10):
                        pe.wait_ge(s_fw, p.count(2, 2))
                        pe.wait_ge(s_fpr, p.count(1, 1))
                        for b in range(2):
                            s = slice(b * P, (b + 1) * P)
                            pe.matmul(ps_f[:, s], f_ct[:, s], f_w14[:, b], start=True, stop=False)
                            pe.matmul(ps_f[:, s], f_c2q[:, s], wl[:, 1], start=False, stop=False)
                            last = pe.matmul(ps_f[:, s], f_prod[:, s], wl[:, 2], start=False, stop=True)
                        last.then_inc(s_fz, 1)
                    if p := due(t, j, G_NORM + 3):
                        pe.wait_ge(s_gq, p.count(1, 1))
                        wait(pe, s_o, p.before().count(2, 2))
                        for b in range(2):
                            last = pe.transpose(ps_g[:, b * HALF:(b + 1) * HALF].bitcast(BF16), g_q[:, b], ident_bf[:])
                        last.then_inc(s_gqt, 1)
                    for u in range(4):
                        if p := due(t, j, G_UNIT[u]):
                            b, c0 = u // 2, 256 * (u % 2)
                            pe.wait_ge(s_gqs, p.count(1, 1))
                            wait(pe, s_gp, p.count(4, u))
                            for n in range(2):
                                last = pe.matmul(ps_g[:, 256 * n:256 * (n + 1)], g_qt[:, b * P:(b + 1) * P],
                                                 wf_q[:, n, c0:c0 + 256], start=True, stop=True)
                            last.then_inc(s_gu, 1)
                    for b in range(2):
                        if p := due(t, j, G_NORM + 12 + 2 * b):
                            pe.wait_ge(s_gpq, p.count(2, b + 1))
                            pe.wait_ge(s_gp, p.count(4, 4))
                            wait(pe, s_o, p.count(2, b))
                            for k in range(NI):
                                last = pe.transpose(ps_g[:, k * HALF:(k + 1) * HALF].bitcast(BF16),
                                                    g_pq[:, b, k * P:(k + 1) * P], ident_bf[:])
                            last.then_inc(s_gpt, 1)
                        if p := due(t, j, G_NORM + 13 + 2 * b):
                            pe.wait_ge(s_gpts, p.count(2, b + 1))
                            for k in range(NI):
                                last = pe.matmul(ps_g[:, 0:P], g_pt[:, b, k * P:(k + 1) * P],
                                                 wf_q[:, 2, k * P:(k + 1) * P], start=(k == 0), stop=(k == NI - 1))
                            last.then_inc(s_gd, 1)
                    for b in range(2):
                        if p := due(t, j, A_OUT[b]):
                            pe.wait_ge(s_attn, p.count(4, 2 * b + 2))
                            if b == 0:
                                pe.wait_ge(s_vd, p.count(2, 2))
                                wait(pe, s_log, p.before().count(1, 1))
                                if n := p.after():
                                    pe.wait_ge(s_rest[1], n.count(1, 1))
                            else:
                                pe.wait_ge(s_x1, p.count(2, 1))
                            for m in range(HEADS):
                                last = pe.matmul(ps_a[:, 0:P], v_diag[:, b, m * P:(m + 1) * P], attn[:, b, m],
                                                 start=(m == 0), stop=(m == HEADS - 1))
                            last.then_inc(s_pv, 1)
                        if p := due(t, j, A_OUT[b] + 1):
                            pe.wait_ge(s_ot, p.count(2, b + 1))
                            pe.matmul(ps_a[:, 0:P], o_t[:, b], wo_t[:], start=True, stop=True).then_inc(s_res, 1)
                    for n in range(EXPERTS):
                        if p := due(t, j, M_UP + TPE * n + 3):
                            pe.wait_ge(s_mh, p.count(TILES, TPE * (n + 1)))
                            wait(pe, s_y, p.count(2 * EXPERTS, 2 * n))
                            for b in range(2):
                                for k in range(TPE):
                                    m = TPE * n + k
                                    last = pe.matmul(ps_d[:, b * P:(b + 1) * P], m_h[:, m % 4, b * P:(b + 1) * P],
                                                     wdn[:, m], start=(k == 0), stop=(k == TPE - 1))
                            last.then_inc(s_dn, 1)
                    for k in range(TILES):
                        if p := due(t, j, M_UP + k):
                            if k == 0:
                                pe.wait_ge(s_mxlo, p.count(1, 1))
                            wait(pe, s_mh, p.count(TILES, k - 1))
                            for n in range(2):
                                w = slice(k * P, (k + 1) * P)
                                last = split_product(ps_z[k % 2][:, n * TOK:(n + 1) * TOK], w01_hi[:, n, w],
                                                     w01_lo[:, n, w], m_xhi[:], m_xlo[:])
                            last.then_inc(s_z, 1)
                if isinstance(t.i, int) and t.c == 1:
                    pe.wait_ge(c_abs, 1)
                    pe.matmul(ps_g[:, 0:3], ones[:], wabs[:], start=True, stop=True).then_inc(c_tot, 1)

            turns(pe, body)

        @block.vector
        def _(dve):
            inv = float(DH) ** -0.5
            dve.wait_ge(w_attn, 160)
            dve.tensor_scalar(wqkv_raw[:, 0], wqkv_raw[:, 0], inv, None, ALU.mult).then_inc(c_wq, 1)
            dve.tensor_scalar(bqk[:, 0:1], bqk[:, 0:1], inv, None, ALU.mult).then_inc(c_wq, 1)
            dve.wait_ge(c_th, 1)
            dve.tensor_scalar(bo_all[:], bo_all[:], th[:, 0:1], None, ALU.mult).then_inc(c_thbo, 1)
            dve.tensor_scalar(th_half[:], th[:, 2:3], 0.5, None, ALU.mult).then_inc(c_thh, 1)
            dve.wait_ge(c_hi, 1)
            dve.tensor_tensor(wqkv_lo[:], wqkv_raw[:], wqkv_hi[:].bitcast(F32), ALU.subtract).then_inc(c_lo, 1)

            def stats(p, src, st, mv, s_st, s_mv, reader):
                wait(dve, s_mv, p.before().count(2, 2))
                for b in range(2):
                    dve.bn_stats(st[:, b], src[:, b]).then_inc(s_st, 1)
                wait(dve, reader, p.before().count(2, 2))
                for b in range(2):
                    dve.wait_ge(s_st, p.count(2, b + 1))
                    dve.sem_inc(s_passed, 1)
                    dve.bn_aggr(mv[:, b], st[:, b]).then_inc(s_mv, 1)

            def normalise(p, dst, src, mv, rs, s_rs, s_done):
                dve.wait_ge(s_rs, p.count(2, 2))
                for b in range(2):
                    dve.tensor_scalar(dst[:, b], src[:, b], mv[:, b, 0:1], rs[:, 1, b:b + 1], ALU.subtract,
                                      ALU.mult).then_inc(s_done, 1)

            def body(t):
                for j in range(SLOTS):
                    for u in range(4):
                        if p := due(t, j, A_UNIT[u]):
                            dve.wait_ge(s_score, p.count(4, u + 1))
                            wait(dve, s_shift, p.count(4, u - 1))
                            sc = ps_sc[:].rearrange("p a (h k) -> p (a h) k", k=HALF)
                            dve.tensor_reduce(head_max[:, u % 2], sc.rearrange("p h k -> p k h"), AX.X,
                                              ALU.max).then_inc(s_hmax, 1)
                            dve.wait_ge(s_hmax, p.count(4, u + 1))
                            wait(dve, s_exp, p.count(4, u - 1))
                            dve.tensor_tensor(shifted[:, u % 2], sc,
                                              head_max[:, u % 2].unsqueeze(1).to_broadcast([P, HEADS, HALF]),
                                              ALU.subtract).then_inc(s_shift, 1)
                        if p := due(t, j, A_UNIT[u] + 2):
                            dve.wait_ge(s_tree, p.count(16, 4 * u + 4))
                            wait(dve, s_attn, p.count(4, u))
                            dve.reciprocal(head_inv[:], tree[:, 14]).then_inc(s_hinv, 1)
                    if p := due(t, j, F_NORM):
                        dve.wait_ge(s_y, p.count(2 * EXPERTS, 2 * EXPERTS))
                        stats(p, y, f_st, f_mv, s_fst, s_fmv, s_fc)
                    if p := due(t, j, F_NORM + 1):
                        wait(dve, s_fq, p.before().count(1, 1))
                        normalise(p, f_c, y, f_mv, f_rs, s_frs, s_fc)
                    if p := due(t, j, M_XT):
                        dve.wait_ge(s_mxhi, p.count(1, 1))
                        dve.tensor_tensor(m_xlo[:], ps_a[:, 0:TOK], m_xhi[:].bitcast(F32),
                                          ALU.subtract).then_inc(s_mxlo, 1)
                    if p := due(t, j, M_GATE):
                        dve.wait_ge(s_gate, p.count(1, 1))
                        wait(dve, s_topi, p.before().count(2, 2))
                        dve.tensor_copy(logits[:], ps_a[:, 0:2 * EXPERTS].rearrange("p (b n) -> p b n", b=2)
                                        ).then_inc(s_log, 1)
                    for k in range(TILES):
                        if p := due(t, j, M_UP + k + 1):
                            dve.wait_ge(s_mt, p.count(TILES, k + 1))
                            wait(dve, s_mh, p.count(TILES, k - 1))
                            z = ps_z[k % 2]
                            dve.scalar_tensor_tensor(m_u[:, k % 2], m_tanh[:, k % 2], 1.0, z[:, 0:TOK], ALU.add,
                                                     ALU.mult).then_inc(s_mu, 1)
                            dve.wait_ge(s_mu, p.count(TILES, k + 1))
                            wait(dve, s_dn, p.count(EXPERTS, k // TPE - 1))
                            dve.tensor_tensor(m_h[:, k % 4], m_u[:, k % 2], z[:, TOK:2 * TOK],
                                              ALU.mult).then_inc(s_mh, 1)
                    if p := due(t, j, M_GATE):
                        dve.wait_ge(s_log, p.count(1, 1))
                        for b in range(2):
                            dve.sem_inc(s_passed, 1)
                            dve.max(top[:, b], logits[:, b]).then_inc(s_top, 1)
                        for b in range(2):
                            dve.wait_ge(s_top, p.count(2, b + 1))
                            dve.sem_inc(s_passed, 1)
                            dve.max_index(top_no[:, b], top[:, b], logits[:, b]).then_inc(s_topi, 1)
                        wait(dve, s_texp, p.before().count(1, 1))
                        dve.tensor_tensor(tdiff[:], top[:, :, 1:2], top[:, :, 0:1], ALU.subtract).then_inc(s_tdf, 1)
                        dve.wait_ge(s_topi, p.count(2, 2))
                        wait(dve, s_w12, p.before().count(4, 4))
                        dve.tensor_copy(top_nof[:], top_no[:]).then_inc(s_tp, 1)
                    for n in range(EXPERTS):
                        if p := due(t, j, M_UP + TPE * n + 4):
                            dve.wait_ge(s_dn, p.count(EXPERTS, n + 1))
                            if n == 0:
                                dve.wait_ge(s_w, p.count(2, 2))
                                wait(dve, s_fyb, p.before().count(1, 1))
                                wait(dve, s_fc, p.before().count(2, 2))
                            for b in range(2):
                                if n:
                                    dve.wait_ge(s_y, p.count(2 * EXPERTS, 2 * n - 1 + b))
                                dve.scalar_tensor_tensor(y[:, b], ps_d[:, b * P:(b + 1) * P],
                                                         weights[:, b, n:n + 1], (y if n else x1)[:, b],
                                                         ALU.mult, ALU.add).then_inc(s_y, 1)
                    if p := due(t, j, M_GATE + 2):
                        dve.wait_ge(s_texp, p.count(1, 1))
                        dve.tensor_scalar(tsum[:], texp[:], 1.0, None, ALU.add).then_inc(s_tp, 1)
                        dve.wait_ge(s_tp, p.count(4, 2))
                        dve.reciprocal(tprob[:, :, 0:1], tsum[:]).then_inc(s_tp, 1)
                        dve.wait_ge(s_tp, p.count(4, 3))
                        dve.tensor_tensor(tprob[:, :, 1:2], texp[:], tprob[:, :, 0:1], ALU.mult).then_inc(s_tp, 1)
                        dve.wait_ge(s_tp, p.count(4, 4))
                        wait(dve, s_w, p.before().count(1, 1))
                        for b in range(2):
                            for k, dst in enumerate((w_first, w_second)):
                                dve.tensor_scalar(dst[:, b], expert_no[:], top_nof[:, b, k:k + 1],
                                                  tprob[:, b, k:k + 1], ALU.is_equal, ALU.mult).then_inc(s_w12, 1)
                        dve.wait_ge(s_w12, p.count(4, 4))
                        wait(dve, s_y, p.before().count(2 * EXPERTS, 2 * EXPERTS))
                        dve.tensor_tensor(w_first[:], w_first[:], w_second[:], ALU.add).then_inc(s_w, 1)
                        dve.wait_ge(s_w, p.count(2, 1))
                        dve.tensor_scalar(weights[:], w_first[:], th_half[:, 0:1], None,
                                          ALU.mult).then_inc(s_w, 1)
                    for b in range(2):
                        if p := due(t, j, A_OUT[b] + 2):
                            dve.wait_ge(s_res, p.count(2, b + 1))
                            dve.wait_ge(s_xb, p.count(1, 1))
                            wait(dve, s_y, p.before().count(2 * EXPERTS, 2))
                            dve.scalar_tensor_tensor(x1[:, b], ps_a[:, 0:P], th[:, 0:1], x_res[:, b], ALU.mult,
                                                     ALU.add).then_inc(s_x1, 1)
                    if p := due(t, j, M_NORM):
                        dve.wait_ge(s_x1, p.count(2, 2))
                        stats(p, x1, m_st, m_mv, s_mst, s_mmv, s_mxn)
                    if p := due(t, j, M_NORM + 1):
                        wait(dve, s_mxt, p.before().count(1, 1))
                        normalise(p, m_xn, x1, m_mv, m_rs, s_mrs, s_mxn)
                    if p := due(t, j, A_NORM):
                        dve.wait_ge(ld_a, p.count(32, 32))
                        stats(p, x_in, a_st, a_mv, s_ast, s_amv, s_axn)
                    if p := due(t, j, A_NORM + 1):
                        if t.first:
                            dve.wait_ge(c_misc, 5)
                        wait(dve, s_axt, p.before().count(1, 1))
                        normalise(p, a_xn, x_in, a_mv, a_rs, s_ars, s_axn)
                    if p := due(t, j, A_XT):
                        dve.wait_ge(s_axhi, p.count(1, 1))
                        dve.tensor_tensor(a_xlo[:], ps_a[:, 0:TOK], a_xhi[:].bitcast(F32),
                                          ALU.subtract).then_inc(s_axlo, 1)
                    for n, at in enumerate((A_K, A_Q)):
                        if p := due(t, j, at + 1):
                            dve.wait_ge(s_p1[n], p.count(1, 1))
                            dve.scalar_tensor_tensor(qk_rest[:, n], ps_a[:, 0:TOK], bqk[:, 1 - n:2 - n],
                                                     qk_parts[:, n, 0], ALU.add, ALU.subtract).then_inc(s_rest[n], 1)
                            dve.wait_ge(s_rest[n], p.count(1, 1))
                            dve.tensor_copy(qk_parts[:, n, 1], qk_rest[:, n]).then_inc(s_p2[n], 1)
                            dve.wait_ge(s_p2[n], p.count(1, 1))
                            dve.tensor_tensor(qk_parts[:, n, 2], qk_rest[:, n], qk_parts[:, n, 1],
                                              ALU.subtract).then_inc(s_p3[n], 1)
                    if p := due(t, j, A_V):
                        if t.first:
                            dve.wait_ge(c_zero, 1)
                        dve.wait_ge(s_v, p.count(1, 1))
                        wait(dve, s_pv, p.before().count(2, 2))
                        for b in range(2):
                            dst = v_diag[:, b].rearrange("p (m s) -> p m s", s=VSTEP)[:, :, 0:DH]
                            dve.tensor_tensor(dst, ps_a[:, b * P:(b + 1) * P].rearrange("p (m d) -> p m d", d=DH),
                                              bv_all[:].rearrange("p (m d) -> p m d", d=DH), ALU.add).then_inc(s_vd, 1)
                    if p := due(t, j, F_NORM + 3):
                        dve.wait_ge(s_fs, p.count(1, 1))
                        wait(dve, s_fa, p.before().count(2, 2))
                        dve.tensor_reduce(f_nmax[:], ps_f[:, 0:TOK].rearrange("p (b q) -> p b q", b=2), AX.X, ALU.max,
                                          negate=True).then_inc(s_fnm, 1)
                        dve.wait_ge(s_fnm, p.count(1, 1))
                        wait(dve, s_fe, p.before().count(4, 4))
                        dve.scalar_tensor_tensor(f_m[:], ps_f[:, TOK:TOK + 2], bsum[:, 0:1], f_nmax[:], ALU.add,
                                                 ALU.subtract).then_inc(s_fm, 1)
                    if p := due(t, j, F_NORM + 5):
                        dve.wait_ge(s_fa, p.count(2, 2))
                        dve.reciprocal(f_ainv[:], f_asum[:]).then_inc(s_fai, 1)
                        dve.wait_ge(s_fai, p.count(1, 1))
                        for b in range(2):
                            dve.tensor_scalar(f_an[:, b], f_a[:, b], f_ainv[:, b:b + 1], None,
                                              ALU.mult).then_inc(s_fan, 1)
                    if p := due(t, j, F_NORM + 6):
                        dve.wait_ge(s_fats, p.count(1, 1))
                        dve.tensor_reduce(f_nmm[:], ps_f[:, TOK:2 * TOK].rearrange("p (b q) -> p b q", b=2), AX.X,
                                          ALU.max, negate=True).then_inc(s_fnmm, 1)
                    if p := due(t, j, F_NORM + 9):
                        dve.wait_ge(s_fe, p.count(4, 2))
                        dve.reciprocal(f_einv[:], f_esum[:]).then_inc(s_fei, 1)
                        dve.wait_ge(s_fei, p.count(1, 1))
                        dve.wait_ge(s_fc2, p.count(1, 1))
                        dve.tensor_tensor(f_q2c[:], ps_f[:, TOK:TOK + 2], f_einv[:], ALU.mult).then_inc(s_fq2, 1)
                        dve.wait_ge(s_fq2, p.count(1, 1))
                        wait(dve, s_fz, p.before().count(1, 1))
                        for b in range(2):
                            dve.scalar_tensor_tensor(f_w14[:, b], wl[:, 3], f_q2c[:, b:b + 1], wl[:, 0], ALU.mult,
                                                     ALU.add).then_inc(s_fw, 1)
                    for b in range(2):
                        if p := due(t, j, G_NORM + 14 + 2 * b):
                            dve.wait_ge(s_gd, p.count(2, b + 1))
                            wait(dve, stored, p.before().count(16, 16))
                            dve.scalar_tensor_tensor(o_sb[:, b], ps_g[:, 0:P], g_ps[:, b, 1:2], x3[:, b], ALU.mult,
                                                     ALU.add).then_inc(s_o, 1)
                    if p := due(t, j, F_NORM + 11):
                        dve.wait_ge(s_fz, p.count(1, 1))
                        dve.wait_ge(s_fyb, p.count(1, 1))
                        wait(dve, s_o, p.before().count(2, 2))
                        dve.scalar_tensor_tensor(x3[:], ps_f[:, 0:TOK].rearrange("p (b d) -> p b d", b=2), th[:, 1:2],
                                                 y_res[:], ALU.mult, ALU.add).then_inc(s_x3, 1)
                        dve.wait_ge(s_x3, p.count(1, 1))
                        stats(p, x3, g_st, g_mv, s_gst, s_gmv, s_gh)
                    if p := due(t, j, G_NORM + 1):
                        wait(dve, s_gr, p.before().count(2, 2))
                        normalise(p, g_h, x3, g_mv, g_rs, s_grs, s_gh)
                        dve.wait_ge(s_gh, p.count(2, 2))
                        dve.tensor_reduce(g_amax[:], g_h[:], AX.X, ALU.max,
                                          apply_absolute_value=True).then_inc(s_gam, 1)
                        dve.wait_ge(s_gam, p.count(1, 1))
                        wait(dve, s_gt, p.before().count(4, 4))
                        dve.tensor_scalar(g_amc[:], g_amax[:], 1e-5, None, ALU.max).then_inc(s_gsc, 1)
                        dve.wait_ge(s_gsc, p.count(5, 1))
                        dve.reciprocal(g_ainv[:], g_amc[:]).then_inc(s_gsc, 1)
                        dve.wait_ge(s_gsc, p.count(5, 2))
                        dve.tensor_scalar(g_sc[:, :, 0], g_ainv[:], 127.0, None, ALU.mult).then_inc(s_gsc, 1)
                        dve.tensor_scalar(g_sc[:, :, 1], g_amc[:], cg[:, 0:1], None, ALU.mult).then_inc(s_gsc, 1)
                        dve.scalar_tensor_tensor(g_sc[:, :, 2], g_amc[:], cg[:, 1:2], g_amc[:], ALU.mult,
                                                 ALU.mult).then_inc(s_gsc, 1)
                        dve.wait_ge(s_gsc, p.count(5, 5))
                        wait(dve, s_gq, p.before().count(1, 1))
                        for b in range(2):
                            dve.tensor_scalar(g_r[:, b], g_h[:, b], g_sc[:, b, 0:1], ROUND, ALU.mult,
                                              ALU.add).then_inc(s_gr, 1)
                        dve.wait_ge(s_gr, p.count(2, 2))
                        wait(dve, s_gqt, p.before().count(1, 1))
                        dve.tensor_scalar(g_q[:], g_r[:], ROUND, 127.0, ALU.subtract, ALU.min).then_inc(s_gq, 1)
                    for u in range(4):
                        if p := due(t, j, G_UNIT[u] + 1):
                            b, c0 = u // 2, 256 * (u % 2)
                            dve.wait_ge(s_gt, p.count(4, u + 1))
                            wait(dve, s_gp, p.count(4, u))
                            dve.scalar_tensor_tensor(g_u[:], g_tanh[:], 1.0, ps_g[:, 0:256], ALU.add,
                                                     ALU.mult).then_inc(s_guu, 1)
                            dve.wait_ge(s_guu, p.count(4, u + 1))
                            wait(dve, s_gpr, p.before().count(2, 2))
                            dve.scalar_tensor_tensor(g_p[:, b, c0:c0 + 256], g_u[:], g_sc[:, b, 2:3], ps_g[:, 256:512],
                                                     ALU.mult, ALU.mult).then_inc(s_gp, 1)
                    for b in range(2):
                        if p := due(t, j, G_UNIT[2 * b + 1] + 1):
                            dve.wait_ge(s_gp, p.count(4, 2 * b + 2))
                            dve.tensor_reduce(g_pmax[:, b:b + 1], g_p[:, b], AX.X, ALU.max,
                                              apply_absolute_value=True).then_inc(s_gpm, 1)
                            dve.wait_ge(s_gpm, p.count(2, b + 1))
                            wait(dve, s_o, p.before().count(2, 2))
                            dve.tensor_scalar(g_pmc[:, b:b + 1], g_pmax[:, b:b + 1], 1e-5, None,
                                              ALU.max).then_inc(s_gps, 1)
                            dve.wait_ge(s_gps, p.count(8, 4 * b + 1))
                            dve.reciprocal(g_pinv[:, b:b + 1], g_pmc[:, b:b + 1]).then_inc(s_gps, 1)
                            dve.wait_ge(s_gps, p.count(8, 4 * b + 2))
                            dve.tensor_scalar(g_ps[:, b, 0:1], g_pinv[:, b:b + 1], 127.0, None,
                                              ALU.mult).then_inc(s_gps, 1)
                            dve.tensor_scalar(g_ps[:, b, 1:2], g_pmc[:, b:b + 1], cg[:, 2:3], None,
                                              ALU.mult).then_inc(s_gps, 1)
                            dve.wait_ge(s_gps, p.count(8, 4 * b + 4))
                            wait(dve, s_gpq, p.before().count(2, 2))
                            dve.tensor_scalar(g_pr[:, b], g_p[:, b], g_ps[:, b, 0:1], ROUND, ALU.mult,
                                              ALU.add).then_inc(s_gpr, 1)
                if t.first:
                    dve.wait_ge(c_mhi, 2)
                    dve.tensor_tensor(w01_lo[:], w01_raw[:], w01_hi[:].bitcast(F32), ALU.subtract).then_inc(c_mlo, 1)
                    dve.tensor_tensor(gate_lo[:], gate_raw[:], gate_hi[:].bitcast(F32), ALU.subtract).then_inc(c_mlo, 1)
                    dve.wait_ge(w_fin, 128)
                    dve.tensor_scalar(bl_all[:], bl_all[:], th[:, 1:2], None, ALU.mult).then_inc(c_thbo, 1)
                    dve.tensor_reduce(bsum[:], bsum3[:], AX.X, ALU.add).then_inc(c_bs, 1)
                    dve.wait_ge(w_ffn, 48)
                    dve.tensor_reduce(wabs[:], wf_raw[:], AX.X, ALU.add, apply_absolute_value=True).then_inc(c_abs, 1)
                if isinstance(t.i, int) and t.c == 1:
                    dve.wait_ge(c_tot, 1)
                    dve.tensor_scalar(wmean[:], ps_g[:, 0:3], 1.0 / (P * INNER), 1e-5, ALU.mult,
                                      ALU.max).then_inc(c_wm, 1)
                    dve.wait_ge(c_wm, 1)
                    dve.reciprocal(wscale[:], wmean[:]).then_inc(c_wm, 1)
                    dve.tensor_scalar(cg[:, 0:1], wmean[:, 0:1], 0.5 / 127.0, None, ALU.mult).then_inc(c_wm, 1)
                    dve.tensor_scalar(cg[:, 2:3], wmean[:, 2:3], th[:, 3:4], 1.0 / 127.0, ALU.mult,
                                      ALU.mult).then_inc(c_wm, 1)
                    dve.wait_ge(c_wm, 3)
                    dve.tensor_scalar(cg[:, 1:2], wmean[:, 1:2], cg[:, 0:1], 1.0 / 127.0, ALU.mult,
                                      ALU.mult).then_inc(c_wm, 1)
                    for n in range(3):
                        dve.tensor_scalar(wf_r[:, n], wf_raw[:, n], wscale[:, n:n + 1], ROUND, ALU.mult,
                                          ALU.add).then_inc(c_wr, 1)
                    dve.wait_ge(c_wr, 3)
                    dve.tensor_scalar(wf_t[:], wf_r[:], ROUND, 1.0, ALU.subtract, ALU.min).then_inc(c_wr, 1)
                    dve.wait_ge(c_wr, 4)
                    dve.tensor_scalar(wf_q[:], wf_t[:], -1.0, None, ALU.max).then_inc(c_wr, 1)

            turns(dve, body)


def kernel(**inputs):
    import numpy as np
    import concourse.bacc as bacc
    from concourse.bass_utils import run_bass_kernel_spmd

    f = {k: np.asarray(v) for k, v in inputs.items()}
    half = HEADS // 2
    rows_qk = lambda w: w.reshape(DH, half, 2, -1).transpose(3, 2, 0, 1).reshape(-1, P)
    rows_v = lambda w: w.reshape(DH, half, 2, -1).transpose(3, 2, 1, 0).reshape(-1, P)
    arrays = {
        "x": f["x"], "ctx": f["ctx_1024"], "ctx_t": f["ctx_1024"].transpose(0, 2, 1),
        "wq": rows_qk(f["L0_xattn_Wq_w"]), "wk": rows_qk(f["L0_xattn_Wk_w"]), "wv": rows_v(f["L0_xattn_Wv_w"]),
        "bq": rows_qk(f["L0_xattn_Wq_b"]).T, "bk": rows_qk(f["L0_xattn_Wk_b"]).T,
        "bv": rows_v(f["L0_xattn_Wv_b"]).reshape(P),
        "wo": rows_v(f["L0_xattn_Wo_w"].T).T, "bo": f["L0_xattn_Wo_b"],
        "g_xattn": f["g_xattn"], "g_ffn": f["g_ffn"],
        "w0": f["L0_ffn_w0_kernel"], "w1": f["L0_ffn_w1_kernel"], "gate": f["L0_ffn_gate_kernel"],
        "wdn": f["L0_ffn_wo_kernel"],
        "w_cq": f["L1_xattn_w_cq"].reshape(P, 1), "w_q": f["L1_xattn_w_q"].reshape(P, 1),
        "w_c": f["L1_xattn_w_c"].reshape(P, 1),
        "b_cq": f["L1_xattn_b_cq"].reshape(1), "b_q": f["L1_xattn_b_q"].reshape(1), "b_c": f["L1_xattn_b_c"].reshape(1),
        "wl": f["L1_xattn_W_l"].T, "bl": f["L1_xattn_b_l"],
        "wg": f["L1_ffn_w_gate"].T, "wu": f["L1_ffn_w_up"].T, "wd": f["L1_ffn_w_down"].T,
    }
    arrays = {k: np.ascontiguousarray(a) for k, a in arrays.items()}
    nc = bacc.Bacc("TRN2", target_bir_lowering=False, num_devices=1)
    aps = {k: nc.dram_tensor(f"in_{k}", a.shape, mybir.dt.from_np(a.dtype), kind="ExternalInput").ap()
           for k, a in arrays.items()}
    out = nc.dram_tensor("out", (BATCH, P, P), F32, kind="ExternalOutput").ap()
    build(nc, aps, out)
    r = run_bass_kernel_spmd(nc, [{f"in_{k}": a for k, a in arrays.items()}], core_ids=[0])
    return r.results[0]["out"]
```

```python
from contextlib import ExitStack

import concourse.bass as bass
from concourse import mybir

ALU = mybir.AluOpType
ACT = mybir.ActivationFunctionType
AX = mybir.AxisListType
F32 = mybir.dt.float32
F32R = mybir.dt.float32r
BF16 = mybir.dt.bfloat16
U32 = mybir.dt.uint32

P = 128
BATCH = 16
PAIRS = BATCH // 2
TOK = 2 * P
HEADS = 16
DH = P // HEADS
HALF = P // 2
EXPERTS = 8
HID = 256
TILES = EXPERTS * HID // P
TPE = HID // P
POOL_TILES = (1, 3, 5, 7, 9, 11, 13)
DVE_TILES = tuple(k for k in range(TILES) if k not in POOL_TILES)
INNER = 512
NI = INNER // P
EPS = 1e-5
ROUND = 1.5 * 2.0 ** 23
VSTEP = P + DH

SLOTS = 189
AT = {
    "sp.load_a": 58, "sp.store_parts": (101, 103), "sp.fetch_rows": (195, 196), "sp.load_res": 278,
    "sp.load_f": 657, "sp.store": 940,
    "pool.ct_lo": 10, "pool.a_rstd": 12, "pool.part3": (107, 116), "pool.x_res": 185,
    "pool.head_sum": (192, 205, 281, 321), "pool.head_norm": (245, 286, 332, 336), "pool.m_rstd": 349,
    "pool.m_h": (427, 465, 507, 515, 523, 527, 528), "pool.top_probs": 448, "pool.f_rstd": 548,
    "pool.y_res": 648, "pool.f_prod": 698, "pool.g_rstd": 750,
    "act.ct_hi": 2, "act.a_xhi": 44, "act.part1": (72, 82), "act.part2": (104, 114),
    "act.head_exp": (182, 194, 230, 312), "act.o_t": (322, 366), "act.m_xhi": 377,
    "act.m_tanh": (389, 412, 418, 426, 438, 452, 461, 502, 514, 516, 544, 548, 552, 554, 558, 559),
    "act.top_exp": 421, "act.f_ct": 570, "act.f_exp": 609, "act.f_an": 622, "act.f_at": 645,
    "act.f_exp_max": 655, "act.f_c2q": 683, "act.g_qt": 769, "act.g_tanh": (778, 791, 806, 829),
    "act.g_pr": (821, 871), "act.g_pq": (836, 883), "act.g_pt": (849, 903),
    "pe.a_xt": 52, "pe.kq": (61, 79), "pe.scores": (165, 206, 217, 265), "pe.v": 193,
    "pe.weighted_v": (301, 302, 345, 346), "pe.out": (323, 368), "pe.m_xt": 399,
    "pe.up": (404, 411, 417, 429, 440, 447, 455, 473, 492, 518, 520, 529, 530, 533, 537, 565), "pe.gate": 408,
    "pe.down": (435, 462, 506, 522, 531, 540, 568, 570), "pe.f_ct": 591, "pe.f_scores": 594, "pe.f_at": 641,
    "pe.f_c2q": 667, "pe.f_z": 715, "pe.g_qt": 785, "pe.g_up": (788, 794, 812, 827), "pe.g_pt": (841, 895),
    "pe.g_down": (867, 902),
    "dve.a_stats": 0, "dve.a_norm": 46, "dve.a_xlo": 59, "dve.part_rest": (78, 99),
    "dve.head_max": (163, 198, 212, 289), "dve.head_shift": (172, 205, 229, 294),
    "dve.head_inv": (220, 287, 298, 319), "dve.v_diag": 242, "dve.x1": (325, 360), "dve.m_stats": 362,
    "dve.m_norm": 385, "dve.m_xlo": 393,
    "dve.m_u": (403, 417, 432, 442, 445, 469, 484, 495, 496, 500, 503, 517, 519, 532, 536, 545),
    "dve.logits": 414, "dve.m_h": (416, 439, 453, 485, 497, 504, 531, 542, 547), "dve.top2": 425,
    "dve.weights": 443, "dve.y": (446, 486, 498, 513, 528, 539, 546, 553), "dve.f_stats": 556,
    "dve.f_norm": 575, "dve.f_max": 587, "dve.f_ainv": 623, "dve.f_max_max": 663, "dve.f_w14": 688,
    "dve.x3": 753, "dve.g_norm": 770, "dve.g_amax": 774, "dve.g_q": 775, "dve.g_u": (790, 801, 819, 842),
    "dve.g_p": (793, 804, 822, 850), "dve.g_pquant": (814, 858), "dve.out": (866, 879),
}
LAST = max(max(v) if isinstance(v, tuple) else v for v in AT.values())
TURNS = PAIRS + LAST // SLOTS
LOOP_FROM, LOOP_TO = LAST // SLOTS + 1, PAIRS


class Pair:

    def __init__(self, i, c):
        self.i, self.c = i, c
        self.first = isinstance(i, int) and c == 0

    def count(self, per_pair, k):
        return self.i * per_pair + (self.c * per_pair + k)

    def before(self, n=1):
        return Pair(self.i, self.c - n)

    def rows(self):
        return slice(self.c, self.c + 1) if isinstance(self.i, int) else bass.ds(self.i + self.c, 1)

    def after(self):
        return Pair(self.i, self.c + 1) if not isinstance(self.i, int) or self.c + 1 < PAIRS else None


def due(turn, j, step, n=None):
    offset = AT[step] if n is None else AT[step][n]
    if (j - offset) % SLOTS:
        return None
    p = Pair(turn.i, turn.c - (offset - j) // SLOTS)
    return p if not isinstance(turn.i, int) or 0 <= p.c < PAIRS else None


def wait(eng, sem, value):
    if not isinstance(value, int) or value > 0:
        eng.wait_ge(sem, value)


def turns(eng, body):
    for t in range(LOOP_FROM):
        body(Pair(0, t))
    with eng.Fori(0, LOOP_TO - LOOP_FROM) as i:
        body(Pair(i, LOOP_FROM))
    for t in range(LOOP_TO, TURNS):
        body(Pair(0, t))


def build(nc, A, out):
    ctx = ExitStack()
    with ctx:
        def sb(name, shape, dt=F32):
            return ctx.enter_context(nc.sbuf_tensor(name, shape, dt))

        def bank(name, shape=(P, 512)):
            return ctx.enter_context(nc.psum_tensor(name, list(shape), F32))

        def sem(name):
            return ctx.enter_context(nc.semaphore(name))

        wqkv_raw = sb("wqkv_raw", [P, 3, P])
        wqkv_hi = sb("wqkv_hi", [P, 3, P], F32R)
        wqkv_lo = sb("wqkv_lo", [P, 3, P], F32R)
        bqk = sb("bqk", [P, 2])
        bv_all = sb("bv_all", [P, P])
        wo_t = sb("wo_t", [P, P])
        bo_all = sb("bo_all", [P, P])
        gains = sb("gains", [P, 4])
        th = sb("th", [P, 4])
        th_half = sb("th_half", [P, 1])
        w01_raw = sb("w01_raw", [P, 2, TILES * P])
        w01_hi = sb("w01_hi", [P, 2, TILES * P], F32R)
        w01_lo = sb("w01_lo", [P, 2, TILES * P], F32R)
        wdn = sb("wdn", [P, TILES, P])
        gate_raw = sb("gate_raw", [P, EXPERTS])
        gate_hi = sb("gate_hi", [P, EXPERTS], F32R)
        gate_lo = sb("gate_lo", [P, EXPERTS], F32R)
        wcq = sb("wcq", [P, 3])
        bsum3 = sb("bsum3", [P, 3])
        bsum = sb("bsum", [P, 1])
        wl = sb("wl", [P, 4, P])
        bl_all = sb("bl_all", [P, P])
        wf_raw = sb("wf_raw", [P, 3, INNER])
        wf_r = sb("wf_r", [P, 3, INNER])
        wf_t = sb("wf_t", [P, 3, INNER])
        wf_q = sb("wf_q", [P, 3, INNER], BF16)
        wabs = sb("wabs", [P, 3])
        wmean = sb("wmean", [P, 3])
        wscale = sb("wscale", [P, 3])
        cg = sb("cg", [P, 3])
        ident = sb("ident", [P, P])
        ident_bf = sb("ident_bf", [P, P], BF16)
        ones = sb("ones", [P, P])
        minus_half = sb("minus_half", [P, 2])
        eps_col = sb("eps_col", [P, 2])
        round_col = sb("round_col", [P, 1])
        minus_one = sb("minus_one", [P, 1])
        expert_no = sb("expert_no", [P, EXPERTS])

        x_in = sb("x_in", [P, 2, P])
        x_res = sb("x_res", [P, 2, P])
        ct_in = sb("ct_in", [P, TOK])
        ct_hi = sb("ct_hi", [P, TOK], F32R)
        ct_lo = sb("ct_lo", [P, TOK], F32R)
        a_st = sb("a_st", [P, 2, 6])
        a_mv = sb("a_mv", [P, 2, 2])
        a_rs = sb("a_rs", [P, 2, 2])
        a_xn = sb("a_xn", [P, 2, P])
        a_xhi = sb("a_xhi", [P, TOK], F32R)
        a_xlo = sb("a_xlo", [P, TOK], F32R)
        qk_parts = sb("qk_parts", [P, 2, 3, TOK], BF16)
        qk_rest = sb("qk_rest", [P, 2, TOK])
        k_rows = sb("k_rows", [P, HEADS // 2, TOK], BF16)
        q_rows = sb("q_rows", [P, HEADS // 2, TOK], BF16)
        v_diag = sb("v_diag", [P, 2, HEADS * VSTEP])
        head_max = sb("head_max", [P, 2, HALF])
        shifted = sb("shifted", [P, 2, HEADS, HALF])
        attn = sb("attn", [P, 2, HEADS, P])
        tree = sb("tree", [P, 2, 15, HALF])
        head_inv = sb("head_inv", [P, 2, HALF])
        o_t = sb("o_t", [P, 2, P])
        x1 = sb("x1", [P, 2, P])

        m_st = sb("m_st", [P, 2, 6])
        m_mv = sb("m_mv", [P, 2, 2])
        m_rs = sb("m_rs", [P, 2, 2])
        m_xn = sb("m_xn", [P, 2, P])
        m_xhi = sb("m_xhi", [P, TOK], F32R)
        m_xlo = sb("m_xlo", [P, TOK], F32R)
        logits = sb("logits", [P, 2, EXPERTS])
        top = sb("top", [P, 2, 8])
        top_no = sb("top_no", [P, 2, 8], U32)
        top_nof = sb("top_nof", [P, 2, 8])
        tdiff = sb("tdiff", [P, 2, 1])
        texp = sb("texp", [P, 2, 1])
        tsum = sb("tsum", [P, 2, 1])
        tprob = sb("tprob", [P, 2, 2])
        w_first = sb("w_first", [P, 2, EXPERTS])
        w_second = sb("w_second", [P, 2, EXPERTS])
        weights = sb("weights", [P, 2, EXPERTS])
        m_tanh = sb("m_tanh", [P, 2, TOK])
        m_u = sb("m_u", [P, 2, TOK])
        m_h = sb("m_h", [P, 4, TOK])
        m_z1 = sb("m_z1", [P, 2, TOK])
        y = sb("y", [P, 2, P])

        ctx_in = sb("ctx_in", [P, 2, P])
        ctf_in = sb("ctf_in", [P, TOK])
        f_st = sb("f_st", [P, 2, 6])
        f_mv = sb("f_mv", [P, 2, 2])
        f_rs = sb("f_rs", [P, 2, 2])
        f_c = sb("f_c", [P, 2, P])
        f_ct = sb("f_ct", [P, TOK])
        f_ctq = sb("f_ctq", [P, TOK])
        f_nmax = sb("f_nmax", [P, 2])
        f_m = sb("f_m", [P, 2])
        f_a = sb("f_a", [P, 2, P])
        f_asum = sb("f_asum", [P, 2])
        f_ainv = sb("f_ainv", [P, 2])
        f_an = sb("f_an", [P, 2, P])
        f_at = sb("f_at", [P, TOK])
        f_nmm = sb("f_nmm", [P, 2])
        f_erow = sb("f_erow", [P, 2, P])
        f_esum = sb("f_esum", [P, 2])
        f_einv = sb("f_einv", [P, 2])
        f_e = sb("f_e", [P, 2])
        f_c2q = sb("f_c2q", [P, TOK])
        f_prod = sb("f_prod", [P, TOK])
        f_q2c = sb("f_q2c", [P, 2])
        f_w14 = sb("f_w14", [P, 2, P])
        y_res = sb("y_res", [P, 2, P])
        x3 = sb("x3", [P, 2, P])

        g_st = sb("g_st", [P, 2, 6])
        g_mv = sb("g_mv", [P, 2, 2])
        g_rs = sb("g_rs", [P, 2, 2])
        g_h = sb("g_h", [P, 2, P])
        g_amax = sb("g_amax", [P, 2])
        g_amc = sb("g_amc", [P, 2])
        g_ainv = sb("g_ainv", [P, 2])
        g_sc = sb("g_sc", [P, 2, 3])
        g_r = sb("g_r", [P, 2, P])
        g_q = sb("g_q", [P, 2, P], BF16)
        g_qt = sb("g_qt", [P, TOK], BF16)
        g_tanh = sb("g_tanh", [P, 256])
        g_u = sb("g_u", [P, 256])
        g_p = sb("g_p", [P, 2, INNER])
        g_pmax = sb("g_pmax", [P, 2])
        g_pmc = sb("g_pmc", [P, 2])
        g_pinv = sb("g_pinv", [P, 2])
        g_ps = sb("g_ps", [P, 2, 2])
        g_pr = sb("g_pr", [P, 2, INNER])
        g_pq = sb("g_pq", [P, 2, INNER], BF16)
        g_pt = sb("g_pt", [P, 2, INNER], BF16)
        o_sb = sb("o_sb", [P, 2, P])

        ps_sc = bank("ps_sc", (P, 2, 512))
        ps_z = [bank("ps_z0"), bank("ps_z1")]
        ps_d = bank("ps_d")
        ps_a = bank("ps_a")
        ps_f = bank("ps_f")
        ps_g = bank("ps_g")

        parts_dram = nc.dram_tensor("parts_dram", (2, PAIRS, P, 3, TOK), BF16, kind="Internal").ap()

        w_attn = sem("w_attn"); w_out = sem("w_out"); w_moe = sem("w_moe"); w_fin = sem("w_fin"); w_ffn = sem("w_ffn")
        ld_a = sem("ld_a"); ld_res = sem("ld_res"); ld_f = sem("ld_f")
        parts_out = [sem("k_parts_out"), sem("q_parts_out")]
        rows_in = [sem("k_rows_in"), sem("q_rows_in")]
        stored = sem("stored")
        c_id = sem("c_id"); c_misc = sem("c_misc"); c_th = sem("c_th"); c_thh = sem("c_thh")
        c_zero = sem("c_zero")
        c_wq = sem("c_wq"); c_hi = sem("c_hi"); c_lo = sem("c_lo"); c_thbo = sem("c_thbo")
        c_mhi = sem("c_mhi"); c_mlo = sem("c_mlo"); c_bs = sem("c_bs")
        c_abs = sem("c_abs"); c_tot = sem("c_tot"); c_wm = sem("c_wm"); c_wr = sem("c_wr")
        s_passed = sem("s_passed"); s_sp_passed = sem("s_sp_passed")
        s_ast = sem("s_ast"); s_amv = sem("s_amv"); s_ars = sem("s_ars"); s_axn = sem("s_axn")
        s_axt = sem("s_axt"); s_axhi = sem("s_axhi"); s_axlo = sem("s_axlo")
        s_cthi = sem("s_cthi"); s_ctlo = sem("s_ctlo")
        s_proj = [sem("s_k"), sem("s_q")]
        s_p1 = [sem("s_k1"), sem("s_q1")]
        s_rest = [sem("s_krest"), sem("s_qrest")]
        s_p2 = [sem("s_k2"), sem("s_q2")]
        s_p3 = [sem("s_k3"), sem("s_q3")]
        s_v = sem("s_v"); s_vd = sem("s_vd")
        s_score = sem("s_score"); s_hmax = sem("s_hmax"); s_shift = sem("s_shift"); s_exp = sem("s_exp")
        s_tree = sem("s_tree"); s_hinv = sem("s_hinv"); s_attn = sem("s_attn")
        s_pv = sem("s_pv"); s_ot = sem("s_ot"); s_res = sem("s_res"); s_xb = sem("s_xb"); s_x1 = sem("s_x1")
        s_mst = sem("s_mst"); s_mmv = sem("s_mmv"); s_mrs = sem("s_mrs"); s_mxn = sem("s_mxn")
        s_mxt = sem("s_mxt"); s_mxhi = sem("s_mxhi"); s_mxlo = sem("s_mxlo")
        s_gate = sem("s_gate"); s_log = sem("s_log"); s_top = sem("s_top"); s_topi = sem("s_topi")
        s_tdf = sem("s_tdf"); s_texp = sem("s_texp"); s_tp = sem("s_tp"); s_tnof = sem("s_tnof"); s_w12 = sem("s_w12"); s_w = sem("s_w")
        s_z = sem("s_z"); s_mt = sem("s_mt"); s_mu = sem("s_mu"); s_mh = sem("s_mh"); s_mhp = sem("s_mhp"); s_z1 = sem("s_z1")
        s_dn = sem("s_dn"); s_y = sem("s_y")
        s_fst = sem("s_fst"); s_fmv = sem("s_fmv"); s_frs = sem("s_frs"); s_fc = sem("s_fc")
        s_fyb = sem("s_fyb"); s_fct = sem("s_fct"); s_fcs = sem("s_fcs"); s_fcq = sem("s_fcq")
        s_fs = sem("s_fs"); s_fnm = sem("s_fnm"); s_fm = sem("s_fm"); s_fa = sem("s_fa"); s_fai = sem("s_fai")
        s_fan = sem("s_fan"); s_fat = sem("s_fat"); s_fats = sem("s_fats"); s_fnmm = sem("s_fnmm")
        s_fe = sem("s_fe"); s_fei = sem("s_fei"); s_fq = sem("s_fq"); s_fc2 = sem("s_fc2"); s_fpr = sem("s_fpr")
        s_fq2 = sem("s_fq2"); s_fw = sem("s_fw"); s_fz = sem("s_fz"); s_x3 = sem("s_x3")
        s_gst = sem("s_gst"); s_gmv = sem("s_gmv"); s_grs = sem("s_grs"); s_gh = sem("s_gh")
        s_gam = sem("s_gam"); s_gsc = sem("s_gsc"); s_gr = sem("s_gr"); s_gq = sem("s_gq")
        s_gqt = sem("s_gqt"); s_gqs = sem("s_gqs"); s_gu = sem("s_gu"); s_gt = sem("s_gt")
        s_guu = sem("s_guu"); s_gp = sem("s_gp"); s_gpm = sem("s_gpm"); s_gps = sem("s_gps")
        s_gpr = sem("s_gpr"); s_gpq = sem("s_gpq"); s_gpt = sem("s_gpt"); s_gpts = sem("s_gpts")
        s_gd = sem("s_gd"); s_o = sem("s_o")

        x_d = A["x"].rearrange("(p b) s d -> p s b d", b=2)
        c_d = A["ctx"].rearrange("(p b) s d -> p s b d", b=2)
        ct_d = A["ctx_t"].rearrange("(p b) d s -> p d b s", b=2)
        o_d = out.rearrange("(p b) s d -> p s b d", b=2)

        def wait_product(eng, p, k):
            q = p.before() if k < 0 else p
            k %= TILES
            if k in POOL_TILES:
                wait(eng, s_mhp, q.count(len(POOL_TILES), POOL_TILES.index(k) + 1))
            else:
                wait(eng, s_mh, q.count(len(DVE_TILES), DVE_TILES.index(k) + 1))

        block = ctx.enter_context(nc.Block())

        @block.sync
        def _(sp):
            def body(t):
                for j in range(SLOTS):
                    if p := due(t, j, "sp.load_a"):
                        q = p.before()
                        wait(sp, s_axn, q.count(2, 2))
                        sp.sem_inc(s_sp_passed, 1)
                        wait(sp, s_ctlo, q.count(1, 1))
                        sp.sem_inc(s_sp_passed, 1)
                        sp.dma_start(x_in[:], x_d[p.rows()].rearrange("o s b d -> s (o b) d")).then_inc(ld_a, 16)
                        sp.dma_start(ct_in[:].rearrange("d (b s) -> d b s", b=2),
                                     ct_d[p.rows()].rearrange("o d b s -> d (o b) s")).then_inc(ld_a, 16)
                    for n in range(2):
                        if p := due(t, j, "sp.store_parts", n):
                            sp.wait_ge(s_p3[n], p.count(1, 1))
                            sp.sem_inc(s_sp_passed, 1)
                            sp.dma_start(parts_dram[n][p.rows()].rearrange("o c r t -> c (o r) t"),
                                         qk_parts[:, n]).then_inc(parts_out[n], 16)
                    for n, rows in enumerate((k_rows, q_rows)):
                        if p := due(t, j, "sp.fetch_rows", n):
                            sp.wait_ge(parts_out[n], p.count(16, 16))
                            sp.sem_inc(s_sp_passed, 1)
                            wait(sp, s_score, p.before().count(4, 4))
                            sp.sem_inc(s_sp_passed, 1)
                            at = 0
                            for a, reps in enumerate((3, 2, 1)):
                                for hq in range(2):
                                    lo = hq * HALF + at * DH
                                    parts = slice(a, a + 1) if n == 0 else slice(0, reps)
                                    src = parts_dram[n][p.rows(), hq * HALF:(hq + 1) * HALF, parts, :]
                                    src = src.rearrange("o (j h) r t -> (o r) j h t", h=HEADS // 2)
                                    if n == 0 and reps > 1:
                                        src = src.to_broadcast([reps, DH, HEADS // 2, TOK])
                                    sp.dma_start(rows[lo:lo + reps * DH, :, :],
                                                 src).then_inc(rows_in[n], 16)
                                at += reps
                    if p := due(t, j, "sp.load_res"):
                        wait(sp, s_x1, p.before().count(2, 2))
                        sp.sem_inc(s_sp_passed, 1)
                        sp.dma_start(x_res[:], x_d[p.rows()].rearrange("o s b d -> s (o b) d")).then_inc(ld_res, 16)
                    if p := due(t, j, "sp.load_f"):
                        wait(sp, s_fq, p.before().count(1, 1))
                        sp.sem_inc(s_sp_passed, 1)
                        sp.dma_start(ctx_in[:], c_d[p.rows()].rearrange("o s b d -> s (o b) d")).then_inc(ld_f, 16)
                        sp.dma_start(ctf_in[:].rearrange("d (b s) -> d b s", b=2),
                                     ct_d[p.rows()].rearrange("o d b s -> d (o b) s")).then_inc(ld_f, 16)
                    if p := due(t, j, "sp.store"):
                        sp.wait_ge(s_o, p.count(2, 2))
                        sp.sem_inc(s_sp_passed, 1)
                        sp.dma_start(o_d[p.rows()].rearrange("o s b d -> s (o b) d"), o_sb[:]).then_inc(stored, 16)

            turns(sp, body)
            sp.wait_ge(stored, 16 * PAIRS)

        @block.gpsimd
        def _(pool):
            pool.memset(ident[:], 0.0).then_inc(c_id, 1)
            pool.wait_ge(c_id, 1)
            pool.affine_select(out=ident[:], in_=ident[:], compare_op=ALU.not_equal, fill=1.0, base=0,
                               pattern=[[-1, P]], channel_multiplier=1).then_inc(c_id, 1)
            pool.memset(minus_half[:], -0.5).then_inc(c_misc, 1)
            pool.memset(eps_col[:], EPS).then_inc(c_misc, 1)
            pool.iota(expert_no[:], pattern=[[1, EXPERTS]], base=0, channel_multiplier=0,
                      allow_small_or_imprecise_dtypes=True).then_inc(c_misc, 1)
            pool.memset(ones[:], 1.0).then_inc(c_misc, 1)
            pool.memset(minus_one[:], -1.0).then_inc(c_misc, 1)
            pool.memset(round_col[:], ROUND).then_inc(c_misc, 1)
            pool.wait_ge(c_id, 2)
            pool.tensor_copy(ident_bf[:], ident[:]).then_inc(c_misc, 1)
            pool.memset(v_diag[:], 0.0).then_inc(c_zero, 1)
            pool.wait_ge(c_misc, 7)

            def rstd(p, s_mv, s_rs, mv, rs, readers):
                pool.wait_ge(s_mv, p.count(2, 2))
                wait(pool, readers, p.before().count(2, 2))
                pool.tensor_tensor(rs[:, 0, :], mv[:, :, 1], eps_col[:], ALU.add).then_inc(s_rs, 1)
                pool.wait_ge(s_rs, p.count(2, 1))
                pool.tensor_tensor(rs[:, 1, :], rs[:, 0, :], minus_half[:], ALU.pow).then_inc(s_rs, 1)

            def body(t):
                for j in range(SLOTS):
                    if p := due(t, j, "pool.ct_lo"):
                        pool.wait_ge(s_cthi, p.count(1, 1))
                        wait(pool, s_v, p.before().count(1, 1))
                        pool.tensor_tensor(ct_lo[:], ct_in[:], ct_hi[:].bitcast(F32), ALU.subtract).then_inc(s_ctlo, 1)
                    if p := due(t, j, "pool.a_rstd"):
                        rstd(p, s_amv, s_ars, a_mv, a_rs, s_axn)
                    for n in range(2):
                        if p := due(t, j, "pool.part3", n):
                            pool.wait_ge(s_p2[n], p.count(1, 1))
                            pool.tensor_tensor(qk_parts[:, n, 2], qk_rest[:, n], qk_parts[:, n, 1],
                                               ALU.subtract).then_inc(s_p3[n], 1)
                    for n, k in enumerate(POOL_TILES):
                        if p := due(t, j, "pool.m_h", n):
                            pool.wait_ge(s_mu, p.count(TILES, k + 1))
                            pool.wait_ge(s_z1, p.count(len(POOL_TILES), n + 1))
                            wait(pool, s_dn, p.count(EXPERTS, k // TPE - 1))
                            pool.tensor_tensor(m_h[:, k % 4], m_u[:, k % 2], m_z1[:, n % 2],
                                               ALU.mult).then_inc(s_mhp, 1)
                    if p := due(t, j, "pool.m_rstd"):
                        rstd(p, s_mmv, s_mrs, m_mv, m_rs, s_mxn)
                    if p := due(t, j, "pool.top_probs"):
                        pool.wait_ge(s_texp, p.count(1, 1))
                        wait(pool, s_w12, p.before().count(4, 4))
                        pool.wait_ge(c_thh, 1)
                        pool.tensor_tensor(tsum[:], texp[:], ones[:, 0:2].unsqueeze(2), ALU.add).then_inc(s_tp, 1)
                        pool.tensor_tensor(texp[:], texp[:], th_half[:].unsqueeze(1).to_broadcast([P, 2, 1]),
                                           ALU.mult).then_inc(s_tp, 1)
                        pool.wait_ge(s_tp, p.count(5, 2))
                        pool.tensor_tensor(tsum[:], tsum[:], minus_one[:].unsqueeze(1).to_broadcast([P, 2, 1]),
                                           ALU.pow).then_inc(s_tp, 1)
                        pool.wait_ge(s_tp, p.count(5, 3))
                        pool.tensor_tensor(tprob[:, :, 0:1], th_half[:].unsqueeze(1).to_broadcast([P, 2, 1]), tsum[:],
                                           ALU.mult).then_inc(s_tp, 1)
                        pool.tensor_tensor(tprob[:, :, 1:2], texp[:], tsum[:], ALU.mult).then_inc(s_tp, 1)
                    if p := due(t, j, "pool.f_rstd"):
                        rstd(p, s_fmv, s_frs, f_mv, f_rs, s_fc)
                    if p := due(t, j, "pool.y_res"):
                        wait(pool, s_x3, p.before().count(1, 1))
                        pool.wait_ge(s_y, p.count(2 * EXPERTS, 2 * EXPERTS))
                        pool.wait_ge(c_thbo, 2)
                        pool.tensor_tensor(y_res[:], y[:], bl_all[:].unsqueeze(1).to_broadcast([P, 2, P]),
                                           ALU.add).then_inc(s_fyb, 1)
                    if p := due(t, j, "pool.g_rstd"):
                        rstd(p, s_gmv, s_grs, g_mv, g_rs, s_gh)
                    if p := due(t, j, "pool.f_prod"):
                        pool.wait_ge(s_fc2, p.count(1, 1))
                        wait(pool, s_fz, p.before().count(1, 1))
                        pool.tensor_tensor(f_prod[:], f_ct[:], f_c2q[:], ALU.mult).then_inc(s_fpr, 1)
                    if p := due(t, j, "pool.x_res"):
                        pool.wait_ge(ld_res, p.count(16, 16))
                        pool.wait_ge(c_thbo, 1)
                        pool.tensor_tensor(x_res[:], x_res[:], bo_all[:].unsqueeze(1).to_broadcast([P, 2, P]),
                                           ALU.add).then_inc(s_xb, 1)
                    for u in range(4):
                        b, k0 = u // 2, HALF * (u % 2)
                        e = attn[:, b, :, k0:k0 + HALF]
                        if p := due(t, j, "pool.head_sum", u):
                            pool.wait_ge(s_exp, p.count(4, u + 1))
                            wait(pool, s_hinv, p.count(4, u - 1))
                            src, at, n = e, 0, HEADS // 2
                            lvl = 0
                            while n:
                                lvl += 1
                                dst = tree[:, u % 2, at:at + n, :]
                                pool.tensor_tensor(dst, src[:, 0:n, :], src[:, n:2 * n, :], ALU.add).then_inc(s_tree, 1)
                                if n > 1:
                                    pool.wait_ge(s_tree, p.count(16, 4 * u + lvl))
                                src, at, n = dst, at + n, n // 2
                        if p := due(t, j, "pool.head_norm", u):
                            pool.wait_ge(s_hinv, p.count(4, u + 1))
                            pool.tensor_tensor(e, e, head_inv[:, u % 2].unsqueeze(1).to_broadcast([P, HEADS, HALF]),
                                               ALU.mult).then_inc(s_attn, 1)

            turns(pool, body)

        @block.scalar
        def _(act):
            act.preload_act_table(ACT.Exp)
            for src, dst in (("wk", wqkv_raw[:, 1]), ("wq", wqkv_raw[:, 0]), ("wv", wqkv_raw[:, 2]),
                             ("bk", bqk[:, 1:2]), ("bq", bqk[:, 0:1])):
                act.dma_start(dst, A[src]).then_inc(w_attn, 16)
            act.dma_start(w01_raw[:, 0].rearrange("e (n h) -> e n h", n=EXPERTS),
                          A["w0"].rearrange("n e h -> e n h")).then_inc(w_moe, 16)
            act.dma_start(w01_raw[:, 1].rearrange("e (n h) -> e n h", n=EXPERTS),
                          A["w1"].rearrange("n e h -> e n h")).then_inc(w_moe, 16)
            act.dma_start(gate_raw[:], A["gate"]).then_inc(w_moe, 16)
            act.dma_start(wdn[:], A["wdn"].rearrange("n (t p) e -> p (n t) e", p=P)).then_inc(w_moe, 16)
            act.dma_start(gains[:, 0:2], A["g_xattn"].partition_broadcast(P)).then_inc(w_out, 16)
            act.dma_start(gains[:, 2:4], A["g_ffn"].partition_broadcast(P)).then_inc(w_out, 16)
            act.dma_start(bo_all[:], A["bo"].partition_broadcast(P)).then_inc(w_out, 16)
            act.dma_start(bv_all[:], A["bv"].partition_broadcast(P)).then_inc(w_out, 16)
            act.dma_start(wo_t[:], A["wo"]).then_inc(w_out, 16)
            for i, src in enumerate(("w_cq", "w_q", "w_c")):
                act.dma_start(wcq[:, i:i + 1], A[src]).then_inc(w_fin, 16)
            for i, src in enumerate(("b_cq", "b_q", "b_c")):
                act.dma_start(bsum3[:, i:i + 1], A[src].partition_broadcast(P)).then_inc(w_fin, 16)
            act.dma_start(wl[:], A["wl"].rearrange("(k d) o -> d k o", d=P)).then_inc(w_fin, 16)
            act.dma_start(bl_all[:], A["bl"].partition_broadcast(P)).then_inc(w_fin, 16)
            act.dma_start(wf_raw[:, 0], A["wg"]).then_inc(w_ffn, 16)
            act.dma_start(wf_raw[:, 1], A["wu"]).then_inc(w_ffn, 16)
            act.dma_start(wf_raw[:, 2].rearrange("p (k o) -> p k o", k=NI),
                          A["wd"].rearrange("(k p) o -> p k o", p=P)).then_inc(w_ffn, 16)
            act.wait_ge(w_attn, 80)
            act.wait_ge(c_wq, 1)
            act.activation(wqkv_hi[:], wqkv_raw[:], ACT.Copy).then_inc(c_hi, 1)

            def first_weights():
                act.wait_ge(w_moe, 64)
                act.activation(w01_hi[:], w01_raw[:], ACT.Copy).then_inc(c_mhi, 1)
                act.activation(gate_hi[:], gate_raw[:], ACT.Copy).then_inc(c_mhi, 1)
                act.wait_ge(w_out, 80)
                act.activation(th[:], gains[:], ACT.Tanh).then_inc(c_th, 1)

            def body(t):
                for j in range(SLOTS):
                    if p := due(t, j, "act.ct_hi"):
                        act.wait_ge(ld_a, p.count(32, 32))
                        wait(act, s_v, p.before().count(1, 1))
                        act.activation(ct_hi[:], ct_in[:], ACT.Copy).then_inc(s_cthi, 1)
                    if p := due(t, j, "act.a_xhi"):
                        act.wait_ge(s_axt, p.count(1, 1))
                        act.activation(a_xhi[:], ps_a[:, 0:TOK], ACT.Copy).then_inc(s_axhi, 1)
                    for n in range(2):
                        if p := due(t, j, "act.part1", n):
                            act.wait_ge(s_proj[n], p.count(1, 1))
                            wait(act, parts_out[n], p.before().count(16, 16))
                            act.activation(qk_parts[:, n, 0], ps_a[:, 0:TOK], ACT.Identity,
                                           bias=bqk[:, 1 - n:2 - n]).then_inc(s_p1[n], 1)
                        if p := due(t, j, "act.part2", n):
                            act.wait_ge(s_rest[n], p.count(1, 1))
                            act.activation(qk_parts[:, n, 1], qk_rest[:, n], ACT.Copy).then_inc(s_p2[n], 1)
                            if p.first and n == 1:
                                first_weights()
                    for k in range(TILES):
                        if p := due(t, j, "act.m_tanh", k):
                            act.wait_ge(s_z, p.count(TILES, k + 1))
                            wait(act, s_mu, p.count(TILES, k - 1))
                            if k in POOL_TILES:
                                n = POOL_TILES.index(k)
                                wait(act, s_mhp, p.count(len(POOL_TILES), n - 1))
                                act.activation(m_z1[:, n % 2], ps_z[k % 2][:, TOK:2 * TOK],
                                               ACT.Copy).then_inc(s_z1, 1)
                            act.activation(m_tanh[:, k % 2], ps_z[k % 2][:, 0:TOK], ACT.Tanh,
                                           scale=0.5).then_inc(s_mt, 1)
                    if p := due(t, j, "act.m_xhi"):
                        act.wait_ge(s_mxt, p.count(1, 1))
                        wait(act, s_z, p.before().count(TILES, TILES))
                        act.activation(m_xhi[:], ps_d[:, 0:TOK], ACT.Copy).then_inc(s_mxhi, 1)
                    for u in range(4):
                        if p := due(t, j, "act.head_exp", u):
                            b, k0 = u // 2, HALF * (u % 2)
                            act.wait_ge(s_shift, p.count(4, u + 1))
                            wait(act, s_pv, p.before().count(2, b + 1))
                            act.activation(attn[:, b, :, k0:k0 + HALF], shifted[:, u % 2], ACT.Exp).then_inc(s_exp, 1)
                    for b in range(2):
                        if p := due(t, j, "act.o_t", b):
                            act.wait_ge(s_pv, p.count(2, b + 1))
                            wait(act, s_res, p.before().count(2, b + 1))
                            act.activation(o_t[:, b], ps_a[:, 0:P], ACT.Copy).then_inc(s_ot, 1)
                    if p := due(t, j, "act.top_exp"):
                        act.wait_ge(s_tdf, p.count(1, 1))
                        wait(act, s_tp, p.before().count(5, 5))
                        act.activation(texp[:], tdiff[:], ACT.Exp).then_inc(s_texp, 1)
                    if p := due(t, j, "act.f_ct"):
                        act.wait_ge(s_fct, p.count(1, 1))
                        wait(act, s_fz, p.before().count(1, 1))
                        act.activation(f_ct[:], ps_f[:, 0:TOK], ACT.Copy).then_inc(s_fcs, 1)
                        wait(act, s_fs, p.before().count(1, 1))
                        act.activation(f_ctq[:], ps_f[:, 0:TOK], ACT.Identity, scale=wcq[:, 0:1],
                                       bias=wcq[:, 1:2]).then_inc(s_fcq, 1)
                    if p := due(t, j, "act.f_exp"):
                        act.wait_ge(s_fm, p.count(1, 1))
                        wait(act, s_fan, p.before().count(2, 2))
                        for b in range(2):
                            act.activation(f_a[:, b], ps_f[:, b * P:(b + 1) * P], ACT.Exp, bias=f_nmax[:, b:b + 1],
                                           accum_out=f_asum[:, b:b + 1]).then_inc(s_fa, 1)
                    if p := due(t, j, "act.f_an"):
                        act.wait_ge(s_fai, p.count(1, 1))
                        wait(act, s_fat, p.before().count(1, 1))
                        for b in range(2):
                            act.activation(f_an[:, b], f_a[:, b], ACT.Identity,
                                           scale=f_ainv[:, b:b + 1]).then_inc(s_fan, 1)
                    if p := due(t, j, "act.f_at"):
                        act.wait_ge(s_fat, p.count(1, 1))
                        wait(act, s_fq, p.before().count(1, 1))
                        act.activation(f_at[:], ps_f[:, 0:TOK], ACT.Copy).then_inc(s_fats, 1)
                    if p := due(t, j, "act.f_exp_max"):
                        act.wait_ge(s_fnmm, p.count(1, 1))
                        wait(act, s_fei, p.before().count(1, 1))
                        wait(act, s_fe, p.before().count(4, 4))
                        wait(act, s_fq, p.before().count(1, 1))
                        for b in range(2):
                            act.activation(f_erow[:, b], ps_f[:, TOK + b * P:TOK + (b + 1) * P], ACT.Exp,
                                           bias=f_nmm[:, b:b + 1], accum_out=f_esum[:, b:b + 1]).then_inc(s_fe, 1)
                        for b in range(2):
                            act.activation(f_e[:, b:b + 1], f_m[:, b:b + 1], ACT.Exp,
                                           bias=f_nmm[:, b:b + 1]).then_inc(s_fe, 1)
                    if p := due(t, j, "act.f_c2q"):
                        act.wait_ge(s_fq, p.count(1, 1))
                        wait(act, s_fz, p.before().count(1, 1))
                        wait(act, s_fpr, p.before().count(1, 1))
                        act.activation(f_c2q[:], ps_f[:, 0:TOK], ACT.Copy).then_inc(s_fc2, 1)
                    if p := due(t, j, "act.g_qt"):
                        act.wait_ge(s_gqt, p.count(1, 1))
                        wait(act, s_gu, p.before().count(4, 4))
                        act.activation(g_qt[:], ps_g[:, 0:P].bitcast(BF16), ACT.Copy).then_inc(s_gqs, 1)
                    for u in range(4):
                        if p := due(t, j, "act.g_tanh", u):
                            act.wait_ge(s_gu, p.count(4, u + 1))
                            wait(act, s_guu, p.count(4, u))
                            act.activation(g_tanh[:], ps_g[:, 0:256], ACT.Tanh,
                                           scale=g_sc[:, u // 2, 1:2]).then_inc(s_gt, 1)
                    for b in range(2):
                        if p := due(t, j, "act.g_pr", b):
                            act.wait_ge(s_gps, p.count(8, 4 * b + 4))
                            wait(act, s_gpq, p.before().count(2, b + 1))
                            act.activation(g_pr[:, b], g_p[:, b], ACT.Identity, scale=g_ps[:, b, 0:1],
                                           bias=round_col[:, 0:1]).then_inc(s_gpr, 1)
                        if p := due(t, j, "act.g_pq", b):
                            act.wait_ge(s_gpr, p.count(2, b + 1))
                            wait(act, s_gpt, p.before().count(2, 2))
                            act.activation(g_pq[:, b], g_pr[:, b], ACT.Copy, bias=-ROUND).then_inc(s_gpq, 1)
                        if p := due(t, j, "act.g_pt", b):
                            act.wait_ge(s_gpt, p.count(2, b + 1))
                            wait(act, s_gd, p.before().count(2, 2))
                            act.activation(g_pt[:, b], ps_g[:, 0:TOK].bitcast(BF16), ACT.Copy).then_inc(s_gpts, 1)

            turns(act, body)

        @block.tensor
        def _(pe):
            def split_product(dst, hi_w, lo_w, hi_x, lo_x):
                pe.matmul(dst, hi_w, hi_x, start=True, stop=False)
                pe.matmul(dst, lo_w, hi_x, start=False, stop=False)
                return pe.matmul(dst, hi_w, lo_x, start=False, stop=True)

            def body(t):
                for j in range(SLOTS):
                    for u in range(4):
                        if p := due(t, j, "pe.scores", u):
                            b, k0 = u // 2, HALF * (u % 2)
                            if u == 0:
                                for n in range(2):
                                    pe.wait_ge(rows_in[n], p.count(96, 96))
                            wait(pe, s_shift, p.count(4, u))
                            for hp in range(HEADS // 2):
                                for hq in range(2):
                                    r = slice(hq * HALF, hq * HALF + 6 * DH)
                                    last = pe.matmul(ps_sc[:, hq, hp * HALF:(hp + 1) * HALF],
                                                     k_rows[r, hp, b * P:(b + 1) * P],
                                                     q_rows[r, hp, b * P + k0:b * P + k0 + HALF],
                                                     start=True, stop=True, tile_position=(hq * HALF, 0))
                            last.then_inc(s_score, 1)
                    if p := due(t, j, "pe.m_xt"):
                        wait(pe, s_y, p.before().count(2 * EXPERTS, 2 * EXPERTS))
                        pe.wait_ge(s_mxn, p.count(2, 2))
                        for b in range(2):
                            last = pe.transpose(ps_d[:, b * P:(b + 1) * P], m_xn[:, b], ident[:])
                        last.then_inc(s_mxt, 1)
                    if p := due(t, j, "pe.gate"):
                        pe.wait_ge(s_mxlo, p.count(1, 1))
                        if p.first:
                            pe.wait_ge(c_mlo, 2)
                        for b in range(2):
                            s = slice(b * P, (b + 1) * P)
                            last = split_product(ps_d[:, b * EXPERTS:(b + 1) * EXPERTS], m_xhi[:, s],
                                                 m_xlo[:, s], gate_hi[:], gate_lo[:])
                        last.then_inc(s_gate, 1)
                    if p := due(t, j, "pe.a_xt"):
                        if t.first:
                            pe.wait_ge(c_id, 2)
                            pe.wait_ge(c_misc, 7)
                        pe.wait_ge(s_axn, p.count(2, 2))
                        wait(pe, s_vd, p.before().count(2, 2))
                        for b in range(2):
                            last = pe.transpose(ps_a[:, b * P:(b + 1) * P], a_xn[:, b], ident[:])
                        last.then_inc(s_axt, 1)
                    if p := due(t, j, "pe.kq", 0):
                        if t.first:
                            pe.wait_ge(c_lo, 1)
                        pe.wait_ge(s_ctlo, p.count(1, 1))
                        pe.wait_ge(s_axlo, p.count(1, 1))
                        split_product(ps_a[:, 0:TOK], wqkv_hi[:, 1], wqkv_lo[:, 1], ct_hi[:], ct_lo[:]
                                      ).then_inc(s_proj[0], 1)
                    if p := due(t, j, "pe.kq", 1):
                        pe.wait_ge(s_rest[0], p.count(1, 1))
                        split_product(ps_a[:, 0:TOK], wqkv_hi[:, 0], wqkv_lo[:, 0], a_xhi[:], a_xlo[:]
                                      ).then_inc(s_proj[1], 1)
                        if p.first:
                            pe.wait_ge(c_abs, 1)
                            pe.matmul(ps_g[:, 0:3], ones[:], wabs[:], start=True, stop=True).then_inc(c_tot, 1)
                    if p := due(t, j, "pe.v"):
                        pe.wait_ge(s_rest[1], p.count(1, 1))
                        wait(pe, s_x1, p.before().count(2, 2))
                        for b in range(2):
                            s = slice(b * P, (b + 1) * P)
                            last = split_product(ps_a[:, s], ct_hi[:, s], ct_lo[:, s], wqkv_hi[:, 2], wqkv_lo[:, 2])
                        last.then_inc(s_v, 1)
                    if p := due(t, j, "pe.f_ct"):
                        pe.wait_ge(s_fc, p.count(2, 2))
                        wait(pe, s_x3, p.before().count(1, 1))
                        for b in range(2):
                            last = pe.transpose(ps_f[:, b * P:(b + 1) * P], f_c[:, b], ident[:])
                        last.then_inc(s_fct, 1)
                    if p := due(t, j, "pe.f_scores"):
                        pe.wait_ge(s_fcq, p.count(1, 1))
                        pe.wait_ge(ld_f, p.count(32, 32))
                        for b in range(2):
                            s = slice(b * P, (b + 1) * P)
                            pe.matmul(ps_f[:, s], f_ctq[:, s], ctf_in[:, s], start=True, stop=True)
                        for b in range(2):
                            s = slice(b * P, (b + 1) * P)
                            last = pe.matmul(ps_f[:, TOK + b:TOK + b + 1], f_ct[:, s], wcq[:, 2:3],
                                             start=True, stop=True)
                        last.then_inc(s_fs, 1)
                    if p := due(t, j, "pe.f_at"):
                        pe.wait_ge(s_fan, p.count(2, 2))
                        for b in range(2):
                            pe.transpose(ps_f[:, b * P:(b + 1) * P], f_an[:, b], ident[:])
                        for b in range(2):
                            last = pe.matmul(ps_f[:, TOK + b * P:TOK + (b + 1) * P],
                                             f_m[:, b:b + 1].to_broadcast([P, P]), ident[:], start=True, stop=True)
                        last.then_inc(s_fat, 1)
                    if p := due(t, j, "pe.f_c2q"):
                        pe.wait_ge(s_fats, p.count(1, 1))
                        pe.wait_ge(s_fe, p.count(4, 4))
                        for b in range(2):
                            pe.matmul(ps_f[:, b * P:(b + 1) * P], ctx_in[:, b], f_at[:, b * P:(b + 1) * P],
                                      start=True, stop=True)
                        for b in range(2):
                            last = pe.matmul(ps_f[:, TOK + b:TOK + b + 1], f_c[:, b], f_e[:, b:b + 1],
                                             start=True, stop=True)
                        last.then_inc(s_fq, 1)
                    if p := due(t, j, "pe.f_z"):
                        pe.wait_ge(s_fw, p.count(2, 2))
                        pe.wait_ge(s_fpr, p.count(1, 1))
                        for b in range(2):
                            s = slice(b * P, (b + 1) * P)
                            pe.matmul(ps_f[:, s], f_ct[:, s], f_w14[:, b], start=True, stop=False)
                            pe.matmul(ps_f[:, s], f_c2q[:, s], wl[:, 1], start=False, stop=False)
                            last = pe.matmul(ps_f[:, s], f_prod[:, s], wl[:, 2], start=False, stop=True)
                        last.then_inc(s_fz, 1)
                    if p := due(t, j, "pe.g_qt"):
                        pe.wait_ge(s_gq, p.count(1, 1))
                        wait(pe, s_o, p.before().count(2, 2))
                        for b in range(2):
                            last = pe.transpose(ps_g[:, b * HALF:(b + 1) * HALF].bitcast(BF16), g_q[:, b], ident_bf[:])
                        last.then_inc(s_gqt, 1)
                    for u in range(4):
                        if p := due(t, j, "pe.g_up", u):
                            b, c0 = u // 2, 256 * (u % 2)
                            pe.wait_ge(s_gqs, p.count(1, 1))
                            wait(pe, s_gp, p.count(4, u))
                            for n in range(2):
                                last = pe.matmul(ps_g[:, 256 * n:256 * (n + 1)], g_qt[:, b * P:(b + 1) * P],
                                                 wf_q[:, n, c0:c0 + 256], start=True, stop=True)
                            last.then_inc(s_gu, 1)
                    for b in range(2):
                        if p := due(t, j, "pe.g_pt", b):
                            pe.wait_ge(s_gpq, p.count(2, b + 1))
                            pe.wait_ge(s_gp, p.count(4, 4))
                            wait(pe, s_o, p.count(2, b))
                            for k in range(NI):
                                last = pe.transpose(ps_g[:, k * HALF:(k + 1) * HALF].bitcast(BF16),
                                                    g_pq[:, b, k * P:(k + 1) * P], ident_bf[:])
                            last.then_inc(s_gpt, 1)
                        if p := due(t, j, "pe.g_down", b):
                            pe.wait_ge(s_gpts, p.count(2, b + 1))
                            for k in range(NI):
                                last = pe.matmul(ps_g[:, 0:P], g_pt[:, b, k * P:(k + 1) * P],
                                                 wf_q[:, 2, k * P:(k + 1) * P], start=(k == 0), stop=(k == NI - 1))
                            last.then_inc(s_gd, 1)
                    for b in range(2):
                        if p := due(t, j, "pe.weighted_v", 2 * b):
                            pe.wait_ge(s_attn, p.count(4, 2 * b + 2))
                            if b == 0:
                                pe.wait_ge(s_vd, p.count(2, 2))
                                if n := p.after():
                                    pe.wait_ge(s_rest[1], n.count(1, 1))
                            else:
                                pe.wait_ge(s_x1, p.count(2, 1))
                            for m in range(HEADS // 2):
                                pe.matmul(ps_a[:, 0:P], v_diag[:, b, m * P:(m + 1) * P], attn[:, b, m],
                                          start=(m == 0), stop=False)
                        if p := due(t, j, "pe.weighted_v", 2 * b + 1):
                            for m in range(HEADS // 2, HEADS):
                                last = pe.matmul(ps_a[:, 0:P], v_diag[:, b, m * P:(m + 1) * P], attn[:, b, m],
                                                 start=False, stop=(m == HEADS - 1))
                            last.then_inc(s_pv, 1)
                        if p := due(t, j, "pe.out", b):
                            pe.wait_ge(s_ot, p.count(2, b + 1))
                            pe.matmul(ps_a[:, 0:P], o_t[:, b], wo_t[:], start=True, stop=True).then_inc(s_res, 1)
                    for n in range(EXPERTS):
                        if p := due(t, j, "pe.down", n):
                            for k in range(TPE * n, TPE * (n + 1)):
                                wait_product(pe, p, k)
                            if n == 0:
                                pe.wait_ge(s_log, p.count(1, 1))
                            wait(pe, s_y, p.count(2 * EXPERTS, 2 * n))
                            for b in range(2):
                                for k in range(TPE):
                                    m = TPE * n + k
                                    last = pe.matmul(ps_d[:, b * P:(b + 1) * P], m_h[:, m % 4, b * P:(b + 1) * P],
                                                     wdn[:, m], start=(k == 0), stop=(k == TPE - 1))
                            last.then_inc(s_dn, 1)
                    for k in range(TILES):
                        if p := due(t, j, "pe.up", k):
                            if k == 0:
                                pe.wait_ge(s_mxlo, p.count(1, 1))
                            wait(pe, s_mu, p.count(TILES, k - 1))
                            r = (k - 2) % TILES
                            q = p.before() if k < 2 else p
                            if r in POOL_TILES:
                                wait(pe, s_z1, q.count(len(POOL_TILES), POOL_TILES.index(r) + 1))
                            else:
                                wait(pe, s_mh, q.count(len(DVE_TILES), DVE_TILES.index(r) + 1))
                            for n in range(2):
                                w = slice(k * P, (k + 1) * P)
                                last = split_product(ps_z[k % 2][:, n * TOK:(n + 1) * TOK], w01_hi[:, n, w],
                                                     w01_lo[:, n, w], m_xhi[:], m_xlo[:])
                            last.then_inc(s_z, 1)

            turns(pe, body)

        @block.vector
        def _(dve):
            inv = float(DH) ** -0.5
            dve.wait_ge(w_attn, 80)
            dve.tensor_scalar(wqkv_raw[:, 0], wqkv_raw[:, 0], inv, None, ALU.mult).then_inc(c_wq, 1)
            dve.tensor_scalar(bqk[:, 0:1], bqk[:, 0:1], inv, None, ALU.mult).then_inc(c_wq, 1)
            dve.wait_ge(c_hi, 1)
            dve.tensor_tensor(wqkv_lo[:], wqkv_raw[:], wqkv_hi[:].bitcast(F32), ALU.subtract).then_inc(c_lo, 1)

            def first_weights():
                dve.wait_ge(c_mhi, 2)
                dve.tensor_tensor(w01_lo[:], w01_raw[:], w01_hi[:].bitcast(F32), ALU.subtract).then_inc(c_mlo, 1)
                dve.tensor_tensor(gate_lo[:], gate_raw[:], gate_hi[:].bitcast(F32), ALU.subtract).then_inc(c_mlo, 1)
                dve.wait_ge(c_th, 1)
                dve.tensor_scalar(bo_all[:], bo_all[:], th[:, 0:1], None, ALU.mult).then_inc(c_thbo, 1)
                dve.tensor_scalar(th_half[:], th[:, 2:3], 0.5, None, ALU.mult).then_inc(c_thh, 1)
                dve.wait_ge(w_fin, 128)
                dve.tensor_scalar(bl_all[:], bl_all[:], th[:, 1:2], None, ALU.mult).then_inc(c_thbo, 1)
                dve.tensor_reduce(bsum[:], bsum3[:], AX.X, ALU.add).then_inc(c_bs, 1)
                dve.wait_ge(w_ffn, 48)
                dve.tensor_reduce(wabs[:], wf_raw[:], AX.X, ALU.add, apply_absolute_value=True).then_inc(c_abs, 1)
                dve.wait_ge(c_tot, 1)
                dve.tensor_scalar(wmean[:], ps_g[:, 0:3], 1.0 / (P * INNER), 1e-5, ALU.mult,
                                  ALU.max).then_inc(c_wm, 1)
                dve.wait_ge(c_wm, 1)
                dve.reciprocal(wscale[:], wmean[:]).then_inc(c_wm, 1)
                dve.tensor_scalar(cg[:, 0:1], wmean[:, 0:1], 0.5 / 127.0, None, ALU.mult).then_inc(c_wm, 1)
                dve.tensor_scalar(cg[:, 2:3], wmean[:, 2:3], th[:, 3:4], 1.0 / 127.0, ALU.mult,
                                  ALU.mult).then_inc(c_wm, 1)
                dve.wait_ge(c_wm, 3)
                dve.tensor_scalar(cg[:, 1:2], wmean[:, 1:2], cg[:, 0:1], 1.0 / 127.0, ALU.mult,
                                  ALU.mult).then_inc(c_wm, 1)
                for n in range(3):
                    dve.tensor_scalar(wf_r[:, n], wf_raw[:, n], wscale[:, n:n + 1], ROUND, ALU.mult,
                                      ALU.add).then_inc(c_wr, 1)
                dve.wait_ge(c_wr, 3)
                dve.tensor_scalar(wf_t[:], wf_r[:], ROUND, 1.0, ALU.subtract, ALU.min).then_inc(c_wr, 1)
                dve.wait_ge(c_wr, 4)
                dve.tensor_scalar(wf_q[:], wf_t[:], -1.0, None, ALU.max).then_inc(c_wr, 1)

            def stats(p, src, st, mv, s_st, s_mv, reader):
                wait(dve, s_mv, p.before().count(2, 2))
                for b in range(2):
                    dve.bn_stats(st[:, b], src[:, b]).then_inc(s_st, 1)
                wait(dve, reader, p.before().count(2, 2))
                for b in range(2):
                    dve.wait_ge(s_st, p.count(2, b + 1))
                    dve.sem_inc(s_passed, 1)
                    dve.bn_aggr(mv[:, b], st[:, b]).then_inc(s_mv, 1)

            def normalise(p, dst, src, mv, rs, s_rs, s_done):
                dve.wait_ge(s_rs, p.count(2, 2))
                for b in range(2):
                    dve.tensor_scalar(dst[:, b], src[:, b], mv[:, b, 0:1], rs[:, 1, b:b + 1], ALU.subtract,
                                      ALU.mult).then_inc(s_done, 1)

            def body(t):
                for j in range(SLOTS):
                    for u in range(4):
                        if p := due(t, j, "dve.head_max", u):
                            dve.wait_ge(s_score, p.count(4, u + 1))
                            wait(dve, s_shift, p.count(4, u - 1))
                            sc = ps_sc[:].rearrange("p a (h k) -> p (a h) k", k=HALF)
                            dve.tensor_reduce(head_max[:, u % 2], sc.rearrange("p h k -> p k h"), AX.X,
                                              ALU.max).then_inc(s_hmax, 1)
                        if p := due(t, j, "dve.head_shift", u):
                            sc = ps_sc[:].rearrange("p a (h k) -> p (a h) k", k=HALF)
                            dve.wait_ge(s_hmax, p.count(4, u + 1))
                            wait(dve, s_exp, p.count(4, u - 1))
                            dve.tensor_tensor(shifted[:, u % 2], sc,
                                              head_max[:, u % 2].unsqueeze(1).to_broadcast([P, HEADS, HALF]),
                                              ALU.subtract).then_inc(s_shift, 1)
                        if p := due(t, j, "dve.head_inv", u):
                            dve.wait_ge(s_tree, p.count(16, 4 * u + 4))
                            wait(dve, s_attn, p.count(4, u - 1))
                            dve.reciprocal(head_inv[:, u % 2], tree[:, u % 2, 14]).then_inc(s_hinv, 1)
                    if p := due(t, j, "dve.f_stats"):
                        dve.wait_ge(s_y, p.count(2 * EXPERTS, 2 * EXPERTS))
                        stats(p, y, f_st, f_mv, s_fst, s_fmv, s_fc)
                    if p := due(t, j, "dve.f_norm"):
                        wait(dve, s_fq, p.before().count(1, 1))
                        normalise(p, f_c, y, f_mv, f_rs, s_frs, s_fc)
                    if p := due(t, j, "dve.m_xlo"):
                        dve.wait_ge(s_mxhi, p.count(1, 1))
                        dve.tensor_tensor(m_xlo[:], ps_d[:, 0:TOK], m_xhi[:].bitcast(F32),
                                          ALU.subtract).then_inc(s_mxlo, 1)
                    if p := due(t, j, "dve.logits"):
                        dve.wait_ge(s_gate, p.count(1, 1))
                        wait(dve, s_topi, p.before().count(2, 2))
                        dve.tensor_copy(logits[:], ps_d[:, 0:2 * EXPERTS].rearrange("p (b n) -> p b n", b=2)
                                        ).then_inc(s_log, 1)
                    for k in range(TILES):
                        if p := due(t, j, "dve.m_u", k):
                            dve.wait_ge(s_mt, p.count(TILES, k + 1))
                            wait_product(dve, p, k - 2)
                            z = ps_z[k % 2]
                            dve.scalar_tensor_tensor(m_u[:, k % 2], m_tanh[:, k % 2], 1.0, z[:, 0:TOK], ALU.add,
                                                     ALU.mult).then_inc(s_mu, 1)
                        if k in POOL_TILES:
                            continue
                        if p := due(t, j, "dve.m_h", DVE_TILES.index(k)):
                            z = ps_z[k % 2]
                            dve.wait_ge(s_mu, p.count(TILES, k + 1))
                            wait(dve, s_dn, p.count(EXPERTS, k // TPE - 1))
                            dve.tensor_tensor(m_h[:, k % 4], m_u[:, k % 2], z[:, TOK:2 * TOK],
                                              ALU.mult).then_inc(s_mh, 1)
                    if p := due(t, j, "dve.top2"):
                        dve.wait_ge(s_log, p.count(1, 1))
                        for b in range(2):
                            dve.sem_inc(s_passed, 1)
                            dve.max(top[:, b], logits[:, b]).then_inc(s_top, 1)
                        for b in range(2):
                            dve.wait_ge(s_top, p.count(2, b + 1))
                            dve.sem_inc(s_passed, 1)
                            dve.max_index(top_no[:, b], top[:, b], logits[:, b]).then_inc(s_topi, 1)
                        wait(dve, s_texp, p.before().count(1, 1))
                        dve.tensor_tensor(tdiff[:], top[:, :, 1:2], top[:, :, 0:1], ALU.subtract).then_inc(s_tdf, 1)
                        dve.wait_ge(s_topi, p.count(2, 2))
                        wait(dve, s_w12, p.before().count(4, 4))
                        dve.tensor_copy(top_nof[:], top_no[:]).then_inc(s_tnof, 1)
                    for n in range(EXPERTS):
                        if p := due(t, j, "dve.y", n):
                            dve.wait_ge(s_dn, p.count(EXPERTS, n + 1))
                            if n == 0:
                                dve.wait_ge(s_w, p.count(1, 1))
                                wait(dve, s_fyb, p.before().count(1, 1))
                                wait(dve, s_fc, p.before().count(2, 2))
                            for b in range(2):
                                if n:
                                    dve.wait_ge(s_y, p.count(2 * EXPERTS, 2 * n - 1 + b))
                                dve.scalar_tensor_tensor(y[:, b], ps_d[:, b * P:(b + 1) * P],
                                                         weights[:, b, n:n + 1], (y if n else x1)[:, b],
                                                         ALU.mult, ALU.add).then_inc(s_y, 1)
                    if p := due(t, j, "dve.weights"):
                        dve.wait_ge(s_tp, p.count(5, 5))
                        dve.wait_ge(s_tnof, p.count(1, 1))
                        wait(dve, s_w, p.before().count(1, 1))
                        for b in range(2):
                            for k, dst in enumerate((w_first, w_second)):
                                dve.tensor_scalar(dst[:, b], expert_no[:], top_nof[:, b, k:k + 1],
                                                  tprob[:, b, k:k + 1], ALU.is_equal, ALU.mult).then_inc(s_w12, 1)
                        dve.wait_ge(s_w12, p.count(4, 4))
                        wait(dve, s_y, p.before().count(2 * EXPERTS, 2 * EXPERTS))
                        dve.tensor_tensor(weights[:], w_first[:], w_second[:], ALU.add).then_inc(s_w, 1)
                    for b in range(2):
                        if p := due(t, j, "dve.x1", b):
                            dve.wait_ge(s_res, p.count(2, b + 1))
                            dve.wait_ge(s_xb, p.count(1, 1))
                            wait(dve, s_y, p.before().count(2 * EXPERTS, 2))
                            dve.scalar_tensor_tensor(x1[:, b], ps_a[:, 0:P], th[:, 0:1], x_res[:, b], ALU.mult,
                                                     ALU.add).then_inc(s_x1, 1)
                    if p := due(t, j, "dve.m_stats"):
                        dve.wait_ge(s_x1, p.count(2, 2))
                        stats(p, x1, m_st, m_mv, s_mst, s_mmv, s_mxn)
                    if p := due(t, j, "dve.m_norm"):
                        wait(dve, s_mxt, p.before().count(1, 1))
                        normalise(p, m_xn, x1, m_mv, m_rs, s_mrs, s_mxn)
                    if p := due(t, j, "dve.a_stats"):
                        dve.wait_ge(ld_a, p.count(32, 32))
                        stats(p, x_in, a_st, a_mv, s_ast, s_amv, s_axn)
                    if p := due(t, j, "dve.a_norm"):
                        if t.first:
                            dve.wait_ge(c_misc, 7)
                        wait(dve, s_axt, p.before().count(1, 1))
                        normalise(p, a_xn, x_in, a_mv, a_rs, s_ars, s_axn)
                    if p := due(t, j, "dve.a_xlo"):
                        dve.wait_ge(s_axhi, p.count(1, 1))
                        dve.tensor_tensor(a_xlo[:], ps_a[:, 0:TOK], a_xhi[:].bitcast(F32),
                                          ALU.subtract).then_inc(s_axlo, 1)
                    for n in range(2):
                        if p := due(t, j, "dve.part_rest", n):
                            dve.wait_ge(s_p1[n], p.count(1, 1))
                            wait(dve, s_p3[n], p.before().count(1, 1))
                            dve.scalar_tensor_tensor(qk_rest[:, n], ps_a[:, 0:TOK], bqk[:, 1 - n:2 - n],
                                                     qk_parts[:, n, 0], ALU.add, ALU.subtract).then_inc(s_rest[n], 1)
                            if p.first and n == 1:
                                first_weights()
                    if p := due(t, j, "dve.v_diag"):
                        if p.first:
                            dve.wait_ge(w_out, 80)
                        if t.first:
                            dve.wait_ge(c_zero, 1)
                        dve.wait_ge(s_v, p.count(1, 1))
                        wait(dve, s_pv, p.before().count(2, 2))
                        for b in range(2):
                            dst = v_diag[:, b].rearrange("p (m s) -> p m s", s=VSTEP)[:, :, 0:DH]
                            dve.tensor_tensor(dst, ps_a[:, b * P:(b + 1) * P].rearrange("p (m d) -> p m d", d=DH),
                                              bv_all[:].rearrange("p (m d) -> p m d", d=DH), ALU.add).then_inc(s_vd, 1)
                    if p := due(t, j, "dve.f_max"):
                        dve.wait_ge(s_fs, p.count(1, 1))
                        wait(dve, s_fa, p.before().count(2, 2))
                        dve.tensor_reduce(f_nmax[:], ps_f[:, 0:TOK].rearrange("p (b q) -> p b q", b=2), AX.X, ALU.max,
                                          negate=True).then_inc(s_fnm, 1)
                        dve.wait_ge(s_fnm, p.count(1, 1))
                        wait(dve, s_fe, p.before().count(4, 4))
                        dve.scalar_tensor_tensor(f_m[:], ps_f[:, TOK:TOK + 2], bsum[:, 0:1], f_nmax[:], ALU.add,
                                                 ALU.subtract).then_inc(s_fm, 1)
                    if p := due(t, j, "dve.f_ainv"):
                        dve.wait_ge(s_fa, p.count(2, 2))
                        wait(dve, s_fan, p.before().count(2, 2))
                        dve.reciprocal(f_ainv[:], f_asum[:]).then_inc(s_fai, 1)
                    if p := due(t, j, "dve.f_max_max"):
                        dve.wait_ge(s_fats, p.count(1, 1))
                        dve.tensor_reduce(f_nmm[:], ps_f[:, TOK:2 * TOK].rearrange("p (b q) -> p b q", b=2), AX.X,
                                          ALU.max, negate=True).then_inc(s_fnmm, 1)
                    if p := due(t, j, "dve.f_w14"):
                        dve.wait_ge(s_fe, p.count(4, 2))
                        dve.reciprocal(f_einv[:], f_esum[:]).then_inc(s_fei, 1)
                        dve.wait_ge(s_fei, p.count(1, 1))
                        dve.wait_ge(s_fc2, p.count(1, 1))
                        dve.tensor_tensor(f_q2c[:], ps_f[:, TOK:TOK + 2], f_einv[:], ALU.mult).then_inc(s_fq2, 1)
                        dve.wait_ge(s_fq2, p.count(1, 1))
                        wait(dve, s_fz, p.before().count(1, 1))
                        for b in range(2):
                            dve.scalar_tensor_tensor(f_w14[:, b], wl[:, 3], f_q2c[:, b:b + 1], wl[:, 0], ALU.mult,
                                                     ALU.add).then_inc(s_fw, 1)
                    for b in range(2):
                        if p := due(t, j, "dve.out", b):
                            dve.wait_ge(s_gd, p.count(2, b + 1))
                            wait(dve, stored, p.before().count(16, 16))
                            dve.scalar_tensor_tensor(o_sb[:, b], ps_g[:, 0:P], g_ps[:, b, 1:2], x3[:, b], ALU.mult,
                                                     ALU.add).then_inc(s_o, 1)
                    if p := due(t, j, "dve.x3"):
                        dve.wait_ge(s_fz, p.count(1, 1))
                        dve.wait_ge(s_fyb, p.count(1, 1))
                        wait(dve, s_o, p.before().count(2, 2))
                        dve.scalar_tensor_tensor(x3[:], ps_f[:, 0:TOK].rearrange("p (b d) -> p b d", b=2), th[:, 1:2],
                                                 y_res[:], ALU.mult, ALU.add).then_inc(s_x3, 1)
                        dve.wait_ge(s_x3, p.count(1, 1))
                        stats(p, x3, g_st, g_mv, s_gst, s_gmv, s_gh)
                    if p := due(t, j, "dve.g_norm"):
                        wait(dve, s_gr, p.before().count(2, 2))
                        normalise(p, g_h, x3, g_mv, g_rs, s_grs, s_gh)
                    if p := due(t, j, "dve.g_amax"):
                        dve.wait_ge(s_gh, p.count(2, 2))
                        dve.tensor_reduce(g_amax[:], g_h[:], AX.X, ALU.max,
                                          apply_absolute_value=True).then_inc(s_gam, 1)
                        dve.wait_ge(s_gam, p.count(1, 1))
                        wait(dve, s_gt, p.before().count(4, 4))
                        dve.tensor_scalar(g_amc[:], g_amax[:], 1e-5, None, ALU.max).then_inc(s_gsc, 1)
                        dve.wait_ge(s_gsc, p.count(5, 1))
                        dve.reciprocal(g_ainv[:], g_amc[:]).then_inc(s_gsc, 1)
                        dve.wait_ge(s_gsc, p.count(5, 2))
                        dve.tensor_scalar(g_sc[:, :, 0], g_ainv[:], 127.0, None, ALU.mult).then_inc(s_gsc, 1)
                        dve.tensor_scalar(g_sc[:, :, 1], g_amc[:], cg[:, 0:1], None, ALU.mult).then_inc(s_gsc, 1)
                        dve.scalar_tensor_tensor(g_sc[:, :, 2], g_amc[:], cg[:, 1:2], g_amc[:], ALU.mult,
                                                 ALU.mult).then_inc(s_gsc, 1)
                        dve.wait_ge(s_gsc, p.count(5, 5))
                        wait(dve, s_gq, p.before().count(1, 1))
                        for b in range(2):
                            dve.tensor_scalar(g_r[:, b], g_h[:, b], g_sc[:, b, 0:1], ROUND, ALU.mult,
                                              ALU.add).then_inc(s_gr, 1)
                    if p := due(t, j, "dve.g_q"):
                        dve.wait_ge(s_gr, p.count(2, 2))
                        wait(dve, s_gqt, p.before().count(1, 1))
                        dve.tensor_scalar(g_q[:], g_r[:], ROUND, 127.0, ALU.subtract, ALU.min).then_inc(s_gq, 1)
                    for u in range(4):
                        if p := due(t, j, "dve.g_u", u):
                            b, c0 = u // 2, 256 * (u % 2)
                            dve.wait_ge(s_gt, p.count(4, u + 1))
                            wait(dve, s_gp, p.count(4, u))
                            dve.scalar_tensor_tensor(g_u[:], g_tanh[:], 1.0, ps_g[:, 0:256], ALU.add,
                                                     ALU.mult).then_inc(s_guu, 1)
                        if p := due(t, j, "dve.g_p", u):
                            b, c0 = u // 2, 256 * (u % 2)
                            dve.wait_ge(s_guu, p.count(4, u + 1))
                            wait(dve, s_gpr, p.before().count(2, 2))
                            dve.scalar_tensor_tensor(g_p[:, b, c0:c0 + 256], g_u[:], g_sc[:, b, 2:3], ps_g[:, 256:512],
                                                     ALU.mult, ALU.mult).then_inc(s_gp, 1)
                    for b in range(2):
                        if p := due(t, j, "dve.g_pquant", b):
                            dve.wait_ge(s_gp, p.count(4, 2 * b + 2))
                            dve.tensor_reduce(g_pmax[:, b:b + 1], g_p[:, b], AX.X, ALU.max,
                                              apply_absolute_value=True).then_inc(s_gpm, 1)
                            dve.wait_ge(s_gpm, p.count(2, b + 1))
                            wait(dve, s_o, p.before().count(2, 2))
                            dve.tensor_scalar(g_pmc[:, b:b + 1], g_pmax[:, b:b + 1], 1e-5, None,
                                              ALU.max).then_inc(s_gps, 1)
                            dve.wait_ge(s_gps, p.count(8, 4 * b + 1))
                            dve.reciprocal(g_pinv[:, b:b + 1], g_pmc[:, b:b + 1]).then_inc(s_gps, 1)
                            dve.wait_ge(s_gps, p.count(8, 4 * b + 2))
                            dve.tensor_scalar(g_ps[:, b, 0:1], g_pinv[:, b:b + 1], 127.0, None,
                                              ALU.mult).then_inc(s_gps, 1)
                            dve.tensor_scalar(g_ps[:, b, 1:2], g_pmc[:, b:b + 1], cg[:, 2:3], None,
                                              ALU.mult).then_inc(s_gps, 1)

            turns(dve, body)


def kernel(**inputs):
    import numpy as np
    import concourse.bacc as bacc
    from concourse.bass_utils import run_bass_kernel_spmd

    f = {k: np.asarray(v) for k, v in inputs.items()}
    half = HEADS // 2
    rows_qk = lambda w: w.reshape(DH, half, 2, -1).transpose(3, 2, 0, 1).reshape(-1, P)
    rows_v = lambda w: w.reshape(DH, half, 2, -1).transpose(3, 2, 1, 0).reshape(-1, P)
    arrays = {
        "x": f["x"], "ctx": f["ctx_1024"], "ctx_t": f["ctx_1024"].transpose(0, 2, 1),
        "wq": rows_qk(f["L0_xattn_Wq_w"]), "wk": rows_qk(f["L0_xattn_Wk_w"]), "wv": rows_v(f["L0_xattn_Wv_w"]),
        "bq": rows_qk(f["L0_xattn_Wq_b"]).T, "bk": rows_qk(f["L0_xattn_Wk_b"]).T,
        "bv": rows_v(f["L0_xattn_Wv_b"]).reshape(P),
        "wo": rows_v(f["L0_xattn_Wo_w"].T).T, "bo": f["L0_xattn_Wo_b"],
        "g_xattn": f["g_xattn"], "g_ffn": f["g_ffn"],
        "w0": f["L0_ffn_w0_kernel"], "w1": f["L0_ffn_w1_kernel"], "gate": f["L0_ffn_gate_kernel"],
        "wdn": f["L0_ffn_wo_kernel"],
        "w_cq": f["L1_xattn_w_cq"].reshape(P, 1), "w_q": f["L1_xattn_w_q"].reshape(P, 1),
        "w_c": f["L1_xattn_w_c"].reshape(P, 1),
        "b_cq": f["L1_xattn_b_cq"].reshape(1), "b_q": f["L1_xattn_b_q"].reshape(1), "b_c": f["L1_xattn_b_c"].reshape(1),
        "wl": f["L1_xattn_W_l"].T, "bl": f["L1_xattn_b_l"],
        "wg": f["L1_ffn_w_gate"].T, "wu": f["L1_ffn_w_up"].T, "wd": f["L1_ffn_w_down"].T,
    }
    arrays = {k: np.ascontiguousarray(a) for k, a in arrays.items()}
    nc = bacc.Bacc("TRN2", target_bir_lowering=False, num_devices=1)
    aps = {k: nc.dram_tensor(f"in_{k}", a.shape, mybir.dt.from_np(a.dtype), kind="ExternalInput").ap()
           for k, a in arrays.items()}
    out = nc.dram_tensor("out", (BATCH, P, P), F32, kind="ExternalOutput").ap()
    build(nc, aps, out)
    r = run_bass_kernel_spmd(nc, [{f"in_{k}": a for k, a in arrays.items()}], core_ids=[0])
    return r.results[0]["out"]
```

```python
from contextlib import ExitStack

import concourse.bass as bass
from concourse import mybir

ALU = mybir.AluOpType
ACT = mybir.ActivationFunctionType
AX = mybir.AxisListType
F32 = mybir.dt.float32
F32R = mybir.dt.float32r
BF16 = mybir.dt.bfloat16
U32 = mybir.dt.uint32

P = 128
BATCH = 16
PAIRS = BATCH // 2
TOK = 2 * P
HEADS = 16
DH = P // HEADS
HALF = P // 2
EXPERTS = 8
HID = 256
TILES = EXPERTS * HID // P
TPE = HID // P

POOL_TILES = (1, 3, 5, 7, 9, 11, 13)
DVE_TILES = tuple(k for k in range(TILES) if k not in POOL_TILES)
INNER = 512
NI = INNER // P
EPS = 1e-5
ROUND = 1.5 * 2.0 ** 23
VSTEP = P + DH

SLOTS = 112
AT = {
    "sp.load_a": 0, "sp.store_parts": (27, 31), "sp.fetch_rows": (45, 106), "sp.load_res": 124,
    "sp.load_f": 355, "sp.store": 553,
    "pool.a_mean": 10, "pool.a_rstd": 30, "pool.ct_lo": 45, "pool.part3": (65, 68),
    "pool.head_sum": (124, 168, 195, 208), "pool.head_norm": (147, 178, 217, 224), "pool.m_mean": 243,
    "pool.m_rstd": 255, "pool.m_h": (283, 293, 317, 327, 331, 345, 351), "pool.top_probs": 291,
    "pool.f_mean": 373, "pool.y_res": 380, "pool.f_rstd": 391, "pool.f_prod": 434, "pool.g_mean": 444,
    "pool.g_rstd": 453,
    "act.a_sum": 0, "act.a_square": 4, "act.a_norm": 31, "act.ct_hi": 40, "act.a_xhi": 44,
    "act.part1": (47, 69), "act.part2": (53, 71), "act.head_exp": (114, 125, 168, 193), "act.v_diag": 146,
    "act.o_t": (202, 229), "act.m_sum": 239, "act.m_square": 248, "act.m_norm": 259, "act.m_xhi": 262,
    "act.m_tanh": (267, 269, 272, 289, 294, 299, 310, 322, 327, 328, 330, 331, 335, 339, 352, 354),
    "act.top_exp": 292, "act.f_sum": 372, "act.f_square": 378, "act.f_norm": 382, "act.f_ct": 390,
    "act.f_exp": 408, "act.f_an": 410, "act.f_at": 415, "act.f_exp_max": 424, "act.f_c2q": 429, "act.f_w4": 437,
    "act.g_sum": 441, "act.g_square": 444, "act.g_norm": 449, "act.g_r": 458, "act.g_qt": 467,
    "act.g_tanh": (473, 487, 497, 521), "act.g_pr": (524, 540), "act.g_pq": (528, 544), "act.g_pt": (539, 547),
    "pe.a_xt": 14, "pe.kq": (25, 37), "pe.scores": (90, 105, 124, 150), "pe.v": 121,
    "pe.weighted_v": (159, 167, 212, 218), "pe.out": (177, 221), "pe.m_xt": 237,
    "pe.up": (241, 242, 250, 260, 264, 269, 273, 280, 301, 306, 309, 312, 317, 322, 334, 335), "pe.gate": 243,
    "pe.down": (265, 283, 303, 308, 313, 332, 340, 346), "pe.f_ct": 365, "pe.f_scores": 375, "pe.f_at": 390,
    "pe.f_c2q": 396, "pe.f_z": 419, "pe.g_qt": 448, "pe.g_up": (456, 463, 475, 490), "pe.g_pt": (505, 526),
    "pe.g_down": (509, 529),
    "dve.a_xlo": 0, "dve.part_rest": (9, 20), "dve.head_max": (76, 85, 104, 133),
    "dve.head_shift": (78, 87, 107, 139), "dve.head_inv": (95, 127, 169, 177), "dve.x1": (174, 204),
    "dve.m_xlo": 218,
    "dve.m_u": (223, 230, 234, 243, 246, 254, 272, 277, 282, 287, 292, 296, 301, 312, 320, 321),
    "dve.m_h": (225, 236, 249, 273, 285, 295, 305, 322, 323), "dve.logits": 232, "dve.top2": 240,
    "dve.weights": 252, "dve.weights_sum": 255, "dve.y": (259, 274, 283, 290, 299, 317, 324, 327),
    "dve.f_max": 353, "dve.f_ainv": 360, "dve.f_max_max": 369, "dve.f_q2c": 388, "dve.x3": 400,
    "dve.g_amax": 415, "dve.g_clamp": 419, "dve.g_scales": 422, "dve.g_q": 430, "dve.g_u": (437, 444, 459, 477),
    "dve.g_p": (438, 453, 461, 480), "dve.g_pmax": (455, 487), "dve.g_pclamp": (466, 488),
    "dve.g_pscales": (471, 493), "dve.out": (499, 502),
}
LAST = max(max(v) if isinstance(v, tuple) else v for v in AT.values())

TURNS = PAIRS + LAST // SLOTS
LOOP_FROM, LOOP_TO = LAST // SLOTS + 1, PAIRS


class Pair:

    def __init__(self, i, c):
        self.i, self.c = i, c
        self.first = isinstance(i, int) and c == 0

    def count(self, per_pair, k):
        return self.i * per_pair + (self.c * per_pair + k)

    def before(self, n=1):
        return Pair(self.i, self.c - n)

    def rows(self):
        return slice(self.c, self.c + 1) if isinstance(self.i, int) else bass.ds(self.i + self.c, 1)

    def after(self):
        return Pair(self.i, self.c + 1) if not isinstance(self.i, int) or self.c + 1 < PAIRS else None


def due(turn, j, step, n=None):
    offset = AT[step] if n is None else AT[step][n]
    if (j - offset) % SLOTS:
        return None
    p = Pair(turn.i, turn.c - (offset - j) // SLOTS)
    return p if not isinstance(turn.i, int) or 0 <= p.c < PAIRS else None


def wait(eng, sem, value):
    if not isinstance(value, int) or value > 0:
        eng.wait_ge(sem, value)


def turns(eng, body):
    for t in range(LOOP_FROM):
        body(Pair(0, t))
    with eng.Fori(0, LOOP_TO - LOOP_FROM) as i:
        body(Pair(i, LOOP_FROM))
    for t in range(LOOP_TO, TURNS):
        body(Pair(0, t))


def build(nc, A, out):
    ctx = ExitStack()
    with ctx:
        def sb(name, shape, dt=F32):
            return ctx.enter_context(nc.sbuf_tensor(name, shape, dt))

        def bank(name, shape=(P, 512)):
            return ctx.enter_context(nc.psum_tensor(name, list(shape), F32))

        def sem(name):
            return ctx.enter_context(nc.semaphore(name))

        wqkv_raw = sb("wqkv_raw", [P, 3, P])
        wqkv_hi = sb("wqkv_hi", [P, 3, P], F32R)
        wqkv_lo = sb("wqkv_lo", [P, 3, P], F32R)
        bqk = sb("bqk", [P, 2])
        bv_row = sb("bv_row", [1, P])
        wo_t = sb("wo_t", [P, P])
        bo_row = sb("bo_row", [1, P])
        gains = sb("gains", [P, 4])
        th = sb("th", [P, 4])
        th_half = sb("th_half", [P, 1])
        w01_raw = sb("w01_raw", [P, 2, TILES * P])
        w01_hi = sb("w01_hi", [P, 2, TILES * P], F32R)
        w01_lo = sb("w01_lo", [P, 2, TILES * P], F32R)
        wdn = sb("wdn", [P, TILES, P])
        gate_raw = sb("gate_raw", [P, EXPERTS])
        gate_hi = sb("gate_hi", [P, EXPERTS], F32R)
        gate_lo = sb("gate_lo", [P, EXPERTS], F32R)
        wcq = sb("wcq", [P, 3])
        bsum3 = sb("bsum3", [P, 3])
        bsum = sb("bsum", [P, 1])
        wl = sb("wl", [P, 4, P])
        bl_all = sb("bl_all", [P, P])
        wf_raw = sb("wf_raw", [P, 3, INNER])
        wf_r = sb("wf_r", [P, 3, INNER])
        wf_t = sb("wf_t", [P, 3, INNER])
        wf_q = sb("wf_q", [P, 3, INNER], BF16)
        wabs = sb("wabs", [P, 3])
        wmean = sb("wmean", [P, 3])
        wscale = sb("wscale", [P, 3])
        cg = sb("cg", [P, 3])
        ident = sb("ident", [P, P])
        ident_bf = sb("ident_bf", [P, P], BF16)
        ones = sb("ones", [P, P])
        minus_half = sb("minus_half", [P, 2])
        eps_col = sb("eps_col", [P, 2])
        inv_width = sb("inv_width", [P, 2])
        minus_inv = sb("minus_inv", [P, 2])
        round_col = sb("round_col", [P, 1])
        minus_one = sb("minus_one", [P, 1])
        expert_no = sb("expert_no", [P, EXPERTS])

        x_in = sb("x_in", [P, 2, P])
        x_res = sb("x_res", [P, 2, P])
        ct_in = sb("ct_in", [P, TOK])
        ct_hi = sb("ct_hi", [P, TOK], F32R)
        ct_lo = sb("ct_lo", [P, TOK], F32R)
        a_sum = sb("a_sum", [P, 2])
        a_nmean = sb("a_nmean", [P, 2])
        a_sq = sb("a_sq", [P, 2])
        a_rs = sb("a_rs", [P, 4, 2])
        a_xn = sb("a_xn", [P, 2, P])
        a_xhi = sb("a_xhi", [P, TOK], F32R)
        a_xlo = sb("a_xlo", [P, TOK], F32R)
        qk_parts = sb("qk_parts", [P, 2, 3, TOK], BF16)
        qk_rest = sb("qk_rest", [P, 2, TOK])
        k_rows = sb("k_rows", [P, HEADS // 2, TOK], BF16)
        q_rows = sb("q_rows", [P, HEADS // 2, TOK], BF16)
        v_diag = sb("v_diag", [P, 2, HEADS * VSTEP])
        head_max = sb("head_max", [P, 2, HALF])
        shifted = sb("shifted", [P, 2, HEADS, HALF])
        attn = sb("attn", [P, 2, HEADS, P])
        tree = sb("tree", [P, 2, 15, HALF])
        head_inv = sb("head_inv", [P, 2, HALF])
        o_t = sb("o_t", [P, 2, P])
        x1 = sb("x1", [P, 2, P])

        m_sum = sb("m_sum", [P, 2])
        m_nmean = sb("m_nmean", [P, 2])
        m_sq = sb("m_sq", [P, 2])
        m_rs = sb("m_rs", [P, 4, 2])
        m_xn = sb("m_xn", [P, 2, P])
        m_xhi = sb("m_xhi", [P, TOK], F32R)
        m_xlo = sb("m_xlo", [P, TOK], F32R)
        logits = sb("logits", [P, 2, EXPERTS])
        top = sb("top", [P, 2, 8])
        top_no = sb("top_no", [P, 2, 8], U32)
        top_nof = sb("top_nof", [P, 2, 8])
        tdiff = sb("tdiff", [P, 2, 1])
        texp = sb("texp", [P, 2, 1])
        tsum = sb("tsum", [P, 2, 1])
        tprob = sb("tprob", [P, 2, 2])
        w_first = sb("w_first", [P, 2, EXPERTS])
        w_second = sb("w_second", [P, 2, EXPERTS])
        weights = sb("weights", [P, 2, EXPERTS])
        m_tanh = sb("m_tanh", [P, 2, TOK])
        m_u = sb("m_u", [P, 2, TOK])
        m_h = sb("m_h", [P, 4, TOK])
        m_z1 = sb("m_z1", [P, 2, TOK])
        y = sb("y", [P, 2, P])

        ctx_in = sb("ctx_in", [P, 2, P])
        ctf_in = sb("ctf_in", [P, TOK])
        f_sum = sb("f_sum", [P, 2])
        f_nmean = sb("f_nmean", [P, 2])
        f_sq = sb("f_sq", [P, 2])
        f_rs = sb("f_rs", [P, 4, 2])
        f_c = sb("f_c", [P, 2, P])
        f_ct = sb("f_ct", [P, TOK])
        f_ctq = sb("f_ctq", [P, TOK])
        f_nmax = sb("f_nmax", [P, 2])
        f_m = sb("f_m", [P, 2])
        f_a = sb("f_a", [P, 2, P])
        f_asum = sb("f_asum", [P, 2])
        f_ainv = sb("f_ainv", [P, 2])
        f_an = sb("f_an", [P, 2, P])
        f_at = sb("f_at", [P, TOK])
        f_nmm = sb("f_nmm", [P, 2])
        f_erow = sb("f_erow", [P, 2, P])
        f_esum = sb("f_esum", [P, 2])
        f_einv = sb("f_einv", [P, 2])
        f_e = sb("f_e", [P, 2])
        f_c2q = sb("f_c2q", [P, TOK])
        f_prod = sb("f_prod", [P, TOK])
        f_q2c = sb("f_q2c", [P, 2])
        f_w4 = sb("f_w4", [P, 2, P])
        y_res = sb("y_res", [P, 2, P])
        x3 = sb("x3", [P, 2, P])

        g_sum = sb("g_sum", [P, 2])
        g_nmean = sb("g_nmean", [P, 2])
        g_sq = sb("g_sq", [P, 2])
        g_rs = sb("g_rs", [P, 4, 2])
        g_h = sb("g_h", [P, 2, P])
        g_amax = sb("g_amax", [P, 2])
        g_amc = sb("g_amc", [P, 2])
        g_ainv = sb("g_ainv", [P, 2])
        g_sc = sb("g_sc", [P, 2, 3])
        g_r = sb("g_r", [P, 2, P])
        g_q = sb("g_q", [P, 2, P], BF16)
        g_qt = sb("g_qt", [P, TOK], BF16)
        g_tanh = sb("g_tanh", [P, 256])
        g_u = sb("g_u", [P, 256])
        g_p = sb("g_p", [P, 2, INNER])
        g_pmax = sb("g_pmax", [P, 2])
        g_pmc = sb("g_pmc", [P, 2])
        g_pinv = sb("g_pinv", [P, 2])
        g_ps = sb("g_ps", [P, 2, 2])
        g_pr = sb("g_pr", [P, 2, INNER])
        g_pq = sb("g_pq", [P, 2, INNER], BF16)
        g_pt = sb("g_pt", [P, 2, INNER], BF16)
        o_sb = sb("o_sb", [P, 2, P])

        ps_sc = bank("ps_sc", (P, 2, 512))
        ps_z = [bank("ps_z0"), bank("ps_z1")]
        ps_d = bank("ps_d")
        ps_a = bank("ps_a")
        ps_f = bank("ps_f")
        ps_g = bank("ps_g")

        parts_dram = nc.dram_tensor("parts_dram", (2, PAIRS, P, 3, TOK), BF16, kind="Internal").ap()

        w_attn = sem("w_attn"); w_out = sem("w_out"); w_moe = sem("w_moe"); w_late = sem("w_late")
        w_fin = sem("w_fin"); w_ffn = sem("w_ffn")
        ld_a = sem("ld_a"); ld_res = sem("ld_res"); ld_f = sem("ld_f")
        parts_out = [sem("k_parts_out"), sem("q_parts_out")]
        rows_in = [sem("k_rows_in"), sem("q_rows_in")]
        stored = sem("stored")
        c_id = sem("c_id"); c_misc = sem("c_misc"); c_th = sem("c_th"); c_thh = sem("c_thh")
        c_zero = sem("c_zero")
        c_wq = sem("c_wq"); c_hi = sem("c_hi"); c_lo = sem("c_lo"); c_thbo = sem("c_thbo")
        c_mhi = sem("c_mhi"); c_mlo = sem("c_mlo"); c_mlo1 = sem("c_mlo1"); c_bs = sem("c_bs")
        c_abs = sem("c_abs"); c_tot = sem("c_tot"); c_wm = sem("c_wm"); c_wr = sem("c_wr")
        s_passed = sem("s_passed"); s_sp_passed = sem("s_sp_passed")
        s_ast = sem("s_ast"); s_asq = sem("s_asq"); s_amv = sem("s_amv"); s_ars = sem("s_ars"); s_axn = sem("s_axn")
        s_axt = sem("s_axt"); s_axhi = sem("s_axhi"); s_axlo = sem("s_axlo")
        s_cthi = sem("s_cthi"); s_ctlo = sem("s_ctlo")
        s_proj = [sem("s_k"), sem("s_q")]
        s_p1 = [sem("s_k1"), sem("s_q1")]
        s_rest = [sem("s_krest"), sem("s_qrest")]
        s_p2 = [sem("s_k2"), sem("s_q2")]
        s_p3 = [sem("s_k3"), sem("s_q3")]
        s_v = sem("s_v"); s_vd = sem("s_vd")
        s_score = sem("s_score"); s_hmax = sem("s_hmax"); s_shift = sem("s_shift"); s_exp = sem("s_exp")
        s_tree = sem("s_tree"); s_hinv = sem("s_hinv"); s_attn = sem("s_attn")
        s_pv = sem("s_pv"); s_ot = sem("s_ot"); s_res = sem("s_res"); s_x1 = sem("s_x1")
        s_mst = sem("s_mst"); s_msq = sem("s_msq"); s_mmv = sem("s_mmv"); s_mrs = sem("s_mrs"); s_mxn = sem("s_mxn")
        s_mxt = sem("s_mxt"); s_mxhi = sem("s_mxhi"); s_mxlo = sem("s_mxlo")
        s_gate = sem("s_gate"); s_log = sem("s_log"); s_top = sem("s_top"); s_topi = sem("s_topi")
        s_tdf = sem("s_tdf"); s_texp = sem("s_texp"); s_tp = sem("s_tp"); s_tnof = sem("s_tnof")
        s_w12 = sem("s_w12"); s_w = sem("s_w")
        s_z = sem("s_z"); s_mt = sem("s_mt"); s_mu = sem("s_mu"); s_mh = sem("s_mh"); s_mhp = sem("s_mhp")
        s_z1 = sem("s_z1")
        s_dn = sem("s_dn"); s_y = sem("s_y")
        s_fst = sem("s_fst"); s_fsq = sem("s_fsq"); s_fmv = sem("s_fmv"); s_frs = sem("s_frs"); s_fc = sem("s_fc")
        s_fyb = sem("s_fyb"); s_fct = sem("s_fct"); s_fcs = sem("s_fcs"); s_fcq = sem("s_fcq")
        s_fs = sem("s_fs"); s_fnm = sem("s_fnm"); s_fm = sem("s_fm"); s_fa = sem("s_fa"); s_fai = sem("s_fai")
        s_fan = sem("s_fan"); s_fat = sem("s_fat"); s_fats = sem("s_fats"); s_fnmm = sem("s_fnmm")
        s_fe = sem("s_fe"); s_fei = sem("s_fei"); s_fq = sem("s_fq"); s_fc2 = sem("s_fc2"); s_fpr = sem("s_fpr")
        s_fq2 = sem("s_fq2"); s_fw = sem("s_fw"); s_fz = sem("s_fz"); s_x3 = sem("s_x3")
        s_gst = sem("s_gst"); s_gsq = sem("s_gsq"); s_gmv = sem("s_gmv"); s_grs = sem("s_grs"); s_gh = sem("s_gh")
        s_gam = sem("s_gam"); s_gsc = sem("s_gsc"); s_gr = sem("s_gr"); s_gq = sem("s_gq")
        s_gqt = sem("s_gqt"); s_gqs = sem("s_gqs"); s_gu = sem("s_gu"); s_gt = sem("s_gt")
        s_guu = sem("s_guu"); s_gp = sem("s_gp"); s_gpm = sem("s_gpm"); s_gps = sem("s_gps")
        s_gpr = sem("s_gpr"); s_gpq = sem("s_gpq"); s_gpt = sem("s_gpt"); s_gpts = sem("s_gpts")
        s_gd = sem("s_gd"); s_o = sem("s_o")

        x_d = A["x"].rearrange("(p b) s d -> p s b d", b=2)
        c_d = A["ctx"].rearrange("(p b) s d -> p s b d", b=2)
        ct_d = A["ctx_t"].rearrange("(p b) d s -> p d b s", b=2)
        o_d = out.rearrange("(p b) s d -> p s b d", b=2)

        def wait_product(eng, p, k):
            q = p.before() if k < 0 else p
            k %= TILES
            if k in POOL_TILES:
                wait(eng, s_mhp, q.count(len(POOL_TILES), POOL_TILES.index(k) + 1))
            else:
                wait(eng, s_mh, q.count(len(DVE_TILES), DVE_TILES.index(k) + 1))

        block = ctx.enter_context(nc.Block())

        @block.sync
        def _(sp):
            def last_weights():
                sp.dma_start(wdn[:], A["wdn"].rearrange("n (t p) e -> p (n t) e", p=P)).then_inc(w_late, 16)
                sp.dma_start(wl[:], A["wl"].rearrange("(k d) o -> d k o", d=P)).then_inc(w_late, 16)

            def later_weights():
                sp.dma_start(w01_raw[:, 0].rearrange("e (n h) -> e n h", n=EXPERTS),
                             A["w0"].rearrange("n e h -> e n h")).then_inc(w_moe, 16)
                sp.dma_start(w01_raw[:, 1].rearrange("e (n h) -> e n h", n=EXPERTS),
                              A["w1"].rearrange("n e h -> e n h")).then_inc(w_moe, 16)
                sp.dma_start(gate_raw[:], A["gate"]).then_inc(w_moe, 16)
                sp.dma_start(gains[:, 0:2], A["g_xattn"].partition_broadcast(P)).then_inc(w_out, 16)
                sp.dma_start(gains[:, 2:4], A["g_ffn"].partition_broadcast(P)).then_inc(w_out, 16)
                sp.dma_start(bo_row[:], A["bo"].partition_broadcast(1)).then_inc(w_out, 16)
                sp.dma_start(bv_row[:], A["bv"].partition_broadcast(1)).then_inc(w_out, 16)
                sp.dma_start(wo_t[:], A["wo"]).then_inc(w_out, 16)
                for i, src in enumerate(("w_cq", "w_q", "w_c")):
                    sp.dma_start(wcq[:, i:i + 1], A[src]).then_inc(w_fin, 16)
                for i, src in enumerate(("b_cq", "b_q", "b_c")):
                    sp.dma_start(bsum3[:, i:i + 1], A[src].partition_broadcast(P)).then_inc(w_fin, 16)
                sp.dma_start(bl_all[:], A["bl"].partition_broadcast(P)).then_inc(w_fin, 16)
                sp.dma_start(wf_raw[:, 0], A["wg"]).then_inc(w_ffn, 16)
                sp.dma_start(wf_raw[:, 1], A["wu"]).then_inc(w_ffn, 16)
                sp.dma_start(wf_raw[:, 2].rearrange("p (k o) -> p k o", k=NI),
                              A["wd"].rearrange("(k p) o -> p k o", p=P)).then_inc(w_ffn, 16)

            def body(t):
                for j in range(SLOTS):
                    if p := due(t, j, "sp.load_a"):
                        q = p.before()
                        wait(sp, s_axn, q.count(2, 2))
                        sp.sem_inc(s_sp_passed, 1)
                        wait(sp, s_ctlo, q.count(1, 1))
                        sp.sem_inc(s_sp_passed, 1)
                        sp.dma_start(x_in[:], x_d[p.rows()].rearrange("o s b d -> s (o b) d")).then_inc(ld_a, 16)
                        sp.dma_start(ct_in[:].rearrange("d (b s) -> d b s", b=2),
                                     ct_d[p.rows()].rearrange("o d b s -> d (o b) s")).then_inc(ld_a, 16)
                        if p.first:
                            sp.wait_ge(w_attn, 80)
                            later_weights()
                    for n in range(2):
                        if p := due(t, j, "sp.store_parts", n):
                            sp.wait_ge(s_p3[n], p.count(1, 1))
                            sp.sem_inc(s_sp_passed, 1)
                            sp.dma_start(parts_dram[n][p.rows()].rearrange("o c r t -> c (o r) t"),
                                         qk_parts[:, n]).then_inc(parts_out[n], 16)
                    for n, rows in enumerate((k_rows, q_rows)):
                        if p := due(t, j, "sp.fetch_rows", n):
                            sp.wait_ge(parts_out[n], p.count(16, 16))
                            sp.sem_inc(s_sp_passed, 1)
                            wait(sp, s_score, p.before().count(4, 4))
                            sp.sem_inc(s_sp_passed, 1)
                            at = 0
                            for a, reps in enumerate((3, 2, 1)):
                                for hq in range(2):
                                    lo = hq * HALF + at * DH
                                    parts = slice(a, a + 1) if n == 0 else slice(0, reps)
                                    src = parts_dram[n][p.rows(), hq * HALF:(hq + 1) * HALF, parts, :]
                                    src = src.rearrange("o (j h) r t -> (o r) j h t", h=HEADS // 2)
                                    if n == 0 and reps > 1:
                                        src = src.to_broadcast([reps, DH, HEADS // 2, TOK])
                                    sp.dma_start(rows[lo:lo + reps * DH, :, :],
                                                 src).then_inc(rows_in[n], 16)
                                at += reps
                            if p.first and n == 1:
                                last_weights()
                    if p := due(t, j, "sp.load_res"):
                        wait(sp, s_x1, p.before().count(2, 2))
                        sp.sem_inc(s_sp_passed, 1)
                        sp.dma_start(x_res[:], x_d[p.rows()].rearrange("o s b d -> s (o b) d")).then_inc(ld_res, 16)
                    if p := due(t, j, "sp.load_f"):
                        wait(sp, s_fq, p.before().count(1, 1))
                        sp.sem_inc(s_sp_passed, 1)
                        sp.dma_start(ctx_in[:], c_d[p.rows()].rearrange("o s b d -> s (o b) d")).then_inc(ld_f, 16)
                        sp.dma_start(ctf_in[:].rearrange("d (b s) -> d b s", b=2),
                                     ct_d[p.rows()].rearrange("o d b s -> d (o b) s")).then_inc(ld_f, 16)
                    if p := due(t, j, "sp.store"):
                        sp.wait_ge(s_o, p.count(2, 2))
                        sp.sem_inc(s_sp_passed, 1)
                        sp.dma_start(o_d[p.rows()].rearrange("o s b d -> s (o b) d"), o_sb[:]).then_inc(stored, 16)

            turns(sp, body)
            sp.wait_ge(stored, 16 * PAIRS)

        @block.gpsimd
        def _(pool):
            pool.memset(ident[:], 0.0).then_inc(c_id, 1)
            pool.wait_ge(c_id, 1)
            pool.affine_select(out=ident[:], in_=ident[:], compare_op=ALU.not_equal, fill=1.0, base=0,
                               pattern=[[-1, P]], channel_multiplier=1).then_inc(c_id, 1)
            pool.memset(minus_half[:], -0.5).then_inc(c_misc, 1)
            pool.memset(eps_col[:], EPS).then_inc(c_misc, 1)
            pool.iota(expert_no[:], pattern=[[1, EXPERTS]], base=0, channel_multiplier=0,
                      allow_small_or_imprecise_dtypes=True).then_inc(c_misc, 1)
            pool.memset(ones[:], 1.0).then_inc(c_misc, 1)
            pool.memset(minus_one[:], -1.0).then_inc(c_misc, 1)
            pool.memset(inv_width[:], 1.0 / P).then_inc(c_misc, 1)
            pool.memset(minus_inv[:], -1.0 / P).then_inc(c_misc, 1)
            pool.memset(round_col[:], ROUND).then_inc(c_misc, 1)
            pool.wait_ge(c_id, 2)
            pool.tensor_copy(ident_bf[:], ident[:]).then_inc(c_misc, 1)
            pool.memset(v_diag[:], 0.0).then_inc(c_zero, 1)
            pool.wait_ge(c_misc, 9)

            def rstd(p, s_sq, s_rs, sq, rs, nmean):
                pool.wait_ge(s_sq, p.count(2, 2))
                pool.tensor_tensor(rs[:, 0], sq[:], inv_width[:], ALU.mult).then_inc(s_rs, 1)
                pool.wait_ge(s_rs, p.count(4, 1))
                pool.tensor_tensor(rs[:, 1], rs[:, 0], eps_col[:], ALU.add).then_inc(s_rs, 1)
                pool.wait_ge(s_rs, p.count(4, 2))
                pool.tensor_tensor(rs[:, 2], rs[:, 1], minus_half[:], ALU.pow).then_inc(s_rs, 1)
                pool.wait_ge(s_rs, p.count(4, 3))
                pool.tensor_tensor(rs[:, 3], rs[:, 2], nmean[:], ALU.mult).then_inc(s_rs, 1)

            def body(t):
                for j in range(SLOTS):
                    if p := due(t, j, "pool.ct_lo"):
                        pool.wait_ge(s_cthi, p.count(1, 1))
                        wait(pool, s_v, p.before().count(1, 1))
                        pool.tensor_tensor(ct_lo[:], ct_in[:], ct_hi[:].bitcast(F32), ALU.subtract).then_inc(s_ctlo, 1)
                    if p := due(t, j, "pool.a_rstd"):
                        rstd(p, s_asq, s_ars, a_sq, a_rs, a_nmean)
                    if p := due(t, j, "pool.a_mean"):
                        pool.wait_ge(s_ast, p.count(2, 2))
                        pool.tensor_tensor(a_nmean[:], a_sum[:], minus_inv[:], ALU.mult).then_inc(s_amv, 1)
                    if p := due(t, j, "pool.m_mean"):
                        pool.wait_ge(s_mst, p.count(2, 2))
                        pool.tensor_tensor(m_nmean[:], m_sum[:], minus_inv[:], ALU.mult).then_inc(s_mmv, 1)
                    if p := due(t, j, "pool.f_mean"):
                        pool.wait_ge(s_fst, p.count(2, 2))
                        pool.tensor_tensor(f_nmean[:], f_sum[:], minus_inv[:], ALU.mult).then_inc(s_fmv, 1)
                    if p := due(t, j, "pool.g_mean"):
                        pool.wait_ge(s_gst, p.count(2, 2))
                        pool.tensor_tensor(g_nmean[:], g_sum[:], minus_inv[:], ALU.mult).then_inc(s_gmv, 1)
                    for n in range(2):
                        if p := due(t, j, "pool.part3", n):
                            pool.wait_ge(s_p2[n], p.count(1, 1))
                            pool.tensor_tensor(qk_parts[:, n, 2], qk_rest[:, n], qk_parts[:, n, 1],
                                               ALU.subtract).then_inc(s_p3[n], 1)
                            if p.first and n == 1:
                                pool.wait_ge(c_mhi, 2)
                                pool.tensor_tensor(w01_lo[:, 1], w01_raw[:, 1], w01_hi[:, 1].bitcast(F32),
                                                   ALU.subtract).then_inc(c_mlo1, 1)
                    for n, k in enumerate(POOL_TILES):
                        if p := due(t, j, "pool.m_h", n):
                            pool.wait_ge(s_mu, p.count(TILES, k + 1))
                            pool.wait_ge(s_z1, p.count(len(POOL_TILES), n + 1))
                            wait(pool, s_dn, p.count(EXPERTS, k // TPE - 1))
                            pool.tensor_tensor(m_h[:, k % 4], m_u[:, k % 2], m_z1[:, n % 2],
                                               ALU.mult).then_inc(s_mhp, 1)
                    if p := due(t, j, "pool.m_rstd"):
                        rstd(p, s_msq, s_mrs, m_sq, m_rs, m_nmean)
                    if p := due(t, j, "pool.top_probs"):
                        pool.wait_ge(s_texp, p.count(1, 1))
                        wait(pool, s_w12, p.before().count(4, 4))
                        pool.wait_ge(c_thh, 1)
                        pool.tensor_tensor(tsum[:], texp[:], ones[:, 0:2].unsqueeze(2), ALU.add).then_inc(s_tp, 1)
                        pool.tensor_tensor(texp[:], texp[:], th_half[:].unsqueeze(1).to_broadcast([P, 2, 1]),
                                           ALU.mult).then_inc(s_tp, 1)
                        pool.wait_ge(s_tp, p.count(5, 2))
                        pool.tensor_tensor(tsum[:], tsum[:], minus_one[:].unsqueeze(1).to_broadcast([P, 2, 1]),
                                           ALU.pow).then_inc(s_tp, 1)
                        pool.wait_ge(s_tp, p.count(5, 3))
                        pool.tensor_tensor(tprob[:, :, 0:1], th_half[:].unsqueeze(1).to_broadcast([P, 2, 1]), tsum[:],
                                           ALU.mult).then_inc(s_tp, 1)
                        pool.tensor_tensor(tprob[:, :, 1:2], texp[:], tsum[:], ALU.mult).then_inc(s_tp, 1)
                    if p := due(t, j, "pool.f_rstd"):
                        rstd(p, s_fsq, s_frs, f_sq, f_rs, f_nmean)
                    if p := due(t, j, "pool.y_res"):
                        wait(pool, s_x3, p.before().count(1, 1))
                        pool.wait_ge(s_y, p.count(2 * EXPERTS, 2 * EXPERTS))
                        pool.wait_ge(c_thbo, 1)
                        pool.tensor_tensor(y_res[:], y[:], bl_all[:].unsqueeze(1).to_broadcast([P, 2, P]),
                                           ALU.add).then_inc(s_fyb, 1)
                    if p := due(t, j, "pool.g_rstd"):
                        rstd(p, s_gsq, s_grs, g_sq, g_rs, g_nmean)
                    if p := due(t, j, "pool.f_prod"):
                        pool.wait_ge(s_fc2, p.count(1, 1))
                        wait(pool, s_fz, p.before().count(1, 1))
                        pool.tensor_tensor(f_prod[:], f_ct[:], f_c2q[:], ALU.mult).then_inc(s_fpr, 1)
                    for u in range(4):
                        b, k0 = u // 2, HALF * (u % 2)
                        e = attn[:, b, :, k0:k0 + HALF]
                        if p := due(t, j, "pool.head_sum", u):
                            pool.wait_ge(s_exp, p.count(4, u + 1))
                            wait(pool, s_hinv, p.count(4, u - 1))
                            src, at, n = e, 0, HEADS // 2
                            lvl = 0
                            while n:
                                lvl += 1
                                dst = tree[:, u % 2, at:at + n, :]
                                pool.tensor_tensor(dst, src[:, 0:n, :], src[:, n:2 * n, :], ALU.add).then_inc(s_tree, 1)
                                if n > 1:
                                    pool.wait_ge(s_tree, p.count(16, 4 * u + lvl))
                                src, at, n = dst, at + n, n // 2
                        if p := due(t, j, "pool.head_norm", u):
                            pool.wait_ge(s_hinv, p.count(4, u + 1))
                            pool.tensor_tensor(e, e, head_inv[:, u % 2].unsqueeze(1).to_broadcast([P, HEADS, HALF]),
                                               ALU.mult).then_inc(s_attn, 1)

            turns(pool, body)

        @block.scalar
        def _(act):
            act.preload_act_table(ACT.Exp)
            for src, dst in (("wk", wqkv_raw[:, 1]), ("wq", wqkv_raw[:, 0]), ("wv", wqkv_raw[:, 2]),
                             ("bk", bqk[:, 1:2]), ("bq", bqk[:, 0:1])):
                act.dma_start(dst, A[src]).then_inc(w_attn, 16)
            def first_weights():
                act.wait_ge(w_moe, 48)
                for n in range(2):
                    act.activation(w01_hi[:, n], w01_raw[:, n], ACT.Copy).then_inc(c_mhi, 1)
                act.activation(gate_hi[:], gate_raw[:], ACT.Copy).then_inc(c_mhi, 1)
                act.wait_ge(w_out, 80)
                act.activation(th[:], gains[:], ACT.Tanh).then_inc(c_th, 1)

            def body(t):
                for j in range(SLOTS):
                    if p := due(t, j, "act.ct_hi"):
                        act.wait_ge(ld_a, p.count(32, 32))
                        wait(act, s_v, p.before().count(1, 1))
                        act.activation(ct_hi[:], ct_in[:], ACT.Copy).then_inc(s_cthi, 1)
                    if p := due(t, j, "act.a_xhi"):
                        act.wait_ge(s_axt, p.count(1, 1))
                        act.activation(a_xhi[:], ps_a[:, 0:TOK], ACT.Copy).then_inc(s_axhi, 1)
                    if p := due(t, j, "act.a_sum"):
                        act.wait_ge(ld_a, p.count(32, 32))
                        wait(act, s_axt, p.before().count(1, 1))
                        for b in range(2):
                            act.activation(a_xn[:, b], x_in[:, b], ACT.Identity,
                                           accum_out=a_sum[:, b:b + 1]).then_inc(s_ast, 1)
                    if p := due(t, j, "act.a_square"):
                        act.wait_ge(s_amv, p.count(1, 1))
                        for b in range(2):
                            act.activation(a_xn[:, b], x_in[:, b], ACT.Square, bias=a_nmean[:, b:b + 1],
                                           accum_out=a_sq[:, b:b + 1]).then_inc(s_asq, 1)
                        if p.first:
                            act.wait_ge(c_wq, 1)
                            act.wait_ge(w_attn, 80)
                            act.activation(wqkv_hi[:], wqkv_raw[:], ACT.Copy).then_inc(c_hi, 1)
                    if p := due(t, j, "act.a_norm"):
                        act.wait_ge(s_ars, p.count(4, 4))
                        for b in range(2):
                            act.activation(a_xn[:, b], x_in[:, b], ACT.Identity, scale=a_rs[:, 2, b:b + 1],
                                           bias=a_rs[:, 3, b:b + 1]).then_inc(s_axn, 1)
                    if p := due(t, j, "act.m_sum"):
                        act.wait_ge(s_x1, p.count(2, 2))
                        wait(act, s_mxt, p.before().count(1, 1))
                        for b in range(2):
                            act.activation(m_xn[:, b], x1[:, b], ACT.Identity,
                                           accum_out=m_sum[:, b:b + 1]).then_inc(s_mst, 1)
                    if p := due(t, j, "act.m_square"):
                        act.wait_ge(s_mmv, p.count(1, 1))
                        for b in range(2):
                            act.activation(m_xn[:, b], x1[:, b], ACT.Square, bias=m_nmean[:, b:b + 1],
                                           accum_out=m_sq[:, b:b + 1]).then_inc(s_msq, 1)
                    if p := due(t, j, "act.m_norm"):
                        act.wait_ge(s_mrs, p.count(4, 4))
                        for b in range(2):
                            act.activation(m_xn[:, b], x1[:, b], ACT.Identity, scale=m_rs[:, 2, b:b + 1],
                                           bias=m_rs[:, 3, b:b + 1]).then_inc(s_mxn, 1)
                    if p := due(t, j, "act.f_sum"):
                        act.wait_ge(s_y, p.count(2 * EXPERTS, 2 * EXPERTS))
                        wait(act, s_fq, p.before().count(1, 1))
                        for b in range(2):
                            act.activation(f_c[:, b], y[:, b], ACT.Identity,
                                           accum_out=f_sum[:, b:b + 1]).then_inc(s_fst, 1)
                    if p := due(t, j, "act.f_square"):
                        act.wait_ge(s_fmv, p.count(1, 1))
                        for b in range(2):
                            act.activation(f_c[:, b], y[:, b], ACT.Square, bias=f_nmean[:, b:b + 1],
                                           accum_out=f_sq[:, b:b + 1]).then_inc(s_fsq, 1)
                    if p := due(t, j, "act.f_norm"):
                        act.wait_ge(s_frs, p.count(4, 4))
                        for b in range(2):
                            act.activation(f_c[:, b], y[:, b], ACT.Identity, scale=f_rs[:, 2, b:b + 1],
                                           bias=f_rs[:, 3, b:b + 1]).then_inc(s_fc, 1)
                    if p := due(t, j, "act.g_sum"):
                        act.wait_ge(s_x3, p.count(1, 1))
                        wait(act, s_gr, p.before().count(2, 2))
                        for b in range(2):
                            act.activation(g_h[:, b], x3[:, b], ACT.Identity,
                                           accum_out=g_sum[:, b:b + 1]).then_inc(s_gst, 1)
                    if p := due(t, j, "act.g_square"):
                        act.wait_ge(s_gmv, p.count(1, 1))
                        for b in range(2):
                            act.activation(g_h[:, b], x3[:, b], ACT.Square, bias=g_nmean[:, b:b + 1],
                                           accum_out=g_sq[:, b:b + 1]).then_inc(s_gsq, 1)
                    if p := due(t, j, "act.g_norm"):
                        act.wait_ge(s_grs, p.count(4, 4))
                        for b in range(2):
                            act.activation(g_h[:, b], x3[:, b], ACT.Identity, scale=g_rs[:, 2, b:b + 1],
                                           bias=g_rs[:, 3, b:b + 1]).then_inc(s_gh, 1)
                    for n in range(2):
                        if p := due(t, j, "act.part1", n):
                            act.wait_ge(s_proj[n], p.count(1, 1))
                            wait(act, parts_out[n], p.before().count(16, 16))
                            act.activation(qk_parts[:, n, 0], ps_a[:, 0:TOK], ACT.Identity,
                                           bias=bqk[:, 1 - n:2 - n]).then_inc(s_p1[n], 1)
                        if p := due(t, j, "act.part2", n):
                            act.wait_ge(s_rest[n], p.count(1, 1))
                            act.activation(qk_parts[:, n, 1], qk_rest[:, n], ACT.Copy).then_inc(s_p2[n], 1)
                            if p.first and n == 1:
                                first_weights()
                    for k in range(TILES):
                        if p := due(t, j, "act.m_tanh", k):
                            act.wait_ge(s_z, p.count(TILES, k + 1))
                            wait(act, s_mu, p.count(TILES, k - 1))
                            if k in POOL_TILES:
                                n = POOL_TILES.index(k)
                                wait(act, s_mhp, p.count(len(POOL_TILES), n - 1))
                                act.activation(m_z1[:, n % 2], ps_z[k % 2][:, TOK:2 * TOK],
                                               ACT.Copy).then_inc(s_z1, 1)
                            act.activation(m_tanh[:, k % 2], ps_z[k % 2][:, 0:TOK], ACT.Tanh,
                                           scale=0.5).then_inc(s_mt, 1)
                    if p := due(t, j, "act.m_xhi"):
                        act.wait_ge(s_mxt, p.count(1, 1))
                        wait(act, s_z, p.before().count(TILES, TILES))
                        act.activation(m_xhi[:], ps_d[:, 0:TOK], ACT.Copy).then_inc(s_mxhi, 1)
                    for u in range(4):
                        if p := due(t, j, "act.head_exp", u):
                            b, k0 = u // 2, HALF * (u % 2)
                            act.wait_ge(s_shift, p.count(4, u + 1))
                            wait(act, s_pv, p.before().count(2, b + 1))
                            act.activation(attn[:, b, :, k0:k0 + HALF], shifted[:, u % 2], ACT.Exp).then_inc(s_exp, 1)
                    for b in range(2):
                        if p := due(t, j, "act.o_t", b):
                            act.wait_ge(s_pv, p.count(2, b + 1))
                            wait(act, s_res, p.before().count(2, b + 1))
                            act.activation(o_t[:, b], ps_a[:, 0:P], ACT.Copy).then_inc(s_ot, 1)
                    if p := due(t, j, "act.v_diag"):
                        if p.first:
                            act.wait_ge(c_zero, 1)
                        act.wait_ge(s_v, p.count(1, 1))
                        wait(act, s_pv, p.before().count(2, 2))
                        for b in range(2):
                            dst = v_diag[:, b].rearrange("p (m s) -> p m s", s=VSTEP)[:, :, 0:DH]
                            src = ps_a[:, b * P:(b + 1) * P].rearrange("p (m d) -> p m d", d=DH)
                            act.activation(dst, src, ACT.Copy).then_inc(s_vd, 1)
                    if p := due(t, j, "act.top_exp"):
                        act.wait_ge(s_tdf, p.count(1, 1))
                        wait(act, s_tp, p.before().count(5, 5))
                        act.activation(texp[:], tdiff[:], ACT.Exp).then_inc(s_texp, 1)
                    if p := due(t, j, "act.f_ct"):
                        act.wait_ge(s_fct, p.count(1, 1))
                        wait(act, s_fz, p.before().count(1, 1))
                        act.activation(f_ct[:], ps_f[:, 0:TOK], ACT.Copy).then_inc(s_fcs, 1)
                        wait(act, s_fs, p.before().count(1, 1))
                        act.activation(f_ctq[:], ps_f[:, 0:TOK], ACT.Identity, scale=wcq[:, 0:1],
                                       bias=wcq[:, 1:2]).then_inc(s_fcq, 1)
                    if p := due(t, j, "act.f_exp"):
                        act.wait_ge(s_fm, p.count(1, 1))
                        wait(act, s_fan, p.before().count(2, 2))
                        for b in range(2):
                            act.activation(f_a[:, b], ps_f[:, b * P:(b + 1) * P], ACT.Exp, bias=f_nmax[:, b:b + 1],
                                           accum_out=f_asum[:, b:b + 1]).then_inc(s_fa, 1)
                    if p := due(t, j, "act.f_an"):
                        act.wait_ge(s_fai, p.count(1, 1))
                        wait(act, s_fat, p.before().count(1, 1))
                        for b in range(2):
                            act.activation(f_an[:, b], f_a[:, b], ACT.Identity,
                                           scale=f_ainv[:, b:b + 1]).then_inc(s_fan, 1)
                    if p := due(t, j, "act.f_at"):
                        act.wait_ge(s_fat, p.count(1, 1))
                        wait(act, s_fq, p.before().count(1, 1))
                        act.activation(f_at[:], ps_f[:, 0:TOK], ACT.Copy).then_inc(s_fats, 1)
                    if p := due(t, j, "act.f_exp_max"):
                        act.wait_ge(s_fnmm, p.count(1, 1))
                        wait(act, s_fei, p.before().count(1, 1))
                        wait(act, s_fe, p.before().count(4, 4))
                        wait(act, s_fq, p.before().count(1, 1))
                        for b in range(2):
                            act.activation(f_erow[:, b], ps_f[:, TOK + b * P:TOK + (b + 1) * P], ACT.Exp,
                                           bias=f_nmm[:, b:b + 1], accum_out=f_esum[:, b:b + 1]).then_inc(s_fe, 1)
                        for b in range(2):
                            act.activation(f_e[:, b:b + 1], f_m[:, b:b + 1], ACT.Exp,
                                           bias=f_nmm[:, b:b + 1]).then_inc(s_fe, 1)
                    if p := due(t, j, "act.f_c2q"):
                        act.wait_ge(s_fq, p.count(1, 1))
                        wait(act, s_fz, p.before().count(1, 1))
                        wait(act, s_fpr, p.before().count(1, 1))
                        act.activation(f_c2q[:], ps_f[:, 0:TOK], ACT.Copy).then_inc(s_fc2, 1)
                    if p := due(t, j, "act.f_w4"):
                        act.wait_ge(s_fq2, p.count(1, 1))
                        wait(act, s_fz, p.before().count(1, 1))
                        for b in range(2):
                            act.activation(f_w4[:, b], wl[:, 3], ACT.Identity,
                                           scale=f_q2c[:, b:b + 1]).then_inc(s_fw, 1)
                    if p := due(t, j, "act.g_r"):
                        act.wait_ge(s_gsc, p.count(5, 5))
                        wait(act, s_gq, p.before().count(1, 1))
                        for b in range(2):
                            act.activation(g_r[:, b], g_h[:, b], ACT.Identity, scale=g_sc[:, b, 0:1],
                                           bias=round_col[:, 0:1]).then_inc(s_gr, 1)
                    if p := due(t, j, "act.g_qt"):
                        act.wait_ge(s_gqt, p.count(1, 1))
                        wait(act, s_gu, p.before().count(4, 4))
                        act.activation(g_qt[:], ps_g[:, 0:P].bitcast(BF16), ACT.Copy).then_inc(s_gqs, 1)
                    for u in range(4):
                        if p := due(t, j, "act.g_tanh", u):
                            act.wait_ge(s_gu, p.count(4, u + 1))
                            wait(act, s_guu, p.count(4, u))
                            act.activation(g_tanh[:], ps_g[:, 0:256], ACT.Tanh,
                                           scale=g_sc[:, u // 2, 1:2]).then_inc(s_gt, 1)
                    for b in range(2):
                        if p := due(t, j, "act.g_pr", b):
                            act.wait_ge(s_gps, p.count(8, 4 * b + 4))
                            wait(act, s_gpq, p.before().count(2, b + 1))
                            act.activation(g_pr[:, b], g_p[:, b], ACT.Identity, scale=g_ps[:, b, 0:1],
                                           bias=round_col[:, 0:1]).then_inc(s_gpr, 1)
                        if p := due(t, j, "act.g_pq", b):
                            act.wait_ge(s_gpr, p.count(2, b + 1))
                            wait(act, s_gpt, p.before().count(2, 2))
                            act.activation(g_pq[:, b], g_pr[:, b], ACT.Copy, bias=-ROUND).then_inc(s_gpq, 1)
                        if p := due(t, j, "act.g_pt", b):
                            act.wait_ge(s_gpt, p.count(2, b + 1))
                            wait(act, s_gd, p.before().count(2, 2))
                            act.activation(g_pt[:, b], ps_g[:, 0:TOK].bitcast(BF16), ACT.Copy).then_inc(s_gpts, 1)

            turns(act, body)

        @block.tensor
        def _(pe):
            def split_product(dst, hi_w, lo_w, hi_x, lo_x, start=True):
                pe.matmul(dst, hi_w, hi_x, start=start, stop=False)
                pe.matmul(dst, lo_w, hi_x, start=False, stop=False)
                return pe.matmul(dst, hi_w, lo_x, start=False, stop=True)

            def body(t):
                for j in range(SLOTS):
                    for u in range(4):
                        if p := due(t, j, "pe.scores", u):
                            b, k0 = u // 2, HALF * (u % 2)
                            if u == 0:
                                for n in range(2):
                                    pe.wait_ge(rows_in[n], p.count(96, 96))
                            wait(pe, s_shift, p.count(4, u))
                            for hp in range(HEADS // 2):
                                for hq in range(2):
                                    r = slice(hq * HALF, hq * HALF + 6 * DH)
                                    last = pe.matmul(ps_sc[:, hq, hp * HALF:(hp + 1) * HALF],
                                                     k_rows[r, hp, b * P:(b + 1) * P],
                                                     q_rows[r, hp, b * P + k0:b * P + k0 + HALF],
                                                     start=True, stop=True, tile_position=(hq * HALF, 0))
                            last.then_inc(s_score, 1)
                    if p := due(t, j, "pe.m_xt"):
                        wait(pe, s_y, p.before().count(2 * EXPERTS, 2 * EXPERTS))
                        pe.wait_ge(s_mxn, p.count(2, 2))
                        for b in range(2):
                            last = pe.transpose(ps_d[:, b * P:(b + 1) * P], m_xn[:, b], ident[:])
                        last.then_inc(s_mxt, 1)
                    if p := due(t, j, "pe.gate"):
                        pe.wait_ge(s_mxlo, p.count(1, 1))
                        if p.first:
                            pe.wait_ge(c_mlo, 2)
                            pe.wait_ge(c_mlo1, 1)
                        for b in range(2):
                            s = slice(b * P, (b + 1) * P)
                            last = split_product(ps_d[:, b * EXPERTS:(b + 1) * EXPERTS], m_xhi[:, s],
                                                 m_xlo[:, s], gate_hi[:], gate_lo[:])
                        last.then_inc(s_gate, 1)
                    if p := due(t, j, "pe.a_xt"):
                        if p.first:
                            pe.wait_ge(c_id, 2)
                            pe.wait_ge(c_misc, 9)
                        pe.wait_ge(s_axn, p.count(2, 2))
                        wait(pe, s_vd, p.before().count(2, 2))
                        for b in range(2):
                            last = pe.transpose(ps_a[:, b * P:(b + 1) * P], a_xn[:, b], ident[:])
                        last.then_inc(s_axt, 1)
                    if p := due(t, j, "pe.kq", 0):
                        if p.first:
                            pe.wait_ge(c_lo, 1)
                        pe.wait_ge(s_ctlo, p.count(1, 1))
                        pe.wait_ge(s_axlo, p.count(1, 1))
                        split_product(ps_a[:, 0:TOK], wqkv_hi[:, 1], wqkv_lo[:, 1], ct_hi[:], ct_lo[:]
                                      ).then_inc(s_proj[0], 1)
                    if p := due(t, j, "pe.kq", 1):
                        pe.wait_ge(s_rest[0], p.count(1, 1))
                        split_product(ps_a[:, 0:TOK], wqkv_hi[:, 0], wqkv_lo[:, 0], a_xhi[:], a_xlo[:]
                                      ).then_inc(s_proj[1], 1)
                        if p.first:
                            pe.wait_ge(c_abs, 1)
                            pe.matmul(ps_g[:, 0:3], ones[:], wabs[:], start=True, stop=True).then_inc(c_tot, 1)
                    if p := due(t, j, "pe.v"):
                        pe.wait_ge(s_rest[1], p.count(1, 1))
                        wait(pe, s_x1, p.before().count(2, 2))
                        if p.first:
                            pe.wait_ge(w_out, 80)
                        for b in range(2):
                            s = slice(b * P, (b + 1) * P)
                            pe.matmul(ps_a[:, s], ones[0:1], bv_row[:], start=True, stop=False)
                            last = split_product(ps_a[:, s], ct_hi[:, s], ct_lo[:, s], wqkv_hi[:, 2], wqkv_lo[:, 2],
                                                 start=False)
                        last.then_inc(s_v, 1)
                    if p := due(t, j, "pe.f_ct"):
                        pe.wait_ge(s_fc, p.count(2, 2))
                        wait(pe, s_x3, p.before().count(1, 1))
                        for b in range(2):
                            last = pe.transpose(ps_f[:, b * P:(b + 1) * P], f_c[:, b], ident[:])
                        last.then_inc(s_fct, 1)
                    if p := due(t, j, "pe.f_scores"):
                        pe.wait_ge(s_fcq, p.count(1, 1))
                        pe.wait_ge(ld_f, p.count(32, 32))
                        for b in range(2):
                            s = slice(b * P, (b + 1) * P)
                            pe.matmul(ps_f[:, s], f_ctq[:, s], ctf_in[:, s], start=True, stop=True)
                        for b in range(2):
                            s = slice(b * P, (b + 1) * P)
                            last = pe.matmul(ps_f[:, TOK + b:TOK + b + 1], f_ct[:, s], wcq[:, 2:3],
                                             start=True, stop=True)
                        last.then_inc(s_fs, 1)
                    if p := due(t, j, "pe.f_at"):
                        pe.wait_ge(s_fan, p.count(2, 2))
                        for b in range(2):
                            pe.transpose(ps_f[:, b * P:(b + 1) * P], f_an[:, b], ident[:])
                        for b in range(2):
                            last = pe.matmul(ps_f[:, TOK + b * P:TOK + (b + 1) * P],
                                             f_m[:, b:b + 1].to_broadcast([P, P]), ident[:], start=True, stop=True)
                        last.then_inc(s_fat, 1)
                    if p := due(t, j, "pe.f_c2q"):
                        pe.wait_ge(s_fats, p.count(1, 1))
                        pe.wait_ge(s_fe, p.count(4, 4))
                        for b in range(2):
                            pe.matmul(ps_f[:, b * P:(b + 1) * P], ctx_in[:, b], f_at[:, b * P:(b + 1) * P],
                                      start=True, stop=True)
                        for b in range(2):
                            last = pe.matmul(ps_f[:, TOK + b:TOK + b + 1], f_c[:, b], f_e[:, b:b + 1],
                                             start=True, stop=True)
                        last.then_inc(s_fq, 1)
                    if p := due(t, j, "pe.f_z"):
                        pe.wait_ge(s_fw, p.count(2, 2))
                        pe.wait_ge(s_fpr, p.count(1, 1))
                        for b in range(2):
                            s = slice(b * P, (b + 1) * P)
                            pe.matmul(ps_f[:, s], f_ct[:, s], wl[:, 0], start=True, stop=False)
                            pe.matmul(ps_f[:, s], f_ct[:, s], f_w4[:, b], start=False, stop=False)
                            pe.matmul(ps_f[:, s], f_c2q[:, s], wl[:, 1], start=False, stop=False)
                            last = pe.matmul(ps_f[:, s], f_prod[:, s], wl[:, 2], start=False, stop=True)
                        last.then_inc(s_fz, 1)
                    if p := due(t, j, "pe.g_qt"):
                        pe.wait_ge(s_gq, p.count(1, 1))
                        wait(pe, s_o, p.before().count(2, 2))
                        for b in range(2):
                            last = pe.transpose(ps_g[:, b * HALF:(b + 1) * HALF].bitcast(BF16), g_q[:, b], ident_bf[:])
                        last.then_inc(s_gqt, 1)
                    for u in range(4):
                        if p := due(t, j, "pe.g_up", u):
                            b, c0 = u // 2, 256 * (u % 2)
                            pe.wait_ge(s_gqs, p.count(1, 1))
                            wait(pe, s_gp, p.count(4, u))
                            for n in range(2):
                                last = pe.matmul(ps_g[:, 256 * n:256 * (n + 1)], g_qt[:, b * P:(b + 1) * P],
                                                 wf_q[:, n, c0:c0 + 256], start=True, stop=True)
                            last.then_inc(s_gu, 1)
                    for b in range(2):
                        if p := due(t, j, "pe.g_pt", b):
                            pe.wait_ge(s_gpq, p.count(2, b + 1))
                            pe.wait_ge(s_gp, p.count(4, 4))
                            wait(pe, s_o, p.count(2, b))
                            for k in range(NI):
                                last = pe.transpose(ps_g[:, k * HALF:(k + 1) * HALF].bitcast(BF16),
                                                    g_pq[:, b, k * P:(k + 1) * P], ident_bf[:])
                            last.then_inc(s_gpt, 1)
                        if p := due(t, j, "pe.g_down", b):
                            pe.wait_ge(s_gpts, p.count(2, b + 1))
                            for k in range(NI):
                                last = pe.matmul(ps_g[:, 0:P], g_pt[:, b, k * P:(k + 1) * P],
                                                 wf_q[:, 2, k * P:(k + 1) * P], start=(k == 0), stop=(k == NI - 1))
                            last.then_inc(s_gd, 1)
                    for b in range(2):
                        if p := due(t, j, "pe.weighted_v", 2 * b):
                            pe.wait_ge(s_attn, p.count(4, 2 * b + 2))
                            if b == 0:
                                pe.wait_ge(s_vd, p.count(2, 2))
                                if n := p.after():
                                    pe.wait_ge(s_rest[1], n.count(1, 1))
                            else:
                                pe.wait_ge(s_x1, p.count(2, 1))
                            for m in range(HEADS // 2):
                                pe.matmul(ps_a[:, 0:P], v_diag[:, b, m * P:(m + 1) * P], attn[:, b, m],
                                          start=(m == 0), stop=False)
                        if p := due(t, j, "pe.weighted_v", 2 * b + 1):
                            for m in range(HEADS // 2, HEADS):
                                last = pe.matmul(ps_a[:, 0:P], v_diag[:, b, m * P:(m + 1) * P], attn[:, b, m],
                                                 start=False, stop=(m == HEADS - 1))
                            last.then_inc(s_pv, 1)
                        if p := due(t, j, "pe.out", b):
                            pe.wait_ge(s_ot, p.count(2, b + 1))
                            pe.matmul(ps_a[:, 0:P], o_t[:, b], wo_t[:], start=True, stop=False)
                            pe.matmul(ps_a[:, 0:P], ones[0:1], bo_row[:], start=False, stop=True).then_inc(s_res, 1)
                    for n in range(EXPERTS):
                        if p := due(t, j, "pe.down", n):
                            for k in range(TPE * n, TPE * (n + 1)):
                                wait_product(pe, p, k)
                            if n == 0:
                                if p.first:
                                    pe.wait_ge(w_late, 32)
                                pe.wait_ge(s_log, p.count(1, 1))
                            wait(pe, s_y, p.count(2 * EXPERTS, 2 * n))
                            for b in range(2):
                                for k in range(TPE):
                                    m = TPE * n + k
                                    last = pe.matmul(ps_d[:, b * P:(b + 1) * P], m_h[:, m % 4, b * P:(b + 1) * P],
                                                     wdn[:, m], start=(k == 0), stop=(k == TPE - 1))
                            last.then_inc(s_dn, 1)
                    for k in range(TILES):
                        if p := due(t, j, "pe.up", k):
                            if k == 0:
                                pe.wait_ge(s_mxlo, p.count(1, 1))
                            wait(pe, s_mu, p.count(TILES, k - 1))
                            r = (k - 2) % TILES
                            q = p.before() if k < 2 else p
                            if r in POOL_TILES:
                                wait(pe, s_z1, q.count(len(POOL_TILES), POOL_TILES.index(r) + 1))
                            else:
                                wait(pe, s_mh, q.count(len(DVE_TILES), DVE_TILES.index(r) + 1))
                            for n in range(2):
                                w = slice(k * P, (k + 1) * P)
                                last = split_product(ps_z[k % 2][:, n * TOK:(n + 1) * TOK], w01_hi[:, n, w],
                                                     w01_lo[:, n, w], m_xhi[:], m_xlo[:])
                            last.then_inc(s_z, 1)

            turns(pe, body)

        @block.vector
        def _(dve):
            inv = float(DH) ** -0.5
            dve.wait_ge(w_attn, 80)
            dve.tensor_scalar(wqkv_raw[:, 0], wqkv_raw[:, 0], inv, None, ALU.mult).then_inc(c_wq, 1)
            dve.tensor_scalar(bqk[:, 0:1], bqk[:, 0:1], inv, None, ALU.mult).then_inc(c_wq, 1)
            dve.wait_ge(c_hi, 1)
            dve.tensor_tensor(wqkv_lo[:], wqkv_raw[:], wqkv_hi[:].bitcast(F32), ALU.subtract).then_inc(c_lo, 1)

            def first_weights():
                dve.wait_ge(c_mhi, 1)
                dve.tensor_tensor(w01_lo[:, 0], w01_raw[:, 0], w01_hi[:, 0].bitcast(F32),
                                  ALU.subtract).then_inc(c_mlo, 1)
                dve.wait_ge(c_mhi, 3)
                dve.tensor_tensor(gate_lo[:], gate_raw[:], gate_hi[:].bitcast(F32), ALU.subtract).then_inc(c_mlo, 1)
                dve.wait_ge(c_th, 1)
                dve.tensor_scalar(th_half[:], th[:, 2:3], 0.5, None, ALU.mult).then_inc(c_thh, 1)
                dve.wait_ge(w_fin, 112)
                dve.tensor_scalar(bl_all[:], bl_all[:], th[:, 1:2], None, ALU.mult).then_inc(c_thbo, 1)
                dve.tensor_reduce(bsum[:], bsum3[:], AX.X, ALU.add).then_inc(c_bs, 1)
                dve.wait_ge(w_ffn, 48)
                dve.tensor_reduce(wabs[:], wf_raw[:], AX.X, ALU.add, apply_absolute_value=True).then_inc(c_abs, 1)
                dve.wait_ge(c_tot, 1)
                dve.tensor_scalar(wmean[:], ps_g[:, 0:3], 1.0 / (P * INNER), 1e-5, ALU.mult,
                                  ALU.max).then_inc(c_wm, 1)
                dve.wait_ge(c_wm, 1)
                dve.reciprocal(wscale[:], wmean[:]).then_inc(c_wm, 1)
                dve.tensor_scalar(cg[:, 0:1], wmean[:, 0:1], 0.5 / 127.0, None, ALU.mult).then_inc(c_wm, 1)
                dve.tensor_scalar(cg[:, 2:3], wmean[:, 2:3], th[:, 3:4], 1.0 / 127.0, ALU.mult,
                                  ALU.mult).then_inc(c_wm, 1)
                dve.wait_ge(c_wm, 3)
                dve.tensor_scalar(cg[:, 1:2], wmean[:, 1:2], cg[:, 0:1], 1.0 / 127.0, ALU.mult,
                                  ALU.mult).then_inc(c_wm, 1)
                for n in range(3):
                    dve.tensor_scalar(wf_r[:, n], wf_raw[:, n], wscale[:, n:n + 1], ROUND, ALU.mult,
                                      ALU.add).then_inc(c_wr, 1)
                dve.wait_ge(c_wr, 3)
                dve.tensor_scalar(wf_t[:], wf_r[:], ROUND, 1.0, ALU.subtract, ALU.min).then_inc(c_wr, 1)
                dve.wait_ge(c_wr, 4)
                dve.tensor_scalar(wf_q[:], wf_t[:], -1.0, None, ALU.max).then_inc(c_wr, 1)

            def body(t):
                for j in range(SLOTS):
                    for u in range(4):
                        if p := due(t, j, "dve.head_max", u):
                            dve.wait_ge(s_score, p.count(4, u + 1))
                            wait(dve, s_shift, p.count(4, u - 1))
                            sc = ps_sc[:].rearrange("p a (h k) -> p (a h) k", k=HALF)
                            dve.tensor_reduce(head_max[:, u % 2], sc.rearrange("p h k -> p k h"), AX.X,
                                              ALU.max).then_inc(s_hmax, 1)
                        if p := due(t, j, "dve.head_shift", u):
                            sc = ps_sc[:].rearrange("p a (h k) -> p (a h) k", k=HALF)
                            dve.wait_ge(s_hmax, p.count(4, u + 1))
                            wait(dve, s_exp, p.count(4, u - 1))
                            dve.tensor_tensor(shifted[:, u % 2], sc,
                                              head_max[:, u % 2].unsqueeze(1).to_broadcast([P, HEADS, HALF]),
                                              ALU.subtract).then_inc(s_shift, 1)
                        if p := due(t, j, "dve.head_inv", u):
                            dve.wait_ge(s_tree, p.count(16, 4 * u + 4))
                            wait(dve, s_attn, p.count(4, u - 1))
                            dve.reciprocal(head_inv[:, u % 2], tree[:, u % 2, 14]).then_inc(s_hinv, 1)
                    if p := due(t, j, "dve.m_xlo"):
                        dve.wait_ge(s_mxhi, p.count(1, 1))
                        dve.tensor_tensor(m_xlo[:], ps_d[:, 0:TOK], m_xhi[:].bitcast(F32),
                                          ALU.subtract).then_inc(s_mxlo, 1)
                    if p := due(t, j, "dve.logits"):
                        dve.wait_ge(s_gate, p.count(1, 1))
                        wait(dve, s_topi, p.before().count(2, 2))
                        dve.tensor_copy(logits[:], ps_d[:, 0:2 * EXPERTS].rearrange("p (b n) -> p b n", b=2)
                                        ).then_inc(s_log, 1)
                    for k in range(TILES):
                        if p := due(t, j, "dve.m_u", k):
                            dve.wait_ge(s_mt, p.count(TILES, k + 1))
                            wait_product(dve, p, k - 2)
                            z = ps_z[k % 2]
                            dve.scalar_tensor_tensor(m_u[:, k % 2], m_tanh[:, k % 2], 1.0, z[:, 0:TOK], ALU.add,
                                                     ALU.mult).then_inc(s_mu, 1)
                        if k in POOL_TILES:
                            continue
                        if p := due(t, j, "dve.m_h", DVE_TILES.index(k)):
                            z = ps_z[k % 2]
                            dve.wait_ge(s_mu, p.count(TILES, k + 1))
                            wait(dve, s_dn, p.count(EXPERTS, k // TPE - 1))
                            dve.tensor_tensor(m_h[:, k % 4], m_u[:, k % 2], z[:, TOK:2 * TOK],
                                              ALU.mult).then_inc(s_mh, 1)
                    if p := due(t, j, "dve.top2"):
                        dve.wait_ge(s_log, p.count(1, 1))
                        for b in range(2):
                            dve.sem_inc(s_passed, 1)
                            dve.max(top[:, b], logits[:, b]).then_inc(s_top, 1)
                        for b in range(2):
                            dve.wait_ge(s_top, p.count(2, b + 1))
                            dve.sem_inc(s_passed, 1)
                            dve.max_index(top_no[:, b], top[:, b], logits[:, b]).then_inc(s_topi, 1)
                        wait(dve, s_texp, p.before().count(1, 1))
                        dve.tensor_tensor(tdiff[:], top[:, :, 1:2], top[:, :, 0:1], ALU.subtract).then_inc(s_tdf, 1)
                        dve.wait_ge(s_topi, p.count(2, 2))
                        wait(dve, s_w12, p.before().count(4, 4))
                        dve.tensor_copy(top_nof[:], top_no[:]).then_inc(s_tnof, 1)
                    for n in range(EXPERTS):
                        if p := due(t, j, "dve.y", n):
                            dve.wait_ge(s_dn, p.count(EXPERTS, n + 1))
                            if n == 0:
                                dve.wait_ge(s_w, p.count(1, 1))
                                wait(dve, s_fyb, p.before().count(1, 1))
                                wait(dve, s_fc, p.before().count(2, 2))
                            for b in range(2):
                                if n:
                                    dve.wait_ge(s_y, p.count(2 * EXPERTS, 2 * n - 1 + b))
                                dve.scalar_tensor_tensor(y[:, b], ps_d[:, b * P:(b + 1) * P],
                                                         weights[:, b, n:n + 1], (y if n else x1)[:, b],
                                                         ALU.mult, ALU.add).then_inc(s_y, 1)
                    if p := due(t, j, "dve.weights"):
                        dve.wait_ge(s_tp, p.count(5, 5))
                        dve.wait_ge(s_tnof, p.count(1, 1))
                        wait(dve, s_w, p.before().count(1, 1))
                        for b in range(2):
                            for k, dst in enumerate((w_first, w_second)):
                                dve.tensor_scalar(dst[:, b], expert_no[:], top_nof[:, b, k:k + 1],
                                                  tprob[:, b, k:k + 1], ALU.is_equal, ALU.mult).then_inc(s_w12, 1)
                    if p := due(t, j, "dve.weights_sum"):
                        dve.wait_ge(s_w12, p.count(4, 4))
                        wait(dve, s_y, p.before().count(2 * EXPERTS, 2 * EXPERTS))
                        dve.tensor_tensor(weights[:], w_first[:], w_second[:], ALU.add).then_inc(s_w, 1)
                    for b in range(2):
                        if p := due(t, j, "dve.x1", b):
                            dve.wait_ge(s_res, p.count(2, b + 1))
                            dve.wait_ge(ld_res, p.count(16, 16))
                            wait(dve, s_y, p.before().count(2 * EXPERTS, 2))
                            dve.scalar_tensor_tensor(x1[:, b], ps_a[:, 0:P], th[:, 0:1], x_res[:, b], ALU.mult,
                                                     ALU.add).then_inc(s_x1, 1)
                    if p := due(t, j, "dve.a_xlo"):
                        dve.wait_ge(s_axhi, p.count(1, 1))
                        dve.tensor_tensor(a_xlo[:], ps_a[:, 0:TOK], a_xhi[:].bitcast(F32),
                                          ALU.subtract).then_inc(s_axlo, 1)
                    for n in range(2):
                        if p := due(t, j, "dve.part_rest", n):
                            dve.wait_ge(s_p1[n], p.count(1, 1))
                            wait(dve, s_p3[n], p.before().count(1, 1))
                            dve.scalar_tensor_tensor(qk_rest[:, n], ps_a[:, 0:TOK], bqk[:, 1 - n:2 - n],
                                                     qk_parts[:, n, 0], ALU.add, ALU.subtract).then_inc(s_rest[n], 1)
                            if p.first and n == 1:
                                first_weights()
                    if p := due(t, j, "dve.f_max"):
                        dve.wait_ge(s_fs, p.count(1, 1))
                        wait(dve, s_fa, p.before().count(2, 2))
                        dve.tensor_reduce(f_nmax[:], ps_f[:, 0:TOK].rearrange("p (b q) -> p b q", b=2), AX.X, ALU.max,
                                          negate=True).then_inc(s_fnm, 1)
                        dve.wait_ge(s_fnm, p.count(1, 1))
                        wait(dve, s_fe, p.before().count(4, 4))
                        dve.scalar_tensor_tensor(f_m[:], ps_f[:, TOK:TOK + 2], bsum[:, 0:1], f_nmax[:], ALU.add,
                                                 ALU.subtract).then_inc(s_fm, 1)
                    if p := due(t, j, "dve.f_ainv"):
                        dve.wait_ge(s_fa, p.count(2, 2))
                        wait(dve, s_fan, p.before().count(2, 2))
                        dve.reciprocal(f_ainv[:], f_asum[:]).then_inc(s_fai, 1)
                    if p := due(t, j, "dve.f_max_max"):
                        dve.wait_ge(s_fats, p.count(1, 1))
                        dve.tensor_reduce(f_nmm[:], ps_f[:, TOK:2 * TOK].rearrange("p (b q) -> p b q", b=2), AX.X,
                                          ALU.max, negate=True).then_inc(s_fnmm, 1)
                    if p := due(t, j, "dve.f_q2c"):
                        dve.wait_ge(s_fe, p.count(4, 2))
                        dve.reciprocal(f_einv[:], f_esum[:]).then_inc(s_fei, 1)
                        dve.wait_ge(s_fei, p.count(1, 1))
                        dve.wait_ge(s_fc2, p.count(1, 1))
                        wait(dve, s_fw, p.before().count(2, 2))
                        dve.tensor_tensor(f_q2c[:], ps_f[:, TOK:TOK + 2], f_einv[:], ALU.mult).then_inc(s_fq2, 1)
                    for b in range(2):
                        if p := due(t, j, "dve.out", b):
                            dve.wait_ge(s_gd, p.count(2, b + 1))
                            wait(dve, stored, p.before().count(16, 16))
                            dve.scalar_tensor_tensor(o_sb[:, b], ps_g[:, 0:P], g_ps[:, b, 1:2], x3[:, b], ALU.mult,
                                                     ALU.add).then_inc(s_o, 1)
                    if p := due(t, j, "dve.x3"):
                        dve.wait_ge(s_fz, p.count(1, 1))
                        dve.wait_ge(s_fyb, p.count(1, 1))
                        wait(dve, s_o, p.before().count(2, 2))
                        dve.scalar_tensor_tensor(x3[:], ps_f[:, 0:TOK].rearrange("p (b d) -> p b d", b=2), th[:, 1:2],
                                                 y_res[:], ALU.mult, ALU.add).then_inc(s_x3, 1)
                    if p := due(t, j, "dve.g_amax"):
                        dve.wait_ge(s_gh, p.count(2, 2))
                        dve.tensor_reduce(g_amax[:], g_h[:], AX.X, ALU.max,
                                          apply_absolute_value=True).then_inc(s_gam, 1)
                    if p := due(t, j, "dve.g_clamp"):
                        dve.wait_ge(s_gam, p.count(1, 1))
                        wait(dve, s_gt, p.before().count(4, 4))
                        dve.tensor_scalar(g_amc[:], g_amax[:], 1e-5, None, ALU.max).then_inc(s_gsc, 1)
                    if p := due(t, j, "dve.g_scales"):
                        dve.wait_ge(s_gsc, p.count(5, 1))
                        dve.reciprocal(g_ainv[:], g_amc[:]).then_inc(s_gsc, 1)
                        dve.tensor_scalar(g_sc[:, :, 1], g_amc[:], cg[:, 0:1], None, ALU.mult).then_inc(s_gsc, 1)
                        dve.scalar_tensor_tensor(g_sc[:, :, 2], g_amc[:], cg[:, 1:2], g_amc[:], ALU.mult,
                                                 ALU.mult).then_inc(s_gsc, 1)
                        dve.wait_ge(s_gsc, p.count(5, 2))
                        dve.tensor_scalar(g_sc[:, :, 0], g_ainv[:], 127.0, None, ALU.mult).then_inc(s_gsc, 1)
                    if p := due(t, j, "dve.g_q"):
                        dve.wait_ge(s_gr, p.count(2, 2))
                        wait(dve, s_gqt, p.before().count(1, 1))
                        dve.tensor_scalar(g_q[:], g_r[:], ROUND, 127.0, ALU.subtract, ALU.min).then_inc(s_gq, 1)
                    for u in range(4):
                        if p := due(t, j, "dve.g_u", u):
                            b, c0 = u // 2, 256 * (u % 2)
                            dve.wait_ge(s_gt, p.count(4, u + 1))
                            wait(dve, s_gp, p.count(4, u))
                            dve.scalar_tensor_tensor(g_u[:], g_tanh[:], 1.0, ps_g[:, 0:256], ALU.add,
                                                     ALU.mult).then_inc(s_guu, 1)
                        if p := due(t, j, "dve.g_p", u):
                            b, c0 = u // 2, 256 * (u % 2)
                            dve.wait_ge(s_guu, p.count(4, u + 1))
                            wait(dve, s_gpr, p.before().count(2, 2))
                            dve.scalar_tensor_tensor(g_p[:, b, c0:c0 + 256], g_u[:], g_sc[:, b, 2:3], ps_g[:, 256:512],
                                                     ALU.mult, ALU.mult).then_inc(s_gp, 1)
                    for b in range(2):
                        if p := due(t, j, "dve.g_pmax", b):
                            dve.wait_ge(s_gp, p.count(4, 2 * b + 2))
                            dve.tensor_reduce(g_pmax[:, b:b + 1], g_p[:, b], AX.X, ALU.max,
                                              apply_absolute_value=True).then_inc(s_gpm, 1)
                        if p := due(t, j, "dve.g_pclamp", b):
                            dve.wait_ge(s_gpm, p.count(2, b + 1))
                            wait(dve, s_o, p.before().count(2, 2))
                            dve.tensor_scalar(g_pmc[:, b:b + 1], g_pmax[:, b:b + 1], 1e-5, None,
                                              ALU.max).then_inc(s_gps, 1)
                        if p := due(t, j, "dve.g_pscales", b):
                            dve.wait_ge(s_gps, p.count(8, 4 * b + 1))
                            dve.reciprocal(g_pinv[:, b:b + 1], g_pmc[:, b:b + 1]).then_inc(s_gps, 1)
                            dve.tensor_scalar(g_ps[:, b, 1:2], g_pmc[:, b:b + 1], cg[:, 2:3], None,
                                              ALU.mult).then_inc(s_gps, 1)
                            dve.wait_ge(s_gps, p.count(8, 4 * b + 2))
                            dve.tensor_scalar(g_ps[:, b, 0:1], g_pinv[:, b:b + 1], 127.0, None,
                                              ALU.mult).then_inc(s_gps, 1)

            turns(dve, body)


def kernel(**inputs):
    import numpy as np
    import concourse.bacc as bacc
    from concourse.bass_utils import run_bass_kernel_spmd

    f = {k: np.asarray(v) for k, v in inputs.items()}
    half = HEADS // 2
    rows_qk = lambda w: w.reshape(DH, half, 2, -1).transpose(3, 2, 0, 1).reshape(-1, P)
    rows_v = lambda w: w.reshape(DH, half, 2, -1).transpose(3, 2, 1, 0).reshape(-1, P)
    arrays = {
        "x": f["x"], "ctx": f["ctx_1024"], "ctx_t": f["ctx_1024"].transpose(0, 2, 1),
        "wq": rows_qk(f["L0_xattn_Wq_w"]), "wk": rows_qk(f["L0_xattn_Wk_w"]), "wv": rows_v(f["L0_xattn_Wv_w"]),
        "bq": rows_qk(f["L0_xattn_Wq_b"]).T, "bk": rows_qk(f["L0_xattn_Wk_b"]).T,
        "bv": rows_v(f["L0_xattn_Wv_b"]).reshape(P),
        "wo": rows_v(f["L0_xattn_Wo_w"].T).T, "bo": f["L0_xattn_Wo_b"],
        "g_xattn": f["g_xattn"], "g_ffn": f["g_ffn"],
        "w0": f["L0_ffn_w0_kernel"], "w1": f["L0_ffn_w1_kernel"], "gate": f["L0_ffn_gate_kernel"],
        "wdn": f["L0_ffn_wo_kernel"],
        "w_cq": f["L1_xattn_w_cq"].reshape(P, 1), "w_q": f["L1_xattn_w_q"].reshape(P, 1),
        "w_c": f["L1_xattn_w_c"].reshape(P, 1),
        "b_cq": f["L1_xattn_b_cq"].reshape(1), "b_q": f["L1_xattn_b_q"].reshape(1), "b_c": f["L1_xattn_b_c"].reshape(1),
        "wl": f["L1_xattn_W_l"].T, "bl": f["L1_xattn_b_l"],
        "wg": f["L1_ffn_w_gate"].T, "wu": f["L1_ffn_w_up"].T, "wd": f["L1_ffn_w_down"].T,
    }
    arrays = {k: np.ascontiguousarray(a) for k, a in arrays.items()}
    nc = bacc.Bacc("TRN2", target_bir_lowering=False, num_devices=1)
    aps = {k: nc.dram_tensor(f"in_{k}", a.shape, mybir.dt.from_np(a.dtype), kind="ExternalInput").ap()
           for k, a in arrays.items()}
    out = nc.dram_tensor("out", (BATCH, P, P), F32, kind="ExternalOutput").ap()
    build(nc, aps, out)
    r = run_bass_kernel_spmd(nc, [{f"in_{k}": a for k, a in arrays.items()}], core_ids=[0])
    return r.results[0]["out"]
```
